# Optimizing a Trainium2 kernel written in Bass

```python
import numpy as np
import jax
import jax.numpy as jnp

def _softmax(x, axis=-1):
    return jax.nn.softmax(x, axis=axis)

def _gelu(x):
    return jax.nn.gelu(x, approximate=True)

def _silu(x):
    return jax.nn.silu(x)

def _sigmoid(x):
    return jax.nn.sigmoid(x)

def _layernorm(x, axis=-1, eps=1e-05):
    m = jnp.mean(x, axis=axis, keepdims=True)
    v = jnp.var(x, axis=axis, keepdims=True)
    return (x - m) / jnp.sqrt(v + eps)

def _scatter_add(tgt, idx, src, axis=0):
    return tgt.at[idx].add(src)

def _segment_sum(src, seg, n):
    return jax.ops.segment_sum(src, seg, n)
kernel_name = 'mk_sandwich_d2_jaxref_r8_347934'

def setup_inputs(seed: int=0):
    np.random.seed(seed)
    _w = jnp.asarray

    def _L0_attn_setup():
        import jax, jax.numpy as jnp
        import numpy as np
        B, T, D = (2, 256, 128)
        H, DK, DV = (16, 64, 64)

        def _hla(x, W_q, W_k, W_v, W_o):
            b, t, _ = x.shape
            q = (x @ W_q).reshape(b, t, H, DK).transpose(1, 0, 2, 3)
            k = (x @ W_k).reshape(b, t, H, DK).transpose(1, 0, 2, 3)
            v = (x @ W_v).reshape(b, t, H, DV).transpose(1, 0, 2, 3)
            S_K0 = jnp.zeros((b, H, DK, DK), x.dtype)
            C_QV0 = jnp.zeros((b, H, DK, DV), x.dtype)
            G0 = jnp.zeros((b, H, DK, DV), x.dtype)

            def step(carry, qkv):
                S_K, C_QV, G = carry
                q_t, k_t, v_t = qkv
                k_C = jnp.einsum('bhk,bhkv->bhv', k_t, C_QV)
                G = G + k_t[..., :, None] * k_C[..., None, :]
                S_K = S_K + k_t[..., :, None] * k_t[..., None, :]
                C_QV = C_QV + q_t[..., :, None] * v_t[..., None, :]
                S_C = jnp.einsum('bhkj,bhjv->bhkv', S_K, C_QV)
                o_t = jnp.einsum('bhk,bhkv->bhv', q_t, S_C - G)
                return ((S_K, C_QV, G), o_t)
            _, outs = jax.lax.scan(step, (S_K0, C_QV0, G0), (q, k, v))
            out = outs.transpose(1, 0, 2, 3).reshape(b, t, H * DV)
            return out @ W_o
        key = jax.random.key(seed)
        ks = jax.random.split(key, 5)
        scale = 0.1 * (6.0 / (D + D)) ** 0.5
        return {'x': jax.random.normal(ks[0], (B, T, D), dtype=jnp.float32), 'W_q': jax.random.normal(ks[1], (D, H * DK), dtype=jnp.float32) * scale, 'W_k': jax.random.normal(ks[2], (D, H * DK), dtype=jnp.float32) * scale, 'W_v': jax.random.normal(ks[3], (D, H * DV), dtype=jnp.float32) * scale, 'W_o': jax.random.normal(ks[4], (H * DV, D), dtype=jnp.float32) * scale}
    _L0_attn_in = _L0_attn_setup()

    def _L0_ffn_setup():
        import jax, jax.numpy as jnp
        import numpy as np
        B, S, DIM = (2, 256, 128)
        HID = 256
        E, NSH, TOPK = (8, 2, 2)

        def _ffn(x, w1, w2, w3):
            return jax.nn.silu(x @ w1.T) * (x @ w3.T) @ w2.T
        key = jax.random.key(seed)
        ks = jax.random.split(key, 8)
        sc = 0.02
        return {'x': jax.random.normal(ks[0], (B, S, DIM), jnp.float32), 'router_w': jax.random.normal(ks[1], (E, DIM), jnp.float32) * sc, 'expert_bias': jnp.zeros((E,), jnp.float32), 'w1': jax.random.normal(ks[2], (E, HID, DIM), jnp.float32) * sc, 'w3': jax.random.normal(ks[3], (E, HID, DIM), jnp.float32) * sc, 'w2': jax.random.normal(ks[4], (E, DIM, HID), jnp.float32) * sc, 'sw1': jax.random.normal(ks[5], (NSH, HID, DIM), jnp.float32) * sc, 'sw3': jax.random.normal(ks[6], (NSH, HID, DIM), jnp.float32) * sc, 'sw2': jax.random.normal(ks[7], (NSH, DIM, HID), jnp.float32) * sc}
    _L0_ffn_in = _L0_ffn_setup()

    def _L1_attn_setup():
        import jax, jax.numpy as jnp
        import numpy as np
        BATCH, SEQ, D_MODEL, STATE_DIM = (2, 512, 128, 16)
        LN_EPS = 1e-05
        IMP_TEMP = 0.5

        def _selective_scan(x, delta, A, B_sel, C_sel):
            Bsz, S, D = x.shape
            N = A.shape[1]
            h0 = jnp.zeros((Bsz, D, N), x.dtype)

            def step(h, inp):
                d_t, x_t, b_t, c_t = inp
                decay = jnp.exp(d_t[:, :, None] * A)
                h = h * decay + (d_t * x_t)[:, :, None] * b_t[:, None, :]
                y = jnp.einsum('bdn,bn->bd', h, c_t)
                return (h, y)
            xs = (delta.transpose(1, 0, 2), x.transpose(1, 0, 2), B_sel.transpose(1, 0, 2), C_sel.transpose(1, 0, 2))
            _, ys = jax.lax.scan(step, h0, xs)
            return ys.transpose(1, 0, 2)

        def _layernorm(x, gamma, beta):
            mu = jnp.mean(x, axis=-1, keepdims=True)
            var = jnp.mean((x - mu) ** 2, axis=-1, keepdims=True)
            return (x - mu) * jax.lax.rsqrt(var + LN_EPS) * gamma + beta

        def _reference_tuple_inner(x, A_log, W_delta, W_B, W_C, ln_gamma, ln_beta, W_ctx, context_scale, W_imp):
            delta = jax.nn.softplus(x @ W_delta)
            B_sel = x @ W_B
            C_sel = x @ W_C
            A = -jnp.exp(A_log)
            ssm_out = _selective_scan(x, delta, A, B_sel, C_sel)
            ssm_out = _layernorm(ssm_out, ln_gamma, ln_beta)
            h_final = ssm_out[:, -1, :]
            h_proj = h_final @ W_imp
            raw_importance = jnp.einsum('bsd,bd->bs', x, h_proj)
            importance = jax.nn.softmax(raw_importance / IMP_TEMP, axis=-1)
            context = ssm_out @ W_ctx * context_scale
            return (importance, context, raw_importance)
        key = jax.random.key(seed)
        ks = jax.random.split(key, 7)
        std = 0.02
        x = jax.random.normal(ks[0], (BATCH, SEQ, D_MODEL), jnp.float32)
        A_log = jax.random.normal(ks[1], (D_MODEL, STATE_DIM), jnp.float32) * 0.1
        W_delta = jax.random.normal(ks[2], (D_MODEL, D_MODEL), jnp.float32) * std
        W_B = jax.random.normal(ks[3], (D_MODEL, STATE_DIM), jnp.float32) * std
        W_C = jax.random.normal(ks[4], (D_MODEL, STATE_DIM), jnp.float32) * std
        W_ctx = jax.random.normal(ks[5], (D_MODEL, D_MODEL), jnp.float32) * std
        W_imp = jax.random.normal(ks[6], (D_MODEL, D_MODEL), jnp.float32) * std
        ln_gamma = jnp.ones((D_MODEL,), jnp.float32)
        ln_beta = jnp.zeros((D_MODEL,), jnp.float32)
        context_scale = jnp.asarray(0.1, jnp.float32)
        return dict(x=x, A_log=A_log, W_delta=W_delta, W_B=W_B, W_C=W_C, ln_gamma=ln_gamma, ln_beta=ln_beta, W_ctx=W_ctx, context_scale=context_scale, W_imp=W_imp)
    _L1_attn_in = _L1_attn_setup()

    def _L1_ffn_setup():
        import jax, jax.numpy as jnp
        import numpy as np
        B, T, D, F_FF, E, K = (8, 256, 128, 512, 8, 2)
        key = jax.random.key(seed)
        ks = jax.random.split(key, 6)
        s = 1.0 / np.sqrt(D)
        return {'x': jax.random.normal(ks[0], (B, T, D), jnp.float32), 'Wr': jax.random.normal(ks[1], (D, E), jnp.float32) * s, 'W1': jax.random.normal(ks[2], (E, D, F_FF), jnp.float32) * s, 'b1': jax.random.normal(ks[3], (E, F_FF), jnp.float32) * 0.01, 'W2': jax.random.normal(ks[4], (E, F_FF, D), jnp.float32) * (1.0 / np.sqrt(F_FF)), 'b2': jax.random.normal(ks[5], (E, D), jnp.float32) * 0.01}
    _L1_ffn_in = _L1_ffn_setup()
    _d = {'L0_attn_x': _L0_attn_in['x'], 'L0_attn_W_q': _L0_attn_in['W_q'], 'L0_attn_W_k': _L0_attn_in['W_k'], 'L0_attn_W_v': _L0_attn_in['W_v'], 'L0_attn_W_o': _L0_attn_in['W_o'], 'L0_ffn_router_w': _L0_ffn_in['router_w'], 'L0_ffn_expert_bias': _L0_ffn_in['expert_bias'], 'L0_ffn_w1': _L0_ffn_in['w1'], 'L0_ffn_w3': _L0_ffn_in['w3'], 'L0_ffn_w2': _L0_ffn_in['w2'], 'L0_ffn_sw1': _L0_ffn_in['sw1'], 'L0_ffn_sw3': _L0_ffn_in['sw3'], 'L0_ffn_sw2': _L0_ffn_in['sw2'], 'L1_attn_A_log': _L1_attn_in['A_log'], 'L1_attn_W_delta': _L1_attn_in['W_delta'], 'L1_attn_W_B': _L1_attn_in['W_B'], 'L1_attn_W_C': _L1_attn_in['W_C'], 'L1_attn_ln_gamma': _L1_attn_in['ln_gamma'], 'L1_attn_ln_beta': _L1_attn_in['ln_beta'], 'L1_attn_W_ctx': _L1_attn_in['W_ctx'], 'L1_attn_context_scale': _L1_attn_in['context_scale'], 'L1_attn_W_imp': _L1_attn_in['W_imp'], 'L1_ffn_Wr': _L1_ffn_in['Wr'], 'L1_ffn_W1': _L1_ffn_in['W1'], 'L1_ffn_b1': _L1_ffn_in['b1'], 'L1_ffn_W2': _L1_ffn_in['W2'], 'L1_ffn_b2': _L1_ffn_in['b2']}
    _x0 = _d['L0_attn_x']
    _d['L0_attn_x'] = jax.random.normal(jax.random.fold_in(jax.random.key(seed), 1), (1, 2048, 128), dtype=_x0.dtype)
    del _x0
    return _d

def reference(L0_attn_x, L0_attn_W_q, L0_attn_W_k, L0_attn_W_v, L0_attn_W_o, L0_ffn_router_w, L0_ffn_expert_bias, L0_ffn_w1, L0_ffn_w3, L0_ffn_w2, L0_ffn_sw1, L0_ffn_sw3, L0_ffn_sw2, L1_attn_A_log, L1_attn_W_delta, L1_attn_W_B, L1_attn_W_C, L1_attn_ln_gamma, L1_attn_ln_beta, L1_attn_W_ctx, L1_attn_context_scale, L1_attn_W_imp, L1_ffn_Wr, L1_ffn_W1, L1_ffn_b1, L1_ffn_W2, L1_ffn_b2):

    def _L0_attn_ref(x, W_q, W_k, W_v, W_o):
        import jax, jax.numpy as jnp
        import numpy as np
        B, T, D = (2, 256, 128)
        H, DK, DV = (16, 64, 64)

        def _hla(x, W_q, W_k, W_v, W_o):
            b, t, _ = x.shape
            q = (x @ W_q).reshape(b, t, H, DK).transpose(1, 0, 2, 3)
            k = (x @ W_k).reshape(b, t, H, DK).transpose(1, 0, 2, 3)
            v = (x @ W_v).reshape(b, t, H, DV).transpose(1, 0, 2, 3)
            S_K0 = jnp.zeros((b, H, DK, DK), x.dtype)
            C_QV0 = jnp.zeros((b, H, DK, DV), x.dtype)
            G0 = jnp.zeros((b, H, DK, DV), x.dtype)

            def step(carry, qkv):
                S_K, C_QV, G = carry
                q_t, k_t, v_t = qkv
                k_C = jnp.einsum('bhk,bhkv->bhv', k_t, C_QV)
                G = G + k_t[..., :, None] * k_C[..., None, :]
                S_K = S_K + k_t[..., :, None] * k_t[..., None, :]
                C_QV = C_QV + q_t[..., :, None] * v_t[..., None, :]
                S_C = jnp.einsum('bhkj,bhjv->bhkv', S_K, C_QV)
                o_t = jnp.einsum('bhk,bhkv->bhv', q_t, S_C - G)
                return ((S_K, C_QV, G), o_t)
            _, outs = jax.lax.scan(step, (S_K0, C_QV0, G0), (q, k, v))
            out = outs.transpose(1, 0, 2, 3).reshape(b, t, H * DV)
            return out @ W_o
        return _hla(x, W_q, W_k, W_v, W_o)

    def _L0_ffn_ref(x, router_w, expert_bias, w1, w3, w2, sw1, sw3, sw2):
        import jax, jax.numpy as jnp
        import numpy as np
        B, S, DIM = (2, 256, 128)
        HID = 256
        E, NSH, TOPK = (8, 2, 2)

        def _ffn(x, w1, w2, w3):
            return jax.nn.silu(x @ w1.T) * (x @ w3.T) @ w2.T
        bs, sl, d = x.shape
        xf = x.reshape(-1, d)
        shared = jnp.zeros_like(xf)
        for i in range(sw1.shape[0]):
            shared = shared + _ffn(xf, sw1[i], sw2[i], sw3[i])
        logits = xf @ router_w.T + expert_bias
        rw, sel = jax.lax.top_k(logits, TOPK)
        rw = jax.nn.softmax(rw.astype(jnp.float32), axis=-1).astype(x.dtype)
        onehot = jax.nn.one_hot(sel, E, dtype=x.dtype)
        combine = jnp.einsum('tk,tke->te', rw, onehot)

        def body(acc, ew):
            e1, e3, e2, cw = ew
            acc = acc + cw[:, None] * _ffn(xf, e1, e2, e3)
            return (acc, None)
        out, _ = jax.lax.scan(body, jnp.zeros_like(xf), (w1, w3, w2, combine.T))
        out = out + shared
        return out.reshape(bs, sl, -1)

    def _L1_attn_ref(x, A_log, W_delta, W_B, W_C, ln_gamma, ln_beta, W_ctx, context_scale, W_imp):
        import jax, jax.numpy as jnp
        import numpy as np
        BATCH, SEQ, D_MODEL, STATE_DIM = (2, 512, 128, 16)
        LN_EPS = 1e-05
        IMP_TEMP = 0.5

        def _selective_scan(x, delta, A, B_sel, C_sel):
            Bsz, S, D = x.shape
            N = A.shape[1]
            h0 = jnp.zeros((Bsz, D, N), x.dtype)

            def step(h, inp):
                d_t, x_t, b_t, c_t = inp
                decay = jnp.exp(d_t[:, :, None] * A)
                h = h * decay + (d_t * x_t)[:, :, None] * b_t[:, None, :]
                y = jnp.einsum('bdn,bn->bd', h, c_t)
                return (h, y)
            xs = (delta.transpose(1, 0, 2), x.transpose(1, 0, 2), B_sel.transpose(1, 0, 2), C_sel.transpose(1, 0, 2))
            _, ys = jax.lax.scan(step, h0, xs)
            return ys.transpose(1, 0, 2)

        def _layernorm(x, gamma, beta):
            mu = jnp.mean(x, axis=-1, keepdims=True)
            var = jnp.mean((x - mu) ** 2, axis=-1, keepdims=True)
            return (x - mu) * jax.lax.rsqrt(var + LN_EPS) * gamma + beta

        def _reference_tuple_inner(x, A_log, W_delta, W_B, W_C, ln_gamma, ln_beta, W_ctx, context_scale, W_imp):
            delta = jax.nn.softplus(x @ W_delta)
            B_sel = x @ W_B
            C_sel = x @ W_C
            A = -jnp.exp(A_log)
            ssm_out = _selective_scan(x, delta, A, B_sel, C_sel)
            ssm_out = _layernorm(ssm_out, ln_gamma, ln_beta)
            h_final = ssm_out[:, -1, :]
            h_proj = h_final @ W_imp
            raw_importance = jnp.einsum('bsd,bd->bs', x, h_proj)
            importance = jax.nn.softmax(raw_importance / IMP_TEMP, axis=-1)
            context = ssm_out @ W_ctx * context_scale
            return (importance, context, raw_importance)
        return _reference_tuple_inner(x, A_log, W_delta, W_B, W_C, ln_gamma, ln_beta, W_ctx, context_scale, W_imp)[1]

    def _L1_ffn_ref(x, Wr, W1, b1, W2, b2):
        import jax, jax.numpy as jnp
        import numpy as np
        B, T, D, F_FF, E, K = (8, 256, 128, 512, 8, 2)
        pooled = x.mean(axis=1)
        logits = pooled @ Wr
        top_scores, top_idx = jax.lax.top_k(logits, K)
        weights = jax.nn.softmax(top_scores, axis=-1)
        W1s, b1s = (W1[top_idx], b1[top_idx])
        W2s, b2s = (W2[top_idx], b2[top_idx])
        h = jnp.einsum('btd,bkdf->bktf', x, W1s) + b1s[:, :, None, :]
        h = jax.nn.gelu(h, approximate=False)
        y = jnp.einsum('bktf,bkfd->bktd', h, W2s) + b2s[:, :, None, :]
        out = jnp.einsum('bk,bktd->btd', weights, y)
        return out
    x = L0_attn_x
    x = x + _layernorm(_L0_attn_ref(_layernorm(x, axis=-1), L0_attn_W_q, L0_attn_W_k, L0_attn_W_v, L0_attn_W_o), axis=-1)
    x = x + _layernorm(_L0_ffn_ref(_layernorm(x, axis=-1), L0_ffn_router_w, L0_ffn_expert_bias, L0_ffn_w1, L0_ffn_w3, L0_ffn_w2, L0_ffn_sw1, L0_ffn_sw3, L0_ffn_sw2), axis=-1)
    x = x + _layernorm(_L1_attn_ref(_layernorm(x, axis=-1), L1_attn_A_log, L1_attn_W_delta, L1_attn_W_B, L1_attn_W_C, L1_attn_ln_gamma, L1_attn_ln_beta, L1_attn_W_ctx, L1_attn_context_scale, L1_attn_W_imp), axis=-1)
    x = x + _layernorm(_L1_ffn_ref(_layernorm(x, axis=-1), L1_ffn_Wr, L1_ffn_W1, L1_ffn_b1, L1_ffn_W2, L1_ffn_b2), axis=-1)
    return x

_drawn_inputs = setup_inputs


def setup_inputs(seed=0):
    import zlib

    import numpy as np

    out = dict(_drawn_inputs(seed))
    spreads = {'L0_ffn_expert_bias': (0.0, 0.1),
     'L1_attn_ln_gamma': (1.0, 0.2),
     'L1_attn_ln_beta': (0.0, 0.1)}
    factors = {'L1_ffn_b1': 8.0, 'L1_ffn_b2': 8.0}
    for name, (base, spread) in spreads.items():
        noise = np.random.default_rng([zlib.crc32(name.encode()), seed]).standard_normal(out[name].shape)
        drawn = base * np.exp(spread * noise) if base else spread * noise
        out[name] = jnp.asarray(drawn.astype(out[name].dtype))
    for name, factor in factors.items():
        out[name] = (out[name] * factor).astype(out[name].dtype)
    return out
```

```python
from contextlib import ExitStack

import concourse.bass as bass
from concourse import mybir

P = 128
D = 128
T = 2048
NT = T // P
GT = 4
G = GT * P
NG = NT // GT
H, DK = 16, 64
NP = H // 2
E0, NSH, HID = 8, 2, 256
NS = 16
E1, FF = 8, 512
NF = FF // P
EPS = 1e-5
EULER = 2.718281828459045

F32 = mybir.dt.float32
BF16 = mybir.dt.bfloat16
U32 = mybir.dt.uint32
ALU = mybir.AluOpType
ACT = mybir.ActivationFunctionType
AX = mybir.AxisListType

STAGE1 = ("q0", "q1", "k0", "k1", "v0", "v1", "kt0", "kt1", "a0", "a1", "a2", "a3")
JOBS = ("w0", "w1", "q0", "q1", "b0", "b1", "b2", "b3", "k0", "k1", "wt0", "wt1",
        "v0", "v1", "o0", "o1", "kt0", "kt1", "a0", "a1", "a2", "a3", "y")
RING = 6


def bank_of(job):
    return JOBS.index(job) % RING


def use_of(slot, job, last=NT):
    b = bank_of(job)
    mine = [j for j in JOBS if bank_of(j) == b]
    first = [j for j in mine if j in STAGE1]
    if isinstance(slot, int) and slot == 0:
        return first.index(job) + 1
    if isinstance(slot, int) and slot == last:
        mine_last = [j for j in mine if j not in STAGE1]
        return len(first) + (last - 1) * len(mine) + mine_last.index(job) + 1
    return (slot - 1) * len(mine) + (len(first) + mine.index(job) + 1)


class Steps:

    def __init__(self, eng, sem, base=0):
        self.eng, self.sem, self.base, self.n = eng, sem, base, 0

    def mark(self, ins):
        ins.then_inc(self.sem, 1)
        self.n += 1

    def wait(self):
        self.eng.wait_ge(self.sem, self.base + self.n)


def sandwich(nc, a, out):
    with ExitStack() as ctx:
        def sb(name, shape, dt=F32):
            return ctx.enter_context(nc.sbuf_tensor(name, shape, dt))

        def sem(name):
            return ctx.enter_context(nc.semaphore(name))

        bank = [ctx.enter_context(nc.psum_tensor(f"bank{i}", [P, G], F32)) for i in range(8)]

        ident = sb("ident", [P, P])
        mask = sb("mask", [P, G])
        rank = sb("rank", [P, NT, E0])
        select = sb("select", [96, 2 * NS, P], BF16)
        neg_half = sb("neg_half", [P, NT])
        euler = sb("euler", [P, NT])
        ones = sb("ones", [P, P])

        x = sb("x", [P, NT, D])
        xn = sb("xn", [P, NT, D])
        xT = sb("xT", [P, T])
        n_stats = sb("n_stats", [P, 4, NT, 6])
        n_mv = sb("n_mv", [P, 4, NT, 2])
        n_var = sb("n_var", [P, 4, NT])
        n_rstd = sb("n_rstd", [P, 4, NT])
        r_stats = sb("r_stats", [P, GT, 6])
        r_mv = sb("r_mv", [P, GT, 2])
        r_var = sb("r_var", [P, GT])
        r_rstd = sb("r_rstd", [P, GT])
        r_val = sb("r_val", [P, GT, D])

        Wq = sb("Wq", [P, H * DK])
        Wk = sb("Wk", [P, H * DK])
        Wv = sb("Wv", [P, H * DK])
        Wo = sb("Wo", [P, NP, D])
        arena = sb("arena", [P, 17408])
        at = [0]

        def part(n):
            at[0] += n
            assert at[0] <= 17408
            return arena[:, at[0] - n:at[0]]

        xt = [part(P) for _ in range(2)]
        q_pad = [part(NP * 2 * P).rearrange("p (n r t) -> p n r t", n=NP, r=2) for _ in range(2)]
        v_tok = [part(H * DK) for _ in range(2)]
        k_T = part(NP * P)
        k_tok = part(H * DK)
        a_T = part(H * P)
        w_T = part(NP * P)
        w_tok = part(H * DK)
        b_T = part(H * P)
        o_T = part(NP * P)
        S_sb = part(NP * DK)
        C_sb = part(NP * DK)

        w1T = sb("w1T", [P, E0 + NSH, HID])
        w3T = sb("w3T", [P, E0 + NSH, HID])
        w2T = sb("w2T", [P, E0 + NSH, 2, D])
        routerT = sb("routerT", [P, E0])
        bias = sb("bias", [P, NT, E0])
        logit = sb("logit", [P, NT, E0])
        hit = sb("hit", [P, NT, E0])
        pick = sb("pick", [P, 2, NT, E0])
        top = sb("top", [P, 2, NT])
        place = sb("place", [P, 2, NT])
        gate = sb("gate", [P, 4, NT])
        combine = sb("combine", [P, NT, E0])
        sil = sb("sil", [P, 2, G])
        hid = sb("hid", [P, 2, 2, G])
        acc = sb("acc", [P, GT, D])

        W_delta = sb("W_delta", [P, D])
        W_BC3 = sb("W_BC3", [P, 96])
        W_ctx = sb("W_ctx", [P, D])
        negA = sb("negA", [P, NS])
        expA = sb("expA", [P, NS])
        gamma = sb("gamma", [P, 1])
        beta = sb("beta", [P, 1])
        ctx_scale = sb("ctx_scale", [P, 1])
        state = sb("state", [P, NS])
        at[0] = 0
        zabs, zexp, zlog, delta, dx, bc_rest, y_T, z_T = [part(G) for _ in range(8)]
        decay, drive, hs, hc = [part(2 * G).rearrange("p (b t) -> p b t", b=2) for _ in range(4)]
        y_n, ctx_v = [part(G).rearrange("p (k d) -> p k d", k=GT) for _ in range(2)]
        bc = sb("bc", [96, G], BF16)
        bc_mid = sb("bc_mid", [96, G], BF16)

        w1s = part(2 * FF).rearrange("p (k f) -> p k f", k=2)
        w2s = part(2 * FF).rearrange("p (k d) -> p k d", k=2)
        w2w = part(2 * FF).rearrange("p (v d) -> p v d", v=2 * NF)
        hg = [part(G) for _ in range(2 * NF)]
        b2c = part(G).rearrange("p (k d) -> p k d", k=GT)
        f_val = part(G).rearrange("p (k d) -> p k d", k=GT)
        Wr = sb("Wr", [P, E1])
        b1s = sb("b1s", [P, 2, NF])
        b2s = sb("b2s", [1, 2 * D])
        pooled = sb("pooled", [P, 2])
        lg = sb("lg", [1, 8])
        top8 = sb("top8", [1, 8])
        idx8 = sb("idx8", [1, 8], U32)
        dif = sb("dif", [1, 4])
        wrow = sb("wrow", [1, 2])
        wts = sb("wts", [P, 2])

        x_in = [sem(f"x_in{g}") for g in range(NG)]
        const_in = sem("const_in")
        qkv_in = sem("qkv_in")
        wo_in = sem("wo_in")
        moe_in = sem("moe_in")
        ssm_in = sem("ssm_in")
        wr_in = sem("wr_in")
        const_set = sem("const_set")
        n_step = sem("n_step")
        n_var_ready = sem("n_var_ready")
        n_rstd_ready = sem("n_rstd_ready")
        xn_ready = sem("xn_ready")
        xT_filled = sem("xT_filled")
        xT_ready = sem("xT_ready")
        filled = [sem(f"filled{b}") for b in range(RING)]
        drained = [sem(f"drained{b}") for b in range(RING)]
        xt_ready = sem("xt_ready")
        pad_zeroed = sem("pad_zeroed")
        S_updated, S_copied = sem("S_updated"), sem("S_copied")
        C_updated, C_copied = sem("C_updated"), sem("C_copied")
        y_step = sem("y_step")
        x_added = sem("x_added")
        r_var_ready = sem("r_var_ready")
        r_rstd_ready = sem("r_rstd_ready")
        logit_filled = sem("logit_filled")
        route_step = sem("route_step")
        gate_dif = sem("gate_dif")
        gate_exp = sem("gate_exp")
        ab_filled = sem("ab_filled")
        sil_ready = sem("sil_ready")
        hid_ready = sem("hid_ready")
        ye_filled = sem("ye_filled")
        acc_done = sem("acc_done")
        moe_step = sem("moe_step")
        expA_ready = sem("expA_ready")
        negA_ready = sem("negA_ready")
        zbc_filled = sem("zbc_filled")
        z_step = sem("z_step")
        zlog_ready = sem("zlog_ready")
        delta_ready = sem("delta_ready")
        bc_ready = sem("bc_ready")
        bcast_filled = sem("bcast_filled")
        decay_ready = sem("decay_ready")
        drive_done = sem("drive_done")
        scan_done = sem("scan_done")
        hc_done = sem("hc_done")
        state_saved = sem("state_saved")
        yacc_done = sem("yacc_done")
        yT_ready = sem("yT_ready")
        ytok_filled = sem("ytok_filled")
        yn_ready = sem("yn_ready")
        zT_filled = sem("zT_filled")
        zT_ready = sem("zT_ready")
        ctx_filled = sem("ctx_filled")
        ctx_drained = sem("ctx_drained")
        ssm_step = sem("ssm_step")
        pooled_ready = sem("pooled_ready")
        lg_filled = sem("lg_filled")
        pick_step = sem("pick_step")
        idx_ready = sem("idx_ready")
        dif_ready = sem("dif_ready")
        dexp_ready = sem("dexp_ready")
        wrow_ready = sem("wrow_ready")
        w1_in = sem("w1_in")
        w2_in = sem("w2_in")
        wb_filled = sem("wb_filled")
        wb_ready = sem("wb_ready")
        hf_filled = sem("hf_filled")
        gelu_done = sem("gelu_done")
        yv_done = sem("yv_done")
        fv_ready = sem("fv_ready")
        ff_step = sem("ff_step")
        x_final = sem("x_final")
        out_done = sem("out_done")

        block = ctx.enter_context(nc.Block())
        x_dram = a["x"].rearrange("(t p) d -> p t d", p=P)
        out_dram = out.rearrange("a (t p) d -> p (a t) d", p=P)

        @block.sync
        def _(sp):
            for g in range(NG):
                sp.dma_start(x[:, GT * g:GT * g + GT, :], x_dram[:, GT * g:GT * g + GT, :]).then_inc(x_in[g], 16)
                if g == 0:
                    sp.dma_start(ident[:], a["ident"]).then_inc(const_in, 16)
                    sp.dma_start(mask[:], a["mask"]).then_inc(const_in, 16)
            sp.dma_start(Wq[:], a["W_q"]).then_inc(qkv_in, 16)
            sp.dma_start(Wk[:], a["W_k"]).then_inc(qkv_in, 16)
            sp.dma_start(Wv[:], a["W_v"]).then_inc(qkv_in, 16)
            sp.dma_start(Wo[:], a["W_o"].rearrange("(n p) d -> p n d", p=P)).then_inc(wo_in, 16)
            sp.dma_start(routerT[:], a["routerT"]).then_inc(moe_in, 16)
            sp.dma_start(bias[:], a["bias"]).then_inc(moe_in, 16)
            sp.dma_start(rank[:], a["rank"]).then_inc(moe_in, 16)
            sp.dma_start(w1T[:, 0:E0], a["w1T"]).then_inc(moe_in, 16)
            sp.dma_start(w1T[:, E0:], a["sw1T"]).then_inc(moe_in, 16)
            sp.dma_start(w3T[:, 0:E0], a["w3T"]).then_inc(moe_in, 16)
            sp.dma_start(w3T[:, E0:], a["sw3T"]).then_inc(moe_in, 16)
            sp.dma_start(w2T[:, 0:E0], a["w2T"]).then_inc(moe_in, 16)
            sp.dma_start(w2T[:, E0:], a["sw2T"]).then_inc(moe_in, 16)
            sp.dma_start(select[:], a["select"]).then_inc(ssm_in, 16)
            sp.dma_start(W_delta[:], a["W_delta"]).then_inc(ssm_in, 16)
            for c in range(3):
                sp.dma_start(W_BC3[:, 32 * c:32 * c + NS], a["W_B"]).then_inc(ssm_in, 16)
                sp.dma_start(W_BC3[:, 32 * c + NS:32 * c + 32], a["W_C"]).then_inc(ssm_in, 16)
            sp.dma_start(W_ctx[:], a["W_ctx"]).then_inc(ssm_in, 16)
            sp.dma_start(expA[:], a["A_log"]).then_inc(ssm_in, 16)
            sp.dma_start(gamma[:], a["gamma"]).then_inc(ssm_in, 16)
            sp.dma_start(beta[:], a["beta"]).then_inc(ssm_in, 16)
            sp.dma_start(ctx_scale[:], a["ctx_scale"]).then_inc(ssm_in, 16)
            sp.dma_start(Wr[:], a["Wr"]).then_inc(wr_in, 16)
            sp.wait_ge(idx_ready, 1)
            for k in range(2):
                e = sp.value_load(idx8[0:1, k:k + 1], min_val=0, max_val=E1 - 1)
                sp.dma_start(w1s[:, k, :], a["W1"][bass.ds(e, 1)].rearrange("a p f -> p (a f)")).then_inc(w1_in, 16)
                sp.dma_start(b1s[:, k, :], a["b1"][bass.ds(e, 1)].rearrange("a p f -> p (a f)")).then_inc(w1_in, 16)
                sp.dma_start(w2s[:, k, :], a["W2"][bass.ds(e, 1)].rearrange("a p f -> p (a f)")).then_inc(w2_in, 16)
                sp.dma_start(b2s[0:1, k * D:(k + 1) * D], a["b2"][bass.ds(e, 1), :]).then_inc(w2_in, 16)
            for g in range(NG):
                sp.wait_ge(x_final, g + 1)
                sp.dma_start(out_dram[:, GT * g:GT * g + GT, :], x[:, GT * g:GT * g + GT, :]).then_inc(out_done, 16)
            sp.wait_ge(out_done, 16 * NG)

        @block.gpsimd
        def _(pool):
            pool.memset(neg_half[:], -0.5).then_inc(const_set, 1)
            pool.memset(q_pad[0][:], 0.0).then_inc(pad_zeroed, 1)
            pool.memset(q_pad[1][:], 0.0).then_inc(pad_zeroed, 1)
            pool.memset(euler[:], EULER).then_inc(const_set, 1)
            pool.memset(ones[:], 1.0).then_inc(const_set, 1)
            pool.memset(state[:], 0.0).then_inc(state_saved, 2)
            pool.memset(wts[:], 0.0).then_inc(ye_filled, 2)
            pool.memset(dif[:], 0.0).then_inc(yacc_done, 2)
            pool.memset(pooled[:], 0.0).then_inc(yv_done, 2 * NF)
            pool.memset(wrow[:], 0.0).then_inc(gelu_done, 4)
            pool.memset(negA[:], 0.0).then_inc(acc_done, 1)
            pool.memset(top8[:], 0.0).then_inc(ctx_drained, 1)
            pool.memset(lg[:], 0.0).then_inc(fv_ready, 1)
            pool.wait_ge(const_set, 3)

            def input_rstd(layer):
                for g in range(NG):
                    t = slice(GT * g, GT * g + GT)
                    pool.wait_ge(n_var_ready, NG * layer + g + 1)
                    pool.tensor_tensor(n_rstd[:, layer, t], n_var[:, layer, t], neg_half[:, 0:GT],
                                       ALU.pow).then_inc(n_rstd_ready, 1)

            def result_rstd(n, cols):
                pool.wait_ge(r_var_ready, n + 1)
                pool.tensor_tensor(r_rstd[:, 0:cols], r_var[:, 0:cols], neg_half[:, 0:cols],
                                   ALU.pow).then_inc(r_rstd_ready, 1)

            input_rstd(0)
            with pool.Fori(0, NT) as t:
                result_rstd(t, 1)
            input_rstd(1)
            pool.wait_ge(gate_dif, 1)
            pool.tensor_tensor(gate[:, 1, :], euler[:], gate[:, 0, :], ALU.pow).then_inc(gate_exp, 1)
            with pool.Fori(0, NG) as g:
                result_rstd(g + NT, GT)
            input_rstd(2)
            with pool.Fori(0, NG) as g:
                for n in range(NS):
                    pool.wait_ge(scan_done, g * NS + (n + 2) + 1)
                    last = hs[:, n % 2, G - 1:G]
                    pool.tensor_tensor(state[:, n:n + 1], last, ones[:, 0:1], ALU.mult).then_inc(state_saved, 1)
                result_rstd(2 * g + (NT + NG), GT)
                result_rstd(2 * g + (NT + NG + 1), GT)
            input_rstd(3)
            pool.wait_ge(dif_ready, 1)
            pool.tensor_tensor(dif[:, 1:2], euler[0:1, 0:1], dif[:, 0:1], ALU.pow).then_inc(dexp_ready, 1)
            with pool.Fori(0, NG) as g:
                result_rstd(g + (NT + 3 * NG), GT)

        @block.tensor
        def _(pe):
            def input_transposes(layer):
                for g in range(NG):
                    n = NG * layer + g
                    pe.wait_ge(xn_ready, n + 1)
                    if n >= 2:
                        pe.wait_ge(xT_ready, n - 1)
                    for k in range(GT):
                        last = pe.transpose(bank[6 + g % 2][:, k * P:(k + 1) * P], xn[:, GT * g + k, :], ident[:])
                    last.then_inc(xT_filled, 1)

            pe.wait_ge(const_in, 32)
            input_transposes(0)

            def attention_slot(s, odd, first=False, last=False, inter=True):
                now, old = odd, 1 - odd

                def bank_free(job):
                    n = use_of(s, job)
                    if not (isinstance(n, int) and n == 1):
                        pe.wait_ge(drained[bank_of(job)], n - 1)

                def copied(slot, job):
                    pe.wait_ge(drained[bank_of(job)], use_of(slot, job))

                def done(job, ins):
                    ins.then_inc(filled[bank_of(job)], 1)

                def w_job(w):
                    job = f"w{w}"
                    bank_free(job)
                    if w == 0:
                        copied(s - 1, "a1")
                        copied(s - 1, "kt0")
                        copied(s - 1, "kt1")
                    else:
                        copied(s - 1, "a2")
                        copied(s - 1, "a3")
                    if inter:
                        pe.wait_ge(S_copied, s - 1)
                    b = bank[bank_of(job)]
                    for i in range(4):
                        p = 4 * w + i
                        for r in range(2):
                            h = 2 * p + r
                            ins = pe.matmul(b[DK * r:DK * r + DK, i * P:(i + 1) * P], k_tok[:, h * DK:(h + 1) * DK],
                                            a_T[:, h * P:(h + 1) * P], start=(i == 0), stop=not inter,
                                            skip_group_check=True)
                        if inter:
                            for r in range(2):
                                ins = pe.matmul(b[DK * r:DK * r + DK, i * P:(i + 1) * P], S_sb[:, p * DK:(p + 1) * DK],
                                                q_pad[old][:, p, r, :], start=False, stop=True,
                                                skip_group_check=True)
                    done(job, ins)

                def state_update(target, keys, values, sem_done):
                    for p in range(NP):
                        for r in range(2):
                            h = 2 * p + r
                            ins = pe.matmul(target[DK * r:DK * r + DK, p * DK:(p + 1) * DK],
                                            keys[:, h * DK:(h + 1) * DK], values[:, h * DK:(h + 1) * DK],
                                            start=(not inter and p == 0), stop=True, skip_group_check=True)
                    ins.then_inc(sem_done, 1)

                def projection(job, w_sb):
                    bank_free(job)
                    for i in range(4):
                        p = 4 * int(job[-1]) + i
                        ins = pe.matmul(bank[bank_of(job)][:, i * P:(i + 1) * P], w_sb[:, p * P:(p + 1) * P],
                                        xt[now], start=True, stop=True)
                    done(job, ins)

                def scores(job, keys, queries):
                    for i in range(2):
                        p = 2 * int(job[-1]) + i
                        ins = pe.matmul(bank[bank_of(job)][:, i * 2 * P:(i + 1) * 2 * P], keys[:, p * P:(p + 1) * P],
                                        queries[:, p, :, :].rearrange("p r t -> p (r t)"), start=True, stop=True)
                    done(job, ins)

                def turn(job, src):
                    for i in range(4):
                        p = 4 * int(job[-1]) + i
                        ins = pe.transpose(bank[bank_of(job)][:, i * P:(i + 1) * P], src[:, p * P:(p + 1) * P], ident[:])
                    done(job, ins)

                if not first:
                    w_job(0)
                    w_job(1)
                    if not last:
                        if not inter:
                            pe.wait_ge(xT_ready, NG)
                        state_update(bank[6], k_tok, k_tok, S_updated)
                if not last:
                    pe.wait_ge(xt_ready, s + 1)
                    if first:
                        pe.wait_ge(qkv_in, 48)
                    projection("q0", Wq)
                    projection("q1", Wq)
                if not first:
                    for n in range(4):
                        bank_free(f"b{n}")
                        if n < 3:
                            copied(s, f"w{n // 2}")
                        scores(f"b{n}", w_T, q_pad[old])
                if not last:
                    projection("k0", Wk)
                    projection("k1", Wk)
                if not first:
                    bank_free("wt0")
                    turn("wt0", w_T)
                    bank_free("wt1")
                    turn("wt1", w_T)
                if not last:
                    for n in range(2):
                        bank_free(f"v{n}")
                        done(f"v{n}", pe.matmul(bank[bank_of(f"v{n}")][:], xt[now], Wv[:, n * G:(n + 1) * G],
                                                start=True, stop=True))
                if not first:
                    for n in range(2):
                        job = f"o{n}"
                        bank_free(job)
                        copied(s, f"b{2 * n}")
                        copied(s, f"b{2 * n + 1}")
                        if n == 0:
                            copied(s - 1, "v0")
                            copied(s - 1, "v1")
                        if inter:
                            pe.wait_ge(C_copied, s - 1)
                        b = bank[bank_of(job)]
                        for i in range(4):
                            p = 4 * n + i
                            for r in range(2):
                                h = 2 * p + r
                                ins = pe.matmul(b[DK * r:DK * r + DK, i * P:(i + 1) * P],
                                                v_tok[old][:, h * DK:(h + 1) * DK], b_T[:, h * P:(h + 1) * P],
                                                start=(i == 0), stop=not inter, skip_group_check=True)
                            if inter:
                                for r in range(2):
                                    ins = pe.matmul(b[DK * r:DK * r + DK, i * P:(i + 1) * P],
                                                    C_sb[:, p * DK:(p + 1) * DK], q_pad[old][:, p, r, :],
                                                    start=False, stop=True, skip_group_check=True)
                        done(job, ins)
                    if not last:
                        copied(s, "wt0")
                        copied(s, "wt1")
                        state_update(bank[7], w_tok, v_tok[old], C_updated)
                if not last:
                    bank_free("kt0")
                    copied(s, "k0")
                    turn("kt0", k_T)
                    bank_free("kt1")
                    copied(s, "k1")
                    turn("kt1", k_T)
                    for n in range(4):
                        bank_free(f"a{n}")
                        if n % 2 == 0:
                            copied(s, f"q{n // 2}")
                        scores(f"a{n}", k_T, q_pad[now])
                if not first:
                    bank_free("y")
                    copied(s, "o0")
                    copied(s, "o1")
                    if not inter:
                        pe.wait_ge(wo_in, 16)
                    for p in range(NP):
                        ins = pe.matmul(bank[bank_of("y")][:, 0:D], o_T[:, p * P:(p + 1) * P], Wo[:, p, :],
                                        start=(p == 0), stop=(p == NP - 1))
                    done("y", ins)

            attention_slot(0, 0, first=True)
            attention_slot(1, 1, inter=False)
            with pe.Fori(0, (NT - 2) // 2) as i:
                for u in range(2):
                    attention_slot(i * 2 + (2 + u), u)
            attention_slot(NT, 0, last=True)

            input_transposes(1)
            pe.wait_ge(moe_in, 16 * 9)
            pe.wait_ge(xT_ready, 2 * NG)
            for t in range(NT):
                ins = pe.matmul(bank[5][:, t * E0:(t + 1) * E0], xT[:, t * P:(t + 1) * P], routerT[:],
                                start=True, stop=True)
            ins.then_inc(logit_filled, 1)
            with pe.Fori(0, NG) as g:
                def expert_out(e):
                    j = min(e, E0)
                    b = bank[4 + j % 2]
                    pe.wait_ge(hid_ready, g * 20 + (2 + 2 * e + 2))
                    if e <= E0:
                        pe.wait_ge(acc_done, g * (E0 + 1) + (j if j == 0 else j - 1) + 1)
                    for k in range(GT):
                        for m in range(2):
                            ins = pe.matmul(b[:, k * P:(k + 1) * P], hid[:, e % 2, m, k * P:(k + 1) * P],
                                            w2T[:, e, m, :], start=(k == 0 and m == 0 and e <= E0), stop=(m == 1),
                                            skip_group_check=True)
                    ins.then_inc(ye_filled, 1)

                for e in range(E0 + NSH):
                    for m in range(2):
                        pe.wait_ge(hid_ready, g * 20 + (2 * e + m + 1))
                        pe.matmul(bank[2 * m][:], w1T[:, e, m * P:(m + 1) * P], xT[:, bass.ds(g * G, G)],
                                  start=True, stop=True)
                        pe.matmul(bank[2 * m + 1][:], w3T[:, e, m * P:(m + 1) * P], xT[:, bass.ds(g * G, G)],
                                  start=True, stop=True).then_inc(ab_filled, 1)
                    if e:
                        expert_out(e - 1)
                expert_out(E0 + NSH - 1)

            input_transposes(2)
            pe.wait_ge(ssm_in, 16 * 13)
            with pe.Fori(0, NG) as g:
                if True:
                    pe.wait_ge(xT_ready, 3 * NG)
                    pe.wait_ge(ctx_drained, g + 1)
                    pe.matmul(bank[0][0:96, :], W_BC3[:], xT[:, bass.ds(g * G, G)], start=True, stop=True)
                    pe.matmul(bank[1][:], W_delta[:], xT[:, bass.ds(g * G, G)], start=True,
                              stop=True).then_inc(zbc_filled, 1)
                    pe.wait_ge(bc_ready, g + 1)

                    def y_sum(n):
                        pe.wait_ge(hc_done, g * NS + (n + 2) + 1)
                        pe.matmul(bank[6][:], ident[:], hc[:, n % 2, :], start=(n == 0),
                                  stop=(n == NS - 1), skip_group_check=True).then_inc(yacc_done, 1)

                    for n in range(NS):
                        pe.wait_ge(hc_done, g * NS + n + 1)
                        pe.matmul(bank[2 + 2 * (n % 2)][:], select[:, n, :], bc[:], start=True,
                                  stop=True).then_inc(bcast_filled, 1)
                        pe.matmul(bank[3 + 2 * (n % 2)][:], select[:, NS + n, :], bc[:], start=True,
                                  stop=True).then_inc(bcast_filled, 1)
                        if n:
                            y_sum(n - 1)
                    y_sum(NS - 1)
                    pe.wait_ge(yT_ready, g + 1)
                    for k in range(GT):
                        ins = pe.transpose(bank[7][:, k * P:(k + 1) * P], y_T[:, k * P:(k + 1) * P], ident[:])
                    ins.then_inc(ytok_filled, 1)
                    pe.wait_ge(yn_ready, g + 1)
                    for k in range(GT):
                        ins = pe.transpose(bank[0][:, k * P:(k + 1) * P], y_n[:, k, :], ident[:])
                    ins.then_inc(zT_filled, 1)
                    pe.wait_ge(zT_ready, g + 1)
                    for k in range(GT):
                        ins = pe.matmul(bank[1][:, k * P:(k + 1) * P], z_T[:, k * P:(k + 1) * P], W_ctx[:],
                                        start=True, stop=True)
                    ins.then_inc(ctx_filled, 1)

            input_transposes(3)
            pe.wait_ge(wr_in, 16)
            pe.wait_ge(pooled_ready, 1)
            pe.matmul(bank[0][0:1, 0:E1], pooled[:, 1:2], Wr[:], start=True, stop=True).then_inc(lg_filled, 1)
            pe.wait_ge(wrow_ready, 1)
            pe.wait_ge(w2_in, 64)
            pe.matmul(bank[1][:, 0:2], ones[0:1, :], wrow[:], start=True, stop=True)
            pe.matmul(bank[1][:, P:3 * P], ones[0:1, :], b2s[:], start=True, stop=True).then_inc(wb_filled, 1)
            pe.wait_ge(w1_in, 64)
            pe.wait_ge(wb_ready, 1)
            with pe.Fori(0, NG) as g:
                def out_part(v):
                    pe.wait_ge(gelu_done, g * (2 * NF) + (v + 4) + 1)
                    if v == 0:
                        pe.wait_ge(fv_ready, g + 1)
                    for k in range(GT):
                        ins = pe.matmul(bank[4][:, k * P:(k + 1) * P], hg[v][:, k * P:(k + 1) * P], w2w[:, v, :],
                                        start=(v == 0 and k == 0), stop=(v == 2 * NF - 1), skip_group_check=True)
                    ins.then_inc(yv_done, 1)

                for v in range(2 * NF):
                    pe.wait_ge(gelu_done, g * (2 * NF) + v + 1)
                    pe.matmul(bank[v % 4][:], w1s[:, v // NF, (v % NF) * P:(v % NF + 1) * P],
                              xT[:, bass.ds(g * G, G)], start=True, stop=True).then_inc(hf_filled, 1)
                    if v >= 2:
                        out_part(v - 2)
                out_part(2 * NF - 2)
                out_part(2 * NF - 1)

        @block.scalar
        def _(act):
            def input_copies(layer):
                for g in range(NG):
                    act.wait_ge(xT_filled, NG * layer + g + 1)
                    act.activation(xT[:, g * G:(g + 1) * G], bank[6 + g % 2][:], ACT.Copy).then_inc(xT_ready, 1)

            input_copies(0)

            def tile_input(s, odd):
                act.wait_ge(xT_ready, NG)
                act.activation(xt[odd], xT[:, s * P:(s + 1) * P] if isinstance(s, int) else xT[:, bass.ds(s * P, P)],
                               ACT.Copy).then_inc(xt_ready, 1)

            def attention_slot(s, odd, first=False, last=False):
                now = odd

                def copy(job, dst):
                    act.wait_ge(filled[bank_of(job)], use_of(s, job))
                    act.activation(dst, bank[bank_of(job)][:], ACT.Copy).then_inc(drained[bank_of(job)], 1)

                def copy_padded(job):
                    act.wait_ge(filled[bank_of(job)], use_of(s, job))
                    p = slice(4 * int(job[-1]), 4 * int(job[-1]) + 4)
                    for r in range(2):
                        half = slice(DK * r, DK * r + DK)
                        ins = act.activation(q_pad[now][half, p, r, :],
                                             bank[bank_of(job)][half, :].rearrange("p (n t) -> p n t", n=4), ACT.Copy)
                    ins.then_inc(drained[bank_of(job)], 1)

                if not first:
                    copy("w0", w_T[:, 0:G])
                    copy("w1", w_T[:, G:2 * G])
                if not last:
                    copy_padded("q0")
                    copy_padded("q1")
                    copy("k0", k_T[:, 0:G])
                    copy("k1", k_T[:, G:2 * G])
                if not first:
                    copy("wt0", w_tok[:, 0:G])
                    copy("wt1", w_tok[:, G:2 * G])
                if not last:
                    copy("v0", v_tok[now][:, 0:G])
                    copy("v1", v_tok[now][:, G:2 * G])
                    if not (isinstance(s, int) and s == NT - 1):
                        tile_input(s + 1, 1 - odd)
                if not first:
                    copy("o0", o_T[:, 0:G])
                    copy("o1", o_T[:, G:2 * G])
                if not last:
                    copy("kt0", k_tok[:, 0:G])
                    copy("kt1", k_tok[:, G:2 * G])

            act.wait_ge(pad_zeroed, 2)
            tile_input(0, 0)
            attention_slot(0, 0, first=True)
            attention_slot(1, 1)
            with act.Fori(0, (NT - 2) // 2 - 1) as i:
                for u in range(2):
                    attention_slot(i * 2 + (2 + u), u)
            attention_slot(NT - 2, 0)
            attention_slot(NT - 1, 1)
            attention_slot(NT, 0, last=True)

            input_copies(1)
            with act.Fori(0, NG) as g:
                for e in range(E0 + NSH):
                    for m in range(2):
                        act.wait_ge(ab_filled, g * 20 + (2 * e + m + 1))
                        act.wait_ge(hid_ready, g * 20 + (2 * e + m + 1))
                        act.activation(sil[:, m, :], bank[2 * m][:], ACT.Silu).then_inc(sil_ready, 1)

            input_copies(2)
            act.wait_ge(ssm_in, 16 * 13)
            act.activation(expA[:], expA[:], ACT.Exp).then_inc(expA_ready, 1)
            act.wait_ge(negA_ready, 1)
            with act.Fori(0, NG) as g:
                act.wait_ge(zbc_filled, g + 1)
                act.activation(zabs, bank[1][:], ACT.Abs).then_inc(z_step, 1)
                act.wait_ge(z_step, g * 2 + 1)
                act.activation(zexp, zabs, ACT.Exp, scale=-1.0).then_inc(z_step, 1)
                act.wait_ge(z_step, g * 2 + 2)
                act.activation(zlog, zexp, ACT.Ln, bias=1.0).then_inc(zlog_ready, 1)
                act.wait_ge(delta_ready, g + 1)
                for n in range(NS):
                    act.wait_ge(scan_done, g * NS + n + 1)
                    act.activation(decay[:, n % 2, :], delta, ACT.Exp,
                                   scale=negA[:, n:n + 1]).then_inc(decay_ready, 1)
                act.wait_ge(yacc_done, g * NS + (NS + 1) + 1)
                act.activation(y_T, bank[6][:], ACT.Copy).then_inc(yT_ready, 1)
                act.wait_ge(zT_filled, g + 1)
                act.activation(z_T, bank[0][:], ACT.Identity, scale=gamma[:, 0:1],
                               bias=beta[:, 0:1]).then_inc(zT_ready, 1)

            input_copies(3)
            act.wait_ge(w1_in, 64)
            with act.Fori(0, NG) as g:
                for v in range(2 * NF):
                    act.wait_ge(hf_filled, g * (2 * NF) + (v + 1))
                    act.wait_ge(yv_done, g * (2 * NF) + v + 1)
                    act.activation(hg[v], bank[v % 4][:], ACT.Gelu,
                                   bias=b1s[:, v // NF, v % NF:v % NF + 1]).then_inc(gelu_done, 1)

        @block.vector
        def _(dve):
            n_steps = Steps(dve, n_step)

            def input_norm(layer):
                def normalise(g):
                    dve.wait_ge(n_rstd_ready, NG * layer + g + 1)
                    if layer:
                        dve.wait_ge(xT_filled, NG * layer - NG + g + 1)
                    for k in range(GT):
                        t = GT * g + k
                        ins = dve.tensor_scalar(xn[:, t, :], x[:, t, :], n_mv[:, layer, t, 0:1],
                                                n_rstd[:, layer, t:t + 1], ALU.subtract, ALU.mult)
                    ins.then_inc(xn_ready, 1)

                for g in range(NG):
                    if layer == 0:
                        dve.wait_ge(x_in[g], 16)
                    for k in range(GT):
                        ins = dve.bn_stats(n_stats[:, layer, GT * g + k, :], x[:, GT * g + k, :])
                    n_steps.mark(ins)
                    n_steps.wait()
                    for k in range(GT):
                        ins = dve.bn_aggr(n_mv[:, layer, GT * g + k, :], n_stats[:, layer, GT * g + k, :])
                    n_steps.mark(ins)
                    n_steps.wait()
                    dve.tensor_scalar(n_var[:, layer, GT * g:GT * g + GT], n_mv[:, layer, GT * g:GT * g + GT, 1],
                                      EPS, None, ALU.add).then_inc(n_var_ready, 1)
                    if g:
                        normalise(g - 1)
                normalise(NG - 1)

            def result_stats(steps, srcs, n_count):
                k_all = len(srcs)
                for k, src in enumerate(srcs):
                    ins = dve.bn_stats(r_stats[:, k, :], src)
                steps.mark(ins)
                steps.wait()
                dve.memset(r_var[:, 0:k_all], 0.0)
                for k in range(k_all):
                    ins = dve.bn_aggr(r_mv[:, k, :], r_stats[:, k, :])
                steps.mark(ins)
                steps.wait()
                dve.tensor_scalar(r_var[:, 0:k_all], r_mv[:, 0:k_all, 1], EPS, None, ALU.add).then_inc(r_var_ready, 1)
                dve.wait_ge(r_rstd_ready, n_count)

            input_norm(0)

            dve.wait_ge(const_in, 32)

            def attention_slot(s, first=False, last=False):
                def masked(job, dst):
                    dve.wait_ge(filled[bank_of(job)], use_of(s, job))
                    dve.tensor_tensor(dst, bank[bank_of(job)][:], mask[:], ALU.mult)\
                       .then_inc(drained[bank_of(job)], 1)

                if not first and not last:
                    dve.wait_ge(S_updated, s)
                    dve.tensor_copy(S_sb, bank[6][:]).then_inc(S_copied, 1)
                if not first:
                    for n in range(4):
                        masked(f"b{n}", b_T[:, n * G:(n + 1) * G])
                    if not last:
                        dve.wait_ge(C_updated, s)
                        dve.tensor_copy(C_sb, bank[7][:]).then_inc(C_copied, 1)
                if not last:
                    for n in range(4):
                        masked(f"a{n}", a_T[:, n * G:(n + 1) * G])
                if not first:
                    y = bank[bank_of("y")][:, 0:D]
                    dve.wait_ge(filled[bank_of("y")], use_of(s, "y"))
                    steps = Steps(dve, y_step, (s - 1) * 2)
                    result_stats(steps, [y], s)
                    dve.tensor_scalar(r_val[:, 0, :], y, r_mv[:, 0, 0:1], r_rstd[:, 0:1], ALU.subtract, ALU.mult)\
                       .then_inc(drained[bank_of("y")], 1)
                    dve.wait_ge(drained[bank_of("y")], use_of(s, "y"))
                    row = x[:, s - 1, :] if isinstance(s, int) else x[:, bass.ds(s - 1, 1), :].rearrange("p a d -> p (a d)")
                    dve.tensor_tensor(row, row, r_val[:, 0, :], ALU.add).then_inc(x_added, 1)

            attention_slot(0, first=True)
            attention_slot(1)
            with dve.Fori(2, NT) as s:
                attention_slot(s)
            attention_slot(NT, last=True)
            dve.wait_ge(x_added, NT)

            input_norm(1)
            dve.wait_ge(moe_in, 16 * 9)
            dve.wait_ge(logit_filled, 1)
            route = Steps(dve, route_step)

            def step(ins):
                route.mark(ins)
                route.wait()

            def wide(v):
                return v.unsqueeze(2).to_broadcast([P, NT, E0])

            step(dve.tensor_tensor(logit[:], bank[5][:, 0:NT * E0].rearrange("p (t e) -> p t e", t=NT), bias[:], ALU.add))
            for c in range(2):
                step(dve.tensor_reduce(top[:, c, :], logit[:], AX.X, ALU.max))
                step(dve.tensor_tensor(hit[:], logit[:], wide(top[:, c, :]), ALU.is_equal))
                step(dve.tensor_tensor(hit[:], hit[:], rank[:], ALU.mult))
                step(dve.tensor_reduce(place[:, c, :], hit[:], AX.X, ALU.min))
                step(dve.tensor_tensor(pick[:, c], rank[:], wide(place[:, c, :]), ALU.is_equal))
                if c == 0:
                    step(dve.scalar_tensor_tensor(out=logit[:], in0=pick[:, 0], scalar=-3e38, in1=logit[:],
                                                  op0=ALU.mult, op1=ALU.add))
            dve.tensor_tensor(gate[:, 0, :], top[:, 1, :], top[:, 0, :], ALU.subtract).then_inc(gate_dif, 1)
            dve.wait_ge(gate_exp, 1)
            step(dve.tensor_scalar(gate[:, 2, :], gate[:, 1, :], 1.0, None, ALU.add))
            step(dve.reciprocal(gate[:, 2, :], gate[:, 2, :]))
            step(dve.tensor_tensor(gate[:, 3, :], gate[:, 1, :], gate[:, 2, :], ALU.mult))
            step(dve.tensor_tensor(pick[:, 0], pick[:, 0], wide(gate[:, 2, :]), ALU.mult))
            step(dve.tensor_tensor(pick[:, 1], pick[:, 1], wide(gate[:, 3, :]), ALU.mult))
            dve.tensor_tensor(combine[:], pick[:, 0], pick[:, 1], ALU.add).then_inc(hid_ready, 2)

            def residual_group(g, srcs, steps, n_count):
                result_stats(steps, srcs, n_count)
                for k, src in enumerate(srcs):
                    ins = dve.tensor_scalar(r_val[:, k, :], src, r_mv[:, k, 0:1], r_rstd[:, k:k + 1],
                                            ALU.subtract, ALU.mult)
                steps.mark(ins)
                steps.wait()
                rows = x[:, bass.ds(g * GT, GT), :]
                return dve.tensor_tensor(rows, rows, r_val[:], ALU.add)

            dve.wait_ge(hid_ready, 2)
            with dve.Fori(0, NG) as g:
                def add_expert(e):
                    j = min(e, E0)
                    b = bank[4 + j % 2]
                    dve.wait_ge(ye_filled, g * 10 + (e + 2) + 1)
                    dve.wait_ge(acc_done, g * (E0 + 1) + j + 1)
                    if e < E0:
                        for k in range(GT):
                            w = combine[:, bass.ds(g * GT + k, 1), e:e + 1].rearrange("p a b -> p (a b)")
                            if e == 0:
                                ins = dve.tensor_scalar(acc[:, k, :], b[:, k * P:(k + 1) * P], w, None, ALU.mult)
                            else:
                                ins = dve.scalar_tensor_tensor(out=acc[:, k, :], in0=b[:, k * P:(k + 1) * P], scalar=w,
                                                               in1=acc[:, k, :], op0=ALU.mult, op1=ALU.add)
                    else:
                        ins = dve.tensor_tensor(acc[:], b[:].rearrange("p (k d) -> p k d", k=GT), acc[:], ALU.add)
                    ins.then_inc(acc_done, 1)

                for e in range(E0 + NSH):
                    for m in range(2):
                        dve.wait_ge(sil_ready, g * 20 + (2 * e + m + 1))
                        dve.wait_ge(ye_filled, g * 10 + e + 1)
                        dve.tensor_tensor(hid[:, e % 2, m, :], bank[2 * m + 1][:], sil[:, m, :], ALU.mult)\
                           .then_inc(hid_ready, 1)
                    if 1 <= e <= E0:
                        add_expert(e - 1)
                add_expert(E0 + NSH - 1)
                dve.wait_ge(acc_done, g * (E0 + 1) + (E0 + 1) + 1)
                steps = Steps(dve, moe_step, g * 4)
                steps.mark(residual_group(g, [acc[:, k, :] for k in range(GT)], steps, g + (NT + 1)))
                steps.wait()

            input_norm(2)
            dve.wait_ge(expA_ready, 1)
            dve.tensor_scalar(negA[:], expA[:], -1.0, None, ALU.mult).then_inc(negA_ready, 1)
            dve.memset(decay[:, 0, 0:1], 0.0).then_inc(scan_done, 2)
            dve.memset(hc[:, 0, 0:1], 0.0).then_inc(hc_done, 2)
            dve.wait_ge(scan_done, 2)
            dve.wait_ge(hc_done, 2)
            dve.wait_ge(xT_ready, 3 * NG)
            with dve.Fori(0, NG) as g:
                steps = Steps(dve, ssm_step, g * 10)
                dve.wait_ge(zbc_filled, g + 1)
                steps.mark(dve.tensor_copy(bc[:], bank[0][0:96, :]))
                steps.wait()
                steps.mark(dve.tensor_tensor(bc_rest[0:96, :], bank[0][0:96, :], bc[:], ALU.subtract))
                steps.wait()
                steps.mark(dve.tensor_copy(bc_mid[:], bc_rest[0:96, :]))
                steps.wait()
                dve.tensor_copy(bc[32:64, :], bc_mid[32:64, :])
                dve.tensor_tensor(bc[64:96, :], bc_rest[64:96, :], bc_mid[64:96, :], ALU.subtract).then_inc(bc_ready, 1)
                dve.wait_ge(zlog_ready, g + 1)
                steps.mark(dve.scalar_tensor_tensor(out=delta, in0=bank[1][:], scalar=0.0, in1=zlog,
                                                    op0=ALU.max, op1=ALU.add))
                steps.wait()
                dve.tensor_tensor(dx, delta, xT[:, bass.ds(g * G, G)], ALU.mult).then_inc(delta_ready, 1)
                dve.wait_ge(delta_ready, g + 1)

                def drive_n(n):
                    dve.wait_ge(bcast_filled, g * (2 * NS) + (2 * n + 1))
                    dve.tensor_tensor(drive[:, n % 2, :], dx, bank[2 + 2 * (n % 2)][:], ALU.mult)\
                       .then_inc(drive_done, 1)

                drive_n(0)
                for n in range(NS):
                    dve.wait_ge(decay_ready, g * NS + (n + 1))
                    dve.wait_ge(drive_done, g * NS + (n + 1))
                    dve.wait_ge(state_saved, g * NS + n + 1)
                    dve.tensor_tensor_scan(hs[:, n % 2, :], decay[:, n % 2, :], drive[:, n % 2, :],
                                           state[:, n:n + 1], ALU.mult, ALU.add).then_inc(scan_done, 1)
                    if n + 1 < NS:
                        drive_n(n + 1)
                    dve.wait_ge(scan_done, g * NS + (n + 2) + 1)
                    dve.wait_ge(bcast_filled, g * (2 * NS) + (2 * n + 2))
                    dve.wait_ge(yacc_done, g * NS + n + 1)
                    dve.tensor_tensor(hc[:, n % 2, :], hs[:, n % 2, :], bank[3 + 2 * (n % 2)][:], ALU.mult)\
                       .then_inc(hc_done, 1)
                dve.wait_ge(ytok_filled, g + 1)
                yt = [bank[7][:, k * P:(k + 1) * P] for k in range(GT)]
                result_stats(steps, yt, 2 * g + (NT + NG + 1))
                for k in range(GT):
                    ins = dve.tensor_scalar(y_n[:, k, :], yt[k], r_mv[:, k, 0:1], r_rstd[:, k:k + 1],
                                            ALU.subtract, ALU.mult)
                ins.then_inc(yn_ready, 1)
                dve.wait_ge(ctx_filled, g + 1)
                dve.tensor_scalar(ctx_v, bank[1][:].rearrange("p (k d) -> p k d", k=GT), ctx_scale[:, 0:1], None,
                                  ALU.mult).then_inc(ctx_drained, 1)
                dve.wait_ge(ctx_drained, g + 1 + 1)
                steps.mark(residual_group(g, [ctx_v[:, k, :] for k in range(GT)], steps, 2 * g + (NT + NG + 2)))
                steps.wait()
                assert steps.n == 10, steps.n

            input_norm(3)
            dve.wait_ge(xT_ready, 4 * NG)
            pick_steps = Steps(dve, pick_step)

            def pick_do(ins):
                pick_steps.mark(ins)
                pick_steps.wait()

            pick_do(dve.tensor_reduce(pooled[:, 0:1], xT[:], AX.X, ALU.add))
            dve.tensor_scalar(pooled[:, 1:2], pooled[:, 0:1], 1.0 / T, None, ALU.mult).then_inc(pooled_ready, 1)
            dve.wait_ge(lg_filled, 1)
            pick_do(dve.tensor_copy(lg[:], bank[0][0:1, 0:E1]))
            pick_do(dve.max(top8[:], lg[:]))
            dve.max_index(idx8[:], top8[:], lg[:]).then_inc(idx_ready, 1)
            dve.tensor_tensor(dif[:, 0:1], top8[:, 1:2], top8[:, 0:1], ALU.subtract).then_inc(dif_ready, 1)
            dve.wait_ge(dexp_ready, 1)
            pick_do(dve.tensor_scalar(dif[:, 2:3], dif[:, 1:2], 1.0, None, ALU.add))
            pick_do(dve.reciprocal(wrow[:, 0:1], dif[:, 2:3]))
            dve.tensor_tensor(wrow[:, 1:2], dif[:, 1:2], wrow[:, 0:1], ALU.mult).then_inc(wrow_ready, 1)
            dve.wait_ge(wb_filled, 1)
            dve.wait_ge(w2_in, 64)
            pick_do(dve.tensor_copy(wts[:], bank[1][:, 0:2]))
            for k in range(2):
                dve.tensor_scalar(w2w[:, NF * k:NF * k + NF, :].rearrange("p v d -> p (v d)"), w2s[:, k, :],
                                  wts[:, k:k + 1], None, ALU.mult)
            pick_do(dve.tensor_scalar(b2c[:, 0, :], bank[1][:, P:2 * P], wts[:, 0:1], None, ALU.mult))
            pick_do(dve.scalar_tensor_tensor(out=b2c[:, 0, :], in0=bank[1][:, 2 * P:3 * P], scalar=wts[:, 1:2],
                                             in1=b2c[:, 0, :], op0=ALU.mult, op1=ALU.add))
            for k in range(1, GT):
                ins = dve.tensor_copy(b2c[:, k, :], b2c[:, 0, :])
            ins.then_inc(wb_ready, 1)
            dve.wait_ge(wb_ready, 1)

            with dve.Fori(0, NG) as g:
                dve.wait_ge(yv_done, g * (2 * NF) + (4 * NF - 1) + 1)
                dve.tensor_tensor(f_val, bank[4][:].rearrange("p (k d) -> p k d", k=GT), b2c, ALU.add)\
                   .then_inc(fv_ready, 1)
                dve.wait_ge(fv_ready, g + 1 + 1)
                steps = Steps(dve, ff_step, g * 3)
                residual_group(g, [f_val[:, k, :] for k in range(GT)], steps, g + (NT + 3 * NG + 1)).then_inc(x_final, 1)
                dve.wait_ge(x_final, g + 1)


def kernel(**inputs):
    import ml_dtypes
    import numpy as np

    import concourse.bacc as bacc
    from concourse.bass_utils import run_bass_kernel_spmd as run

    i = {k: np.asarray(v) for k, v in inputs.items()}
    later = np.triu(np.ones((P, P), np.float32))
    select = np.zeros((96, 2 * NS, P), ml_dtypes.bfloat16)
    for c in range(3):
        for n in range(2 * NS):
            select[32 * c + n, n, :] = 1
    arrays = {
        "x": i["L0_attn_x"].reshape(T, D),
        "ident": np.eye(P, dtype=np.float32),
        "mask": np.tile(later, (1, GT)),
        "W_q": i["L0_attn_W_q"], "W_k": i["L0_attn_W_k"], "W_v": i["L0_attn_W_v"], "W_o": i["L0_attn_W_o"],
        "routerT": i["L0_ffn_router_w"].T,
        "bias": np.broadcast_to(i["L0_ffn_expert_bias"], (P, NT, E0)),
        "rank": np.broadcast_to(np.arange(E0, dtype=np.float32) - E0, (P, NT, E0)),
        "w1T": i["L0_ffn_w1"].transpose(2, 0, 1), "sw1T": i["L0_ffn_sw1"].transpose(2, 0, 1),
        "w3T": i["L0_ffn_w3"].transpose(2, 0, 1), "sw3T": i["L0_ffn_sw3"].transpose(2, 0, 1),
        "w2T": i["L0_ffn_w2"].reshape(E0, D, 2, P).transpose(3, 0, 2, 1),
        "sw2T": i["L0_ffn_sw2"].reshape(NSH, D, 2, P).transpose(3, 0, 2, 1),
        "select": select,
        "W_delta": i["L1_attn_W_delta"], "W_B": i["L1_attn_W_B"], "W_C": i["L1_attn_W_C"],
        "W_ctx": i["L1_attn_W_ctx"], "A_log": i["L1_attn_A_log"],
        "gamma": i["L1_attn_ln_gamma"].reshape(D, 1), "beta": i["L1_attn_ln_beta"].reshape(D, 1),
        "ctx_scale": np.broadcast_to(i["L1_attn_context_scale"].reshape(1, 1), (P, 1)),
        "Wr": i["L1_ffn_Wr"], "W1": i["L1_ffn_W1"],
        "b1": i["L1_ffn_b1"].reshape(E1, NF, P).transpose(0, 2, 1),
        "W2": i["L1_ffn_W2"].reshape(E1, NF, P, D).transpose(0, 2, 1, 3).reshape(E1, P, NF * D),
        "b2": i["L1_ffn_b2"],
    }
    arrays = {f"{k}_dram": np.ascontiguousarray(v) for k, v in arrays.items()}
    nc = bacc.Bacc("TRN2", target_bir_lowering=False, num_devices=1)
    aps = {k[:-5]: nc.dram_tensor(k, v.shape, mybir.dt.from_np(v.dtype), kind="ExternalInput").ap()
           for k, v in arrays.items()}
    out = nc.dram_tensor("out_dram", (1, T, D), F32, kind="ExternalOutput").ap()
    sandwich(nc, aps, out)
    r = run(nc, [arrays], core_ids=[0])
    return r.results[0]["out_dram"]
```

```python
from contextlib import ExitStack

import concourse.bass as bass
from concourse import mybir

P = 128
D = 128
T = 2048
NT = T // P
GT = 4
G = GT * P
NG = NT // GT
H, DK = 16, 64
NP = H // 2
E0, NSH, HID = 8, 2, 256
NS = 16
RS = 4
E1, FF = 8, 512
NF = FF // P
EPS = 1e-5
EULER = 2.718281828459045

F32 = mybir.dt.float32
BF16 = mybir.dt.bfloat16
U32 = mybir.dt.uint32
ALU = mybir.AluOpType
ACT = mybir.ActivationFunctionType
AX = mybir.AxisListType

STAGE1 = ("q0", "q1", "k0", "k1", "v0", "v1", "kt0", "kt1", "a0", "a1", "a2", "a3")
JOBS = ("w0", "w1", "q0", "q1", "b0", "b1", "b2", "b3", "k0", "k1", "wt0", "wt1",
        "v0", "v1", "o0", "o1", "kt0", "kt1", "a0", "a1", "a2", "a3", "y")
RING = 6


def bank_of(job):
    return JOBS.index(job) % RING


def use_of(slot, job, last=NT):
    b = bank_of(job)
    mine = [j for j in JOBS if bank_of(j) == b]
    first = [j for j in mine if j in STAGE1]
    if isinstance(slot, int) and slot == 0:
        return first.index(job) + 1
    if isinstance(slot, int) and slot == last:
        mine_last = [j for j in mine if j not in STAGE1]
        return len(first) + (last - 1) * len(mine) + mine_last.index(job) + 1
    return (slot - 1) * len(mine) + (len(first) + mine.index(job) + 1)


class Steps:

    def __init__(self, eng, sem, base=0):
        self.eng, self.sem, self.base, self.n = eng, sem, base, 0

    def mark(self, ins):
        ins.then_inc(self.sem, 1)
        self.n += 1

    def wait(self):
        self.eng.wait_ge(self.sem, self.base + self.n)


def sandwich(nc, a, out):
    with ExitStack() as ctx:
        def sb(name, shape, dt=F32):
            return ctx.enter_context(nc.sbuf_tensor(name, shape, dt))

        def sem(name):
            return ctx.enter_context(nc.semaphore(name))

        bank = [ctx.enter_context(nc.psum_tensor(f"bank{i}", [P, G], F32)) for i in range(8)]

        ident = sb("ident", [P, P])
        mask = sb("mask", [P, G])
        rank = sb("rank", [P, NT, E0])
        select = sb("select", [96, 2 * NS, P], BF16)
        neg_half = sb("neg_half", [P, NT])
        euler = sb("euler", [P, NT])
        ones = sb("ones", [P, P])

        x = sb("x", [P, NT, D])
        xn = sb("xn", [P, NT, D])
        xT = sb("xT", [P, T])
        n_stats = sb("n_stats", [P, 4, NT, 6])
        n_mv = sb("n_mv", [P, 4, NT, 2])
        n_var = sb("n_var", [P, 4, NT])
        n_rstd = sb("n_rstd", [P, 4, NT])
        r_stats = sb("r_stats", [P, GT, 6])
        r_mv = sb("r_mv", [P, GT, 2])
        r_var = sb("r_var", [P, GT])
        r_rstd = sb("r_rstd", [P, GT])
        r_val = sb("r_val", [P, GT, D])

        Wq = sb("Wq", [P, H * DK])
        Wk = sb("Wk", [P, H * DK])
        Wv = sb("Wv", [P, H * DK])
        Wo = sb("Wo", [P, NP, D])
        arena = sb("arena", [P, 17408])
        at = [0]

        def part(n):
            at[0] += n
            assert at[0] <= 17408
            return arena[:, at[0] - n:at[0]]

        xt = [part(P) for _ in range(2)]
        q_pad = [part(NP * 2 * P).rearrange("p (n r t) -> p n r t", n=NP, r=2) for _ in range(2)]
        v_tok = [part(H * DK) for _ in range(2)]
        k_T = part(NP * P)
        k_tok = part(H * DK)
        a_T = part(H * P)
        w_T = part(NP * P)
        w_tok = part(H * DK)
        b_T = part(H * P)
        o_T = part(NP * P)
        S_sb = part(NP * DK)
        C_sb = part(NP * DK)

        w1T = sb("w1T", [P, E0 + NSH, HID])
        w3T = sb("w3T", [P, E0 + NSH, HID])
        w2T = sb("w2T", [P, E0 + NSH, 2, D])
        routerT = sb("routerT", [P, E0])
        bias = sb("bias", [P, NT, E0])
        logit = sb("logit", [P, NT, E0])
        hit = sb("hit", [P, NT, E0])
        pick = sb("pick", [P, 2, NT, E0])
        top = sb("top", [P, 2, NT])
        place = sb("place", [P, 2, NT])
        gate = sb("gate", [P, 4, NT])
        combine = sb("combine", [P, NT, E0])
        sil = sb("sil", [P, 2, G])
        hid = sb("hid", [P, 2, 2, G])
        acc = sb("acc", [P, GT, D])

        W_delta = sb("W_delta", [P, D])
        W_BC3 = sb("W_BC3", [P, 96])
        W_ctx = sb("W_ctx", [P, D])
        negA = sb("negA", [P, NS])
        expA = sb("expA", [P, NS])
        gamma = sb("gamma", [P, 1])
        beta = sb("beta", [P, 1])
        ctx_scale = sb("ctx_scale", [P, 1])
        state = sb("state", [P, NS])
        at[0] = 0
        delta, dx, y_T = [part(T) for _ in range(3)]
        drive = part(RS * G).rearrange("p (b t) -> p b t", b=RS)
        c_sb = part(2 * G).rearrange("p (b t) -> p b t", b=2)
        hs = part(RS * G).rearrange("p (b t) -> p b t", b=RS)
        hc = part(RS * G).rearrange("p (b t) -> p b t", b=RS)
        at[0] -= RS * G
        soft = part(T)
        bc_rest = hs[0:96, 0, :]
        y_n, z_T, ctx_v = [part(2 * G).rearrange("p (b t) -> p b t", b=2) for _ in range(3)]
        delta_g = part(G)
        wait_slot = sb("wait_slot", [P, 1])
        bc = sb("bc", [96, T], BF16)
        bc_mid = sb("bc_mid", [96, G], BF16)

        at[0] = 0
        w1s = part(2 * FF).rearrange("p (k f) -> p k f", k=2)
        w2s = part(2 * FF).rearrange("p (k d) -> p k d", k=2)
        w2w = part(2 * FF).rearrange("p (v d) -> p v d", v=2 * NF)
        hg = [part(G) for _ in range(2 * NF)]
        b2c = part(G).rearrange("p (k d) -> p k d", k=GT)
        f_val = part(G).rearrange("p (k d) -> p k d", k=GT)
        Wr = sb("Wr", [P, E1])
        b1s = sb("b1s", [P, 2, NF])
        b2s = sb("b2s", [1, 2 * D])
        pooled = sb("pooled", [P, 2])
        lg = sb("lg", [1, 8])
        top8 = sb("top8", [1, 8])
        idx8 = sb("idx8", [1, 8], U32)
        dif = sb("dif", [1, 4])
        wrow = sb("wrow", [1, 2])
        wts = sb("wts", [P, 2])

        x_in = [sem(f"x_in{g}") for g in range(NG)]
        const_in = sem("const_in")
        qkv_in = sem("qkv_in")
        wo_in = sem("wo_in")
        moe_in = sem("moe_in")
        ssm_in = sem("ssm_in")
        wr_in = sem("wr_in")
        const_set = sem("const_set")
        n_step = sem("n_step")
        n_var_ready = sem("n_var_ready")
        n_rstd_ready = sem("n_rstd_ready")
        xn_ready = sem("xn_ready")
        xT_filled = sem("xT_filled")
        xT_ready = sem("xT_ready")
        filled = [sem(f"filled{b}") for b in range(RING)]
        drained = [sem(f"drained{b}") for b in range(RING)]
        xt_ready = sem("xt_ready")
        pad_zeroed = sem("pad_zeroed")
        S_updated, S_copied = sem("S_updated"), sem("S_copied")
        C_updated, C_copied = sem("C_updated"), sem("C_copied")
        y_step = sem("y_step")
        x_added = sem("x_added")
        r_var_ready = sem("r_var_ready")
        r_rstd_ready = sem("r_rstd_ready")
        logit_filled = sem("logit_filled")
        route_step = sem("route_step")
        gate_dif = sem("gate_dif")
        gate_exp = sem("gate_exp")
        ab_filled = sem("ab_filled")
        sil_ready = sem("sil_ready")
        hid_ready = sem("hid_ready")
        ye_filled = sem("ye_filled")
        acc_done = sem("acc_done")
        moe_step = sem("moe_step")
        expA_ready = sem("expA_ready")
        negA_ready = sem("negA_ready")
        zbc_filled = sem("zbc_filled")
        z_step = sem("z_step")
        zlog_ready = sem("zlog_ready")
        delta_ready = sem("delta_ready")
        dx_ready = sem("dx_ready")
        delta_copied = sem("delta_copied")
        head_step = sem("head_step")
        bc_ready = sem("bc_ready")
        B_filled, C_filled = sem("B_filled"), sem("C_filled")
        C_copied_out = sem("C_copied_out")
        decay_ready = sem("decay_ready")
        drive_done = sem("drive_done")
        scan_done = sem("scan_done")
        hc_done = sem("hc_done")
        state_zeroed = sem("state_zeroed")
        state_saved = sem("state_saved")
        yacc_done = sem("yacc_done")
        yT_ready = sem("yT_ready")
        ytok_filled = sem("ytok_filled")
        yn_ready = sem("yn_ready")
        zT_filled = sem("zT_filled")
        zT_ready = sem("zT_ready")
        ctx_filled = sem("ctx_filled")
        ctx_drained = sem("ctx_drained")
        tail_step = sem("tail_step")
        x_summed = sem("x_summed")
        pooled_ready = sem("pooled_ready")
        lg_filled = sem("lg_filled")
        pick_step = sem("pick_step")
        idx_ready = sem("idx_ready")
        dif_ready = sem("dif_ready")
        dexp_ready = sem("dexp_ready")
        wrow_ready = sem("wrow_ready")
        w1_in = sem("w1_in")
        w2_in = sem("w2_in")
        wb_filled = sem("wb_filled")
        wb_ready = sem("wb_ready")
        hf_filled = sem("hf_filled")
        gelu_done = sem("gelu_done")
        yv_done = sem("yv_done")
        fv_ready = sem("fv_ready")
        ff_step = sem("ff_step")
        x_final = sem("x_final")
        out_done = sem("out_done")

        block = ctx.enter_context(nc.Block())
        x_dram = a["x"].rearrange("(t p) d -> p t d", p=P)
        out_dram = out.rearrange("a (t p) d -> p (a t) d", p=P)

        @block.sync
        def _(sp):
            for g in range(NG):
                sp.dma_start(x[:, GT * g:GT * g + GT, :], x_dram[:, GT * g:GT * g + GT, :]).then_inc(x_in[g], 16)
                if g == 0:
                    sp.dma_start(ident[:], a["ident"]).then_inc(const_in, 16)
                    sp.dma_start(mask[:], a["mask"]).then_inc(const_in, 16)
            sp.dma_start(Wq[:], a["W_q"]).then_inc(qkv_in, 16)
            sp.dma_start(Wk[:], a["W_k"]).then_inc(qkv_in, 16)
            sp.dma_start(Wv[:], a["W_v"]).then_inc(qkv_in, 16)
            sp.dma_start(Wo[:], a["W_o"].rearrange("(n p) d -> p n d", p=P)).then_inc(wo_in, 16)
            sp.dma_start(routerT[:], a["routerT"]).then_inc(moe_in, 16)
            sp.dma_start(bias[:], a["bias"]).then_inc(moe_in, 16)
            sp.dma_start(rank[:], a["rank"]).then_inc(moe_in, 16)
            sp.dma_start(w1T[:, 0:E0], a["w1T"]).then_inc(moe_in, 16)
            sp.dma_start(w1T[:, E0:], a["sw1T"]).then_inc(moe_in, 16)
            sp.dma_start(w3T[:, 0:E0], a["w3T"]).then_inc(moe_in, 16)
            sp.dma_start(w3T[:, E0:], a["sw3T"]).then_inc(moe_in, 16)
            sp.dma_start(w2T[:, 0:E0], a["w2T"]).then_inc(moe_in, 16)
            sp.dma_start(w2T[:, E0:], a["sw2T"]).then_inc(moe_in, 16)
            sp.dma_start(select[:], a["select"]).then_inc(ssm_in, 16)
            sp.dma_start(W_delta[:], a["W_delta"]).then_inc(ssm_in, 16)
            for c in range(3):
                sp.dma_start(W_BC3[:, 32 * c:32 * c + NS], a["W_B"]).then_inc(ssm_in, 16)
                sp.dma_start(W_BC3[:, 32 * c + NS:32 * c + 32], a["W_C"]).then_inc(ssm_in, 16)
            sp.dma_start(W_ctx[:], a["W_ctx"]).then_inc(ssm_in, 16)
            sp.dma_start(expA[:], a["A_log"]).then_inc(ssm_in, 16)
            sp.dma_start(gamma[:], a["gamma"]).then_inc(ssm_in, 16)
            sp.dma_start(beta[:], a["beta"]).then_inc(ssm_in, 16)
            sp.dma_start(ctx_scale[:], a["ctx_scale"]).then_inc(ssm_in, 16)
            sp.dma_start(Wr[:], a["Wr"]).then_inc(wr_in, 16)
            sp.wait_ge(idx_ready, 1)
            for k in range(2):
                e = sp.value_load(idx8[0:1, k:k + 1], min_val=0, max_val=E1 - 1)
                sp.dma_start(w1s[:, k, :], a["W1"][bass.ds(e, 1)].rearrange("a p f -> p (a f)")).then_inc(w1_in, 16)
                sp.dma_start(b1s[:, k, :], a["b1"][bass.ds(e, 1)].rearrange("a p f -> p (a f)")).then_inc(w1_in, 16)
                sp.dma_start(w2s[:, k, :], a["W2"][bass.ds(e, 1)].rearrange("a p f -> p (a f)")).then_inc(w2_in, 16)
                sp.dma_start(b2s[0:1, k * D:(k + 1) * D], a["b2"][bass.ds(e, 1), :]).then_inc(w2_in, 16)
            for g in range(NG):
                sp.wait_ge(x_final, g + 1)
                sp.dma_start(out_dram[:, GT * g:GT * g + GT, :], x[:, GT * g:GT * g + GT, :]).then_inc(out_done, 16)
            sp.wait_ge(out_done, 16 * NG)

        @block.gpsimd
        def _(pool):
            pool.memset(neg_half[:], -0.5).then_inc(const_set, 1)
            pool.memset(q_pad[0][:], 0.0).then_inc(pad_zeroed, 1)
            pool.memset(q_pad[1][:], 0.0).then_inc(pad_zeroed, 1)
            pool.memset(euler[:], EULER).then_inc(const_set, 1)
            pool.memset(ones[:], 1.0).then_inc(const_set, 1)
            pool.memset(state[:], 0.0).then_inc(state_zeroed, 1)
            pool.memset(wts[:], 0.0).then_inc(ye_filled, 2)
            pool.memset(pooled[:], 0.0).then_inc(yv_done, 2 * NF)
            pool.memset(wrow[:], 0.0).then_inc(gelu_done, 4)
            pool.memset(negA[:], 0.0).then_inc(acc_done, 1)
            pool.memset(lg[:], 0.0).then_inc(fv_ready, 1)
            pool.wait_ge(const_set, 3)

            def input_rstd(layer):
                for g in range(NG):
                    t = slice(GT * g, GT * g + GT)
                    pool.wait_ge(n_var_ready, NG * layer + g + 1)
                    pool.tensor_tensor(n_rstd[:, layer, t], n_var[:, layer, t], neg_half[:, 0:GT],
                                       ALU.pow).then_inc(n_rstd_ready, 1)

            def result_rstd(n, cols):
                pool.wait_ge(r_var_ready, n + 1)
                pool.tensor_tensor(r_rstd[:, 0:cols], r_var[:, 0:cols], neg_half[:, 0:cols],
                                   ALU.pow).then_inc(r_rstd_ready, 1)

            input_rstd(0)
            with pool.Fori(0, NT) as t:
                result_rstd(t, 1)
            input_rstd(1)
            pool.wait_ge(gate_dif, 1)
            pool.tensor_tensor(gate[:, 1, :], euler[:], gate[:, 0, :], ALU.pow).then_inc(gate_exp, 1)
            with pool.Fori(0, NG) as g:
                result_rstd(g + NT, GT)
            input_rstd(2)
            for g in range(NG):
                pool.wait_ge(delta_ready, g + 1)
                pool.tensor_tensor(dx[:, g * G:(g + 1) * G], delta[:, g * G:(g + 1) * G], xT[:, g * G:(g + 1) * G],
                                   ALU.mult).then_inc(dx_ready, 1)

            def state_group(g):
                for n in range(NS):
                    step = g * NS + n
                    pool.wait_ge(scan_done, step + 1)
                    pool.tensor_tensor(state[:, n:n + 1], hs[:, n % RS, G - 1:G], ones[:, 0:1],
                                       ALU.mult).then_inc(state_saved, 1)
                    pool.wait_ge(C_copied_out, step + 1)
                    if not (isinstance(step, int) and step < RS):
                        pool.wait_ge(yacc_done, step - (RS - 1))
                    pool.tensor_tensor(hc[:, n % RS, :], hs[:, n % RS, :], c_sb[:, n % 2, :],
                                       ALU.mult).then_inc(hc_done, 1)

            pool.wait_ge(state_zeroed, 1)
            state_group(0)
            with pool.Fori(1, NG) as g:
                state_group(g)
            for n in range(2 * NG):
                result_rstd(n + (NT + NG), GT)
            input_rstd(3)
            pool.wait_ge(dif_ready, 1)
            pool.tensor_tensor(dif[:, 1:2], euler[0:1, 0:1], dif[:, 0:1], ALU.pow).then_inc(dexp_ready, 1)
            with pool.Fori(0, NG) as g:
                result_rstd(g + (NT + 3 * NG), GT)

        @block.tensor
        def _(pe):
            def input_transposes(layer):
                for g in range(NG):
                    n = NG * layer + g
                    pe.wait_ge(xn_ready, n + 1)
                    if n >= 2:
                        pe.wait_ge(xT_ready, n - 1)
                    for k in range(GT):
                        last = pe.transpose(bank[6 + g % 2][:, k * P:(k + 1) * P], xn[:, GT * g + k, :], ident[:])
                    last.then_inc(xT_filled, 1)

            pe.wait_ge(const_in, 32)
            input_transposes(0)

            def attention_slot(s, odd, first=False, last=False, inter=True):
                now, old = odd, 1 - odd

                def bank_free(job):
                    n = use_of(s, job)
                    if not (isinstance(n, int) and n == 1):
                        pe.wait_ge(drained[bank_of(job)], n - 1)

                def copied(slot, job):
                    pe.wait_ge(drained[bank_of(job)], use_of(slot, job))

                def done(job, ins):
                    ins.then_inc(filled[bank_of(job)], 1)

                def w_job(w):
                    job = f"w{w}"
                    bank_free(job)
                    if w == 0:
                        copied(s - 1, "a1")
                        copied(s - 1, "kt0")
                        copied(s - 1, "kt1")
                    else:
                        copied(s - 1, "a2")
                        copied(s - 1, "a3")
                    if inter:
                        pe.wait_ge(S_copied, s - 1)
                    b = bank[bank_of(job)]
                    for i in range(4):
                        p = 4 * w + i
                        for r in range(2):
                            h = 2 * p + r
                            ins = pe.matmul(b[DK * r:DK * r + DK, i * P:(i + 1) * P], k_tok[:, h * DK:(h + 1) * DK],
                                            a_T[:, h * P:(h + 1) * P], start=(i == 0), stop=not inter,
                                            skip_group_check=True)
                        if inter:
                            for r in range(2):
                                ins = pe.matmul(b[DK * r:DK * r + DK, i * P:(i + 1) * P], S_sb[:, p * DK:(p + 1) * DK],
                                                q_pad[old][:, p, r, :], start=False, stop=True,
                                                skip_group_check=True)
                    done(job, ins)

                def state_update(target, keys, values, sem_done):
                    for p in range(NP):
                        for r in range(2):
                            h = 2 * p + r
                            ins = pe.matmul(target[DK * r:DK * r + DK, p * DK:(p + 1) * DK],
                                            keys[:, h * DK:(h + 1) * DK], values[:, h * DK:(h + 1) * DK],
                                            start=(not inter and p == 0), stop=True, skip_group_check=True)
                    ins.then_inc(sem_done, 1)

                def projection(job, w_sb):
                    bank_free(job)
                    for i in range(4):
                        p = 4 * int(job[-1]) + i
                        ins = pe.matmul(bank[bank_of(job)][:, i * P:(i + 1) * P], w_sb[:, p * P:(p + 1) * P],
                                        xt[now], start=True, stop=True)
                    done(job, ins)

                def scores(job, keys, queries):
                    for i in range(2):
                        p = 2 * int(job[-1]) + i
                        ins = pe.matmul(bank[bank_of(job)][:, i * 2 * P:(i + 1) * 2 * P], keys[:, p * P:(p + 1) * P],
                                        queries[:, p, :, :].rearrange("p r t -> p (r t)"), start=True, stop=True)
                    done(job, ins)

                def turn(job, src):
                    for i in range(4):
                        p = 4 * int(job[-1]) + i
                        ins = pe.transpose(bank[bank_of(job)][:, i * P:(i + 1) * P], src[:, p * P:(p + 1) * P], ident[:])
                    done(job, ins)

                if not first:
                    w_job(0)
                    w_job(1)
                    if not last:
                        if not inter:
                            pe.wait_ge(xT_ready, NG)
                        state_update(bank[6], k_tok, k_tok, S_updated)
                if not last:
                    pe.wait_ge(xt_ready, s + 1)
                    if first:
                        pe.wait_ge(qkv_in, 48)
                    projection("q0", Wq)
                    projection("q1", Wq)
                if not first:
                    for n in range(4):
                        bank_free(f"b{n}")
                        if n < 3:
                            copied(s, f"w{n // 2}")
                        scores(f"b{n}", w_T, q_pad[old])
                if not last:
                    projection("k0", Wk)
                    projection("k1", Wk)
                if not first:
                    bank_free("wt0")
                    turn("wt0", w_T)
                    bank_free("wt1")
                    turn("wt1", w_T)
                if not last:
                    for n in range(2):
                        bank_free(f"v{n}")
                        done(f"v{n}", pe.matmul(bank[bank_of(f"v{n}")][:], xt[now], Wv[:, n * G:(n + 1) * G],
                                                start=True, stop=True))
                if not first:
                    for n in range(2):
                        job = f"o{n}"
                        bank_free(job)
                        copied(s, f"b{2 * n}")
                        copied(s, f"b{2 * n + 1}")
                        if n == 0:
                            copied(s - 1, "v0")
                            copied(s - 1, "v1")
                        if inter:
                            pe.wait_ge(C_copied, s - 1)
                        b = bank[bank_of(job)]
                        for i in range(4):
                            p = 4 * n + i
                            for r in range(2):
                                h = 2 * p + r
                                ins = pe.matmul(b[DK * r:DK * r + DK, i * P:(i + 1) * P],
                                                v_tok[old][:, h * DK:(h + 1) * DK], b_T[:, h * P:(h + 1) * P],
                                                start=(i == 0), stop=not inter, skip_group_check=True)
                            if inter:
                                for r in range(2):
                                    ins = pe.matmul(b[DK * r:DK * r + DK, i * P:(i + 1) * P],
                                                    C_sb[:, p * DK:(p + 1) * DK], q_pad[old][:, p, r, :],
                                                    start=False, stop=True, skip_group_check=True)
                        done(job, ins)
                    if not last:
                        copied(s, "wt0")
                        copied(s, "wt1")
                        state_update(bank[7], w_tok, v_tok[old], C_updated)
                if not last:
                    bank_free("kt0")
                    copied(s, "k0")
                    turn("kt0", k_T)
                    bank_free("kt1")
                    copied(s, "k1")
                    turn("kt1", k_T)
                    for n in range(4):
                        bank_free(f"a{n}")
                        if n % 2 == 0:
                            copied(s, f"q{n // 2}")
                        scores(f"a{n}", k_T, q_pad[now])
                if not first:
                    bank_free("y")
                    copied(s, "o0")
                    copied(s, "o1")
                    if not inter:
                        pe.wait_ge(wo_in, 16)
                    for p in range(NP):
                        ins = pe.matmul(bank[bank_of("y")][:, 0:D], o_T[:, p * P:(p + 1) * P], Wo[:, p, :],
                                        start=(p == 0), stop=(p == NP - 1))
                    done("y", ins)

            attention_slot(0, 0, first=True)
            attention_slot(1, 1, inter=False)
            with pe.Fori(0, (NT - 2) // 2) as i:
                for u in range(2):
                    attention_slot(i * 2 + (2 + u), u)
            attention_slot(NT, 0, last=True)

            input_transposes(1)
            pe.wait_ge(moe_in, 16 * 9)
            pe.wait_ge(xT_ready, 2 * NG)
            for t in range(NT):
                ins = pe.matmul(bank[5][:, t * E0:(t + 1) * E0], xT[:, t * P:(t + 1) * P], routerT[:],
                                start=True, stop=True)
            ins.then_inc(logit_filled, 1)
            with pe.Fori(0, NG) as g:
                def expert_out(e):
                    j = min(e, E0)
                    b = bank[4 + j % 2]
                    pe.wait_ge(hid_ready, g * 20 + (2 + 2 * e + 2))
                    if e <= E0:
                        pe.wait_ge(acc_done, g * (E0 + 1) + (j if j == 0 else j - 1) + 1)
                    for k in range(GT):
                        for m in range(2):
                            ins = pe.matmul(b[:, k * P:(k + 1) * P], hid[:, e % 2, m, k * P:(k + 1) * P],
                                            w2T[:, e, m, :], start=(k == 0 and m == 0 and e <= E0), stop=(m == 1),
                                            skip_group_check=True)
                    ins.then_inc(ye_filled, 1)

                for e in range(E0 + NSH):
                    for m in range(2):
                        pe.wait_ge(hid_ready, g * 20 + (2 * e + m + 1))
                        pe.matmul(bank[2 * m][:], w1T[:, e, m * P:(m + 1) * P], xT[:, bass.ds(g * G, G)],
                                  start=True, stop=True)
                        pe.matmul(bank[2 * m + 1][:], w3T[:, e, m * P:(m + 1) * P], xT[:, bass.ds(g * G, G)],
                                  start=True, stop=True).then_inc(ab_filled, 1)
                    if e:
                        expert_out(e - 1)
                expert_out(E0 + NSH - 1)

            input_transposes(2)
            pe.wait_ge(ssm_in, 16 * 13)
            pe.wait_ge(acc_done, NG * (E0 + 1) + 1)
            for g in range(NG):
                pe.wait_ge(xT_ready, 2 * NG + g + 1 + (1 if g == 2 else 0))
                if g == 2:
                    pe.wait_ge(xT_ready, 3 * NG)
                pe.matmul(bank[g][0:96, :], W_BC3[:], xT[:, g * G:(g + 1) * G], start=True, stop=True)
                pe.matmul(bank[4 + g][:], W_delta[:], xT[:, g * G:(g + 1) * G], start=True,
                          stop=True).then_inc(zbc_filled, 1)

            def y_sum(g, n):
                pe.wait_ge(hc_done, g * NS + (n + 1))
                if n == 0 and not isinstance(g, int):
                    pe.wait_ge(yT_ready, g)
                pe.matmul(bank[5][:], ident[:], hc[:, n % RS, :], start=(n == 0), stop=(n == NS - 1),
                          skip_group_check=True).then_inc(yacc_done, 1)

            def state_group(g):
                first = isinstance(g, int)
                for n in range(NS):
                    step = g * NS + n
                    if not (first and n < 2):
                        pe.wait_ge(drive_done, step - 1)
                    elif n == 0:
                        pe.wait_ge(bc_ready, NG)
                        pe.wait_ge(delta_ready, NG)
                    pe.matmul(bank[n % 2][:], select[:, n, :], bc[:, bass.ds(g * G, G)], start=True,
                              stop=True).then_inc(B_filled, 1)
                    if not (first and n == 0):
                        pe.wait_ge(C_copied_out, step)
                    pe.matmul(bank[2][:], select[:, NS + n, :], bc[:, bass.ds(g * G, G)], start=True,
                              stop=True).then_inc(C_filled, 1)
                    if n >= 2:
                        y_sum(g, n - 2)
                    elif not first:
                        y_sum(g - 1, NS - 2 + n)

            state_group(0)
            with pe.Fori(1, NG) as g:
                state_group(g)
            y_sum(NG - 1, NS - 2)
            y_sum(NG - 1, NS - 1)

            def tail_in(g):
                pe.wait_ge(yT_ready, g + 1)
                if g >= 2:
                    pe.wait_ge(yn_ready, g - 1)
                for k in range(GT):
                    ins = pe.transpose(bank[g % 2][:, k * P:(k + 1) * P], y_T[:, g * G + k * P:g * G + (k + 1) * P],
                                       ident[:])
                ins.then_inc(ytok_filled, 1)

            tail_in(0)
            tail_in(1)
            for g in range(NG):
                pe.wait_ge(yn_ready, g + 1)
                if g >= 2:
                    pe.wait_ge(zT_ready, g - 1)
                for k in range(GT):
                    ins = pe.transpose(bank[2 + g % 2][:, k * P:(k + 1) * P], y_n[:, g % 2, k * P:(k + 1) * P], ident[:])
                ins.then_inc(zT_filled, 1)
                if g + 2 < NG:
                    tail_in(g + 2)
                pe.wait_ge(zT_ready, g + 1)
                if g >= 2:
                    pe.wait_ge(ctx_drained, g - 1)
                for k in range(GT):
                    ins = pe.matmul(bank[6 + g % 2][:, k * P:(k + 1) * P], z_T[:, g % 2, k * P:(k + 1) * P], W_ctx[:],
                                    start=True, stop=True)
                ins.then_inc(ctx_filled, 1)
            pe.wait_ge(ctx_drained, NG)

            input_transposes(3)
            pe.wait_ge(wr_in, 16)
            pe.wait_ge(pooled_ready, 1)
            pe.matmul(bank[0][0:1, 0:E1], pooled[:, 1:2], Wr[:], start=True, stop=True).then_inc(lg_filled, 1)
            pe.wait_ge(wrow_ready, 1)
            pe.wait_ge(w2_in, 64)
            pe.matmul(bank[1][:, 0:2], ones[0:1, :], wrow[:], start=True, stop=True)
            pe.matmul(bank[1][:, P:3 * P], ones[0:1, :], b2s[:], start=True, stop=True).then_inc(wb_filled, 1)
            pe.wait_ge(w1_in, 64)
            pe.wait_ge(wb_ready, 1)
            with pe.Fori(0, NG) as g:
                def out_part(v):
                    pe.wait_ge(gelu_done, g * (2 * NF) + (v + 4) + 1)
                    if v == 0:
                        pe.wait_ge(fv_ready, g + 1)
                    for k in range(GT):
                        ins = pe.matmul(bank[4][:, k * P:(k + 1) * P], hg[v][:, k * P:(k + 1) * P], w2w[:, v, :],
                                        start=(v == 0 and k == 0), stop=(v == 2 * NF - 1), skip_group_check=True)
                    ins.then_inc(yv_done, 1)

                for v in range(2 * NF):
                    pe.wait_ge(gelu_done, g * (2 * NF) + v + 1)
                    pe.matmul(bank[v % 4][:], w1s[:, v // NF, (v % NF) * P:(v % NF + 1) * P],
                              xT[:, bass.ds(g * G, G)], start=True, stop=True).then_inc(hf_filled, 1)
                    if v >= 2:
                        out_part(v - 2)
                out_part(2 * NF - 2)
                out_part(2 * NF - 1)

        @block.scalar
        def _(act):
            def input_copies(layer):
                for g in range(NG):
                    act.wait_ge(xT_filled, NG * layer + g + 1)
                    act.activation(xT[:, g * G:(g + 1) * G], bank[6 + g % 2][:], ACT.Copy).then_inc(xT_ready, 1)

            input_copies(0)

            def tile_input(s, odd):
                act.wait_ge(xT_ready, NG)
                act.activation(xt[odd], xT[:, s * P:(s + 1) * P] if isinstance(s, int) else xT[:, bass.ds(s * P, P)],
                               ACT.Copy).then_inc(xt_ready, 1)

            def attention_slot(s, odd, first=False, last=False):
                now = odd

                def copy(job, dst):
                    act.wait_ge(filled[bank_of(job)], use_of(s, job))
                    act.activation(dst, bank[bank_of(job)][:], ACT.Copy).then_inc(drained[bank_of(job)], 1)

                def copy_padded(job):
                    act.wait_ge(filled[bank_of(job)], use_of(s, job))
                    p = slice(4 * int(job[-1]), 4 * int(job[-1]) + 4)
                    for r in range(2):
                        half = slice(DK * r, DK * r + DK)
                        ins = act.activation(q_pad[now][half, p, r, :],
                                             bank[bank_of(job)][half, :].rearrange("p (n t) -> p n t", n=4), ACT.Copy)
                    ins.then_inc(drained[bank_of(job)], 1)

                if not first:
                    copy("w0", w_T[:, 0:G])
                    copy("w1", w_T[:, G:2 * G])
                if not last:
                    copy_padded("q0")
                    copy_padded("q1")
                    copy("k0", k_T[:, 0:G])
                    copy("k1", k_T[:, G:2 * G])
                if not first:
                    copy("wt0", w_tok[:, 0:G])
                    copy("wt1", w_tok[:, G:2 * G])
                if not last:
                    copy("v0", v_tok[now][:, 0:G])
                    copy("v1", v_tok[now][:, G:2 * G])
                    if not (isinstance(s, int) and s == NT - 1):
                        tile_input(s + 1, 1 - odd)
                if not first:
                    copy("o0", o_T[:, 0:G])
                    copy("o1", o_T[:, G:2 * G])
                if not last:
                    copy("kt0", k_tok[:, 0:G])
                    copy("kt1", k_tok[:, G:2 * G])

            act.wait_ge(pad_zeroed, 2)
            tile_input(0, 0)
            attention_slot(0, 0, first=True)
            attention_slot(1, 1)
            with act.Fori(0, (NT - 2) // 2 - 1) as i:
                for u in range(2):
                    attention_slot(i * 2 + (2 + u), u)
            attention_slot(NT - 2, 0)
            attention_slot(NT - 1, 1)
            attention_slot(NT, 0, last=True)

            input_copies(1)
            with act.Fori(0, NG) as g:
                for e in range(E0 + NSH):
                    for m in range(2):
                        act.wait_ge(ab_filled, g * 20 + (2 * e + m + 1))
                        act.wait_ge(hid_ready, g * 20 + (2 * e + m + 1))
                        act.activation(sil[:, m, :], bank[2 * m][:], ACT.Silu).then_inc(sil_ready, 1)

            input_copies(2)
            act.wait_ge(ssm_in, 16 * 13)
            act.activation(expA[:], expA[:], ACT.Exp).then_inc(expA_ready, 1)
            act.wait_ge(negA_ready, 1)
            for g in range(NG):
                act.wait_ge(zbc_filled, g + 1)
                act.activation(soft[:, g * G:(g + 1) * G], bank[4 + g][:], ACT.Abs).then_inc(z_step, 1)
            for g in range(NG):
                act.wait_ge(z_step, g + 1)
                act.activation(soft[:, g * G:(g + 1) * G], soft[:, g * G:(g + 1) * G], ACT.Exp,
                               scale=-1.0).then_inc(z_step, 1)
            for g in range(NG):
                act.wait_ge(z_step, NG + g + 1)
                act.activation(soft[:, g * G:(g + 1) * G], soft[:, g * G:(g + 1) * G], ACT.Ln,
                               bias=1.0).then_inc(zlog_ready, 1)

            def y_copy(g):
                act.wait_ge(yacc_done, g * NS + NS)
                act.activation(wait_slot[:], neg_half[:, 0:1], ACT.Copy)
                dst = y_T[:, g * G:(g + 1) * G] if isinstance(g, int) else y_T[:, bass.ds(g * G, G)]
                act.activation(dst, bank[5][:], ACT.Copy).then_inc(yT_ready, 1)

            act.wait_ge(delta_ready, NG)

            def state_group(g):
                first = isinstance(g, int)
                for n in range(NS):
                    step = g * NS + n
                    if n == 0:
                        if not first:
                            act.wait_ge(decay_ready, g * NS)
                            act.activation(wait_slot[:], neg_half[:, 0:1], ACT.Copy)
                        act.activation(delta_g, delta[:, bass.ds(g * G, G)], ACT.Copy).then_inc(delta_copied, 1)
                        act.wait_ge(delta_copied, g + 1)
                    if not (first and n < 2):
                        act.wait_ge(scan_done, step - 1)
                    act.activation(bank[3 + n % 2][:], delta_g, ACT.Exp,
                                   scale=negA[:, n:n + 1]).then_inc(decay_ready, 1)
                    act.wait_ge(C_filled, step + 1)
                    if not (first and n < 2):
                        act.wait_ge(hc_done, step - 1)
                    act.activation(c_sb[:, n % 2, :], bank[2][:], ACT.Copy).then_inc(C_copied_out, 1)
                    if n == 2 and not first:
                        y_copy(g - 1)

            state_group(0)
            with act.Fori(1, NG) as g:
                state_group(g)
            y_copy(NG - 1)
            for g in range(NG + 1):
                if g < NG:
                    act.wait_ge(zT_filled, g + 1)
                    if g >= 2:
                        act.wait_ge(ctx_filled, g - 1)
                    act.activation(z_T[:, g % 2, :], bank[2 + g % 2][:], ACT.Identity, scale=gamma[:, 0:1],
                                   bias=beta[:, 0:1]).then_inc(zT_ready, 1)
                if g:
                    act.wait_ge(ctx_filled, g)
                    if g >= 3:
                        act.wait_ge(x_summed, g - 2)
                    act.activation(ctx_v[:, (g - 1) % 2, :], bank[6 + (g - 1) % 2][:], ACT.Copy,
                                   scale=ctx_scale[:, 0:1]).then_inc(ctx_drained, 1)

            input_copies(3)
            act.wait_ge(w1_in, 64)
            with act.Fori(0, NG) as g:
                for v in range(2 * NF):
                    act.wait_ge(hf_filled, g * (2 * NF) + (v + 1))
                    act.wait_ge(yv_done, g * (2 * NF) + v + 1)
                    act.activation(hg[v], bank[v % 4][:], ACT.Gelu,
                                   bias=b1s[:, v // NF, v % NF:v % NF + 1]).then_inc(gelu_done, 1)

        @block.vector
        def _(dve):
            n_steps = Steps(dve, n_step)

            def input_norm(layer):
                def normalise(g):
                    dve.wait_ge(n_rstd_ready, NG * layer + g + 1)
                    if layer:
                        dve.wait_ge(xT_filled, NG * layer - NG + g + 1)
                    for k in range(GT):
                        t = GT * g + k
                        ins = dve.tensor_scalar(xn[:, t, :], x[:, t, :], n_mv[:, layer, t, 0:1],
                                                n_rstd[:, layer, t:t + 1], ALU.subtract, ALU.mult)
                    ins.then_inc(xn_ready, 1)

                for g in range(NG):
                    if layer == 0:
                        dve.wait_ge(x_in[g], 16)
                    for k in range(GT):
                        ins = dve.bn_stats(n_stats[:, layer, GT * g + k, :], x[:, GT * g + k, :])
                    n_steps.mark(ins)
                    n_steps.wait()
                    for k in range(GT):
                        ins = dve.bn_aggr(n_mv[:, layer, GT * g + k, :], n_stats[:, layer, GT * g + k, :])
                    n_steps.mark(ins)
                    n_steps.wait()
                    dve.tensor_scalar(n_var[:, layer, GT * g:GT * g + GT], n_mv[:, layer, GT * g:GT * g + GT, 1],
                                      EPS, None, ALU.add).then_inc(n_var_ready, 1)
                    if g:
                        normalise(g - 1)
                normalise(NG - 1)

            def result_stats(steps, srcs, n_count):
                k_all = len(srcs)
                for k, src in enumerate(srcs):
                    ins = dve.bn_stats(r_stats[:, k, :], src)
                steps.mark(ins)
                steps.wait()
                dve.memset(r_var[:, 0:k_all], 0.0)
                for k in range(k_all):
                    ins = dve.bn_aggr(r_mv[:, k, :], r_stats[:, k, :])
                steps.mark(ins)
                steps.wait()
                dve.tensor_scalar(r_var[:, 0:k_all], r_mv[:, 0:k_all, 1], EPS, None, ALU.add).then_inc(r_var_ready, 1)
                dve.wait_ge(r_rstd_ready, n_count)

            input_norm(0)

            dve.wait_ge(const_in, 32)

            def attention_slot(s, first=False, last=False):
                def masked(job, dst):
                    dve.wait_ge(filled[bank_of(job)], use_of(s, job))
                    dve.tensor_tensor(dst, bank[bank_of(job)][:], mask[:], ALU.mult)\
                       .then_inc(drained[bank_of(job)], 1)

                if not first and not last:
                    dve.wait_ge(S_updated, s)
                    dve.tensor_copy(S_sb, bank[6][:]).then_inc(S_copied, 1)
                if not first:
                    for n in range(4):
                        masked(f"b{n}", b_T[:, n * G:(n + 1) * G])
                    if not last:
                        dve.wait_ge(C_updated, s)
                        dve.tensor_copy(C_sb, bank[7][:]).then_inc(C_copied, 1)
                if not last:
                    for n in range(4):
                        masked(f"a{n}", a_T[:, n * G:(n + 1) * G])
                if not first:
                    y = bank[bank_of("y")][:, 0:D]
                    dve.wait_ge(filled[bank_of("y")], use_of(s, "y"))
                    steps = Steps(dve, y_step, (s - 1) * 2)
                    result_stats(steps, [y], s)
                    dve.tensor_scalar(r_val[:, 0, :], y, r_mv[:, 0, 0:1], r_rstd[:, 0:1], ALU.subtract, ALU.mult)\
                       .then_inc(drained[bank_of("y")], 1)
                    dve.wait_ge(drained[bank_of("y")], use_of(s, "y"))
                    row = x[:, s - 1, :] if isinstance(s, int) else x[:, bass.ds(s - 1, 1), :].rearrange("p a d -> p (a d)")
                    dve.tensor_tensor(row, row, r_val[:, 0, :], ALU.add).then_inc(x_added, 1)

            attention_slot(0, first=True)
            attention_slot(1)
            with dve.Fori(2, NT) as s:
                attention_slot(s)
            attention_slot(NT, last=True)
            dve.wait_ge(x_added, NT)

            input_norm(1)
            dve.wait_ge(moe_in, 16 * 9)
            dve.wait_ge(logit_filled, 1)
            route = Steps(dve, route_step)

            def step(ins):
                route.mark(ins)
                route.wait()

            def wide(v):
                return v.unsqueeze(2).to_broadcast([P, NT, E0])

            step(dve.tensor_tensor(logit[:], bank[5][:, 0:NT * E0].rearrange("p (t e) -> p t e", t=NT), bias[:], ALU.add))
            for c in range(2):
                step(dve.tensor_reduce(top[:, c, :], logit[:], AX.X, ALU.max))
                step(dve.tensor_tensor(hit[:], logit[:], wide(top[:, c, :]), ALU.is_equal))
                step(dve.tensor_tensor(hit[:], hit[:], rank[:], ALU.mult))
                step(dve.tensor_reduce(place[:, c, :], hit[:], AX.X, ALU.min))
                step(dve.tensor_tensor(pick[:, c], rank[:], wide(place[:, c, :]), ALU.is_equal))
                if c == 0:
                    step(dve.scalar_tensor_tensor(out=logit[:], in0=pick[:, 0], scalar=-3e38, in1=logit[:],
                                                  op0=ALU.mult, op1=ALU.add))
            dve.tensor_tensor(gate[:, 0, :], top[:, 1, :], top[:, 0, :], ALU.subtract).then_inc(gate_dif, 1)
            dve.wait_ge(gate_exp, 1)
            step(dve.tensor_scalar(gate[:, 2, :], gate[:, 1, :], 1.0, None, ALU.add))
            step(dve.reciprocal(gate[:, 2, :], gate[:, 2, :]))
            step(dve.tensor_tensor(gate[:, 3, :], gate[:, 1, :], gate[:, 2, :], ALU.mult))
            step(dve.tensor_tensor(pick[:, 0], pick[:, 0], wide(gate[:, 2, :]), ALU.mult))
            step(dve.tensor_tensor(pick[:, 1], pick[:, 1], wide(gate[:, 3, :]), ALU.mult))
            dve.tensor_tensor(combine[:], pick[:, 0], pick[:, 1], ALU.add).then_inc(hid_ready, 2)

            def residual_group(g, srcs, steps, n_count):
                result_stats(steps, srcs, n_count)
                for k, src in enumerate(srcs):
                    ins = dve.tensor_scalar(r_val[:, k, :], src, r_mv[:, k, 0:1], r_rstd[:, k:k + 1],
                                            ALU.subtract, ALU.mult)
                steps.mark(ins)
                steps.wait()
                rows = x[:, bass.ds(g * GT, GT), :]
                return dve.tensor_tensor(rows, rows, r_val[:], ALU.add)

            dve.wait_ge(hid_ready, 2)
            with dve.Fori(0, NG) as g:
                def add_expert(e):
                    j = min(e, E0)
                    b = bank[4 + j % 2]
                    dve.wait_ge(ye_filled, g * 10 + (e + 2) + 1)
                    dve.wait_ge(acc_done, g * (E0 + 1) + j + 1)
                    if e < E0:
                        for k in range(GT):
                            w = combine[:, bass.ds(g * GT + k, 1), e:e + 1].rearrange("p a b -> p (a b)")
                            if e == 0:
                                ins = dve.tensor_scalar(acc[:, k, :], b[:, k * P:(k + 1) * P], w, None, ALU.mult)
                            else:
                                ins = dve.scalar_tensor_tensor(out=acc[:, k, :], in0=b[:, k * P:(k + 1) * P], scalar=w,
                                                               in1=acc[:, k, :], op0=ALU.mult, op1=ALU.add)
                    else:
                        ins = dve.tensor_tensor(acc[:], b[:].rearrange("p (k d) -> p k d", k=GT), acc[:], ALU.add)
                    ins.then_inc(acc_done, 1)

                for e in range(E0 + NSH):
                    for m in range(2):
                        dve.wait_ge(sil_ready, g * 20 + (2 * e + m + 1))
                        dve.wait_ge(ye_filled, g * 10 + e + 1)
                        dve.tensor_tensor(hid[:, e % 2, m, :], bank[2 * m + 1][:], sil[:, m, :], ALU.mult)\
                           .then_inc(hid_ready, 1)
                    if 1 <= e <= E0:
                        add_expert(e - 1)
                add_expert(E0 + NSH - 1)
                dve.wait_ge(acc_done, g * (E0 + 1) + (E0 + 1) + 1)
                steps = Steps(dve, moe_step, g * 4)
                steps.mark(residual_group(g, [acc[:, k, :] for k in range(GT)], steps, g + (NT + 1)))
                steps.wait()

            input_norm(2)
            dve.wait_ge(expA_ready, 1)
            dve.tensor_scalar(negA[:], expA[:], -1.0, None, ALU.mult).then_inc(negA_ready, 1)
            head = Steps(dve, head_step)
            for g in range(NG):
                cols = slice(g * G, (g + 1) * G)
                dve.wait_ge(zbc_filled, g + 1)
                head.mark(dve.tensor_copy(bc[:, cols], bank[g][0:96, :]))
                head.wait()
                head.mark(dve.tensor_tensor(bc_rest, bank[g][0:96, :], bc[:, cols], ALU.subtract))
                head.wait()
                head.mark(dve.tensor_copy(bc_mid[:], bc_rest))
                head.wait()
                dve.tensor_copy(bc[32:64, cols], bc_mid[32:64, :])
                dve.tensor_tensor(bc[64:96, cols], bc_rest[64:96, :], bc_mid[64:96, :],
                                  ALU.subtract).then_inc(bc_ready, 1)
            for g in range(NG):
                cols = slice(g * G, (g + 1) * G)
                dve.wait_ge(zlog_ready, g + 1)
                dve.scalar_tensor_tensor(out=delta[:, cols], in0=bank[4 + g][:], scalar=0.0, in1=soft[:, cols],
                                         op0=ALU.max, op1=ALU.add).then_inc(delta_ready, 1)
            dve.wait_ge(state_zeroed, 1)

            def state_group(g):
                first = isinstance(g, int)

                def drive_n(n):
                    if n == 0:
                        dve.wait_ge(dx_ready, g + 1)
                    dve.wait_ge(B_filled, g * NS + (n + 1))
                    if not (first and n < RS):
                        dve.wait_ge(scan_done, g * NS + n - (RS - 1))
                    dve.tensor_tensor(drive[:, n % RS, :], dx[:, bass.ds(g * G, G)], bank[n % 2][:], ALU.mult)\
                       .then_inc(drive_done, 1)

                drive_n(0)
                for n in range(NS):
                    step = g * NS + n
                    if n + 1 < NS:
                        drive_n(n + 1)
                    dve.wait_ge(decay_ready, step + 1)
                    dve.wait_ge(drive_done, step + 1)
                    if not (first and n < RS):
                        dve.wait_ge(state_saved, step - (RS - 1))
                        dve.wait_ge(hc_done, step - (RS - 1))
                    dve.tensor_tensor_scan(hs[:, n % RS, :], bank[3 + n % 2][:], drive[:, n % RS, :],
                                           state[:, n:n + 1], ALU.mult, ALU.add).then_inc(scan_done, 1)

            state_group(0)
            with dve.Fori(1, NG) as g:
                state_group(g)

            tail = Steps(dve, tail_step)
            for g in range(NG + 1):
                if g < NG:
                    dve.wait_ge(ytok_filled, g + 1)
                    yt = [bank[g % 2][:, k * P:(k + 1) * P] for k in range(GT)]
                    result_stats(tail, yt, NT + NG + max(2 * g, 1))
                    if g >= 2:
                        dve.wait_ge(zT_filled, g - 1)
                    for k in range(GT):
                        ins = dve.tensor_scalar(y_n[:, g % 2, k * P:(k + 1) * P], yt[k], r_mv[:, k, 0:1],
                                                r_rstd[:, k:k + 1], ALU.subtract, ALU.mult)
                    ins.then_inc(yn_ready, 1)
                if g:
                    o = g - 1
                    dve.wait_ge(ctx_drained, g)
                    residual_group(o, [ctx_v[:, o % 2, k * P:(k + 1) * P] for k in range(GT)], tail,
                                   NT + NG + min(2 * g + 1, 2 * NG)).then_inc(x_summed, 1)
            dve.wait_ge(x_summed, NG)

            input_norm(3)
            dve.wait_ge(xT_ready, 4 * NG)
            pick_steps = Steps(dve, pick_step)

            def pick_do(ins):
                pick_steps.mark(ins)
                pick_steps.wait()

            pick_do(dve.tensor_reduce(pooled[:, 0:1], xT[:], AX.X, ALU.add))
            dve.tensor_scalar(pooled[:, 1:2], pooled[:, 0:1], 1.0 / T, None, ALU.mult).then_inc(pooled_ready, 1)
            dve.wait_ge(lg_filled, 1)
            pick_do(dve.tensor_copy(lg[:], bank[0][0:1, 0:E1]))
            pick_do(dve.max(top8[:], lg[:]))
            dve.max_index(idx8[:], top8[:], lg[:]).then_inc(idx_ready, 1)
            dve.tensor_tensor(dif[:, 0:1], top8[:, 1:2], top8[:, 0:1], ALU.subtract).then_inc(dif_ready, 1)
            dve.wait_ge(dexp_ready, 1)
            pick_do(dve.tensor_scalar(dif[:, 2:3], dif[:, 1:2], 1.0, None, ALU.add))
            pick_do(dve.reciprocal(wrow[:, 0:1], dif[:, 2:3]))
            dve.tensor_tensor(wrow[:, 1:2], dif[:, 1:2], wrow[:, 0:1], ALU.mult).then_inc(wrow_ready, 1)
            dve.wait_ge(wb_filled, 1)
            dve.wait_ge(w2_in, 64)
            pick_do(dve.tensor_copy(wts[:], bank[1][:, 0:2]))
            for k in range(2):
                dve.tensor_scalar(w2w[:, NF * k:NF * k + NF, :].rearrange("p v d -> p (v d)"), w2s[:, k, :],
                                  wts[:, k:k + 1], None, ALU.mult)
            pick_do(dve.tensor_scalar(b2c[:, 0, :], bank[1][:, P:2 * P], wts[:, 0:1], None, ALU.mult))
            pick_do(dve.scalar_tensor_tensor(out=b2c[:, 0, :], in0=bank[1][:, 2 * P:3 * P], scalar=wts[:, 1:2],
                                             in1=b2c[:, 0, :], op0=ALU.mult, op1=ALU.add))
            for k in range(1, GT):
                ins = dve.tensor_copy(b2c[:, k, :], b2c[:, 0, :])
            ins.then_inc(wb_ready, 1)
            dve.wait_ge(wb_ready, 1)

            with dve.Fori(0, NG) as g:
                dve.wait_ge(yv_done, g * (2 * NF) + (4 * NF - 1) + 1)
                dve.tensor_tensor(f_val, bank[4][:].rearrange("p (k d) -> p k d", k=GT), b2c, ALU.add)\
                   .then_inc(fv_ready, 1)
                dve.wait_ge(fv_ready, g + 1 + 1)
                steps = Steps(dve, ff_step, g * 3)
                residual_group(g, [f_val[:, k, :] for k in range(GT)], steps, g + (NT + 3 * NG + 1)).then_inc(x_final, 1)
                dve.wait_ge(x_final, g + 1)


def kernel(**inputs):
    import ml_dtypes
    import numpy as np

    import concourse.bacc as bacc
    from concourse.bass_utils import run_bass_kernel_spmd as run

    i = {k: np.asarray(v) for k, v in inputs.items()}
    later = np.triu(np.ones((P, P), np.float32))
    select = np.zeros((96, 2 * NS, P), ml_dtypes.bfloat16)
    for c in range(3):
        for n in range(2 * NS):
            select[32 * c + n, n, :] = 1
    arrays = {
        "x": i["L0_attn_x"].reshape(T, D),
        "ident": np.eye(P, dtype=np.float32),
        "mask": np.tile(later, (1, GT)),
        "W_q": i["L0_attn_W_q"], "W_k": i["L0_attn_W_k"], "W_v": i["L0_attn_W_v"], "W_o": i["L0_attn_W_o"],
        "routerT": i["L0_ffn_router_w"].T,
        "bias": np.broadcast_to(i["L0_ffn_expert_bias"], (P, NT, E0)),
        "rank": np.broadcast_to(np.arange(E0, dtype=np.float32) - E0, (P, NT, E0)),
        "w1T": i["L0_ffn_w1"].transpose(2, 0, 1), "sw1T": i["L0_ffn_sw1"].transpose(2, 0, 1),
        "w3T": i["L0_ffn_w3"].transpose(2, 0, 1), "sw3T": i["L0_ffn_sw3"].transpose(2, 0, 1),
        "w2T": i["L0_ffn_w2"].reshape(E0, D, 2, P).transpose(3, 0, 2, 1),
        "sw2T": i["L0_ffn_sw2"].reshape(NSH, D, 2, P).transpose(3, 0, 2, 1),
        "select": select,
        "W_delta": i["L1_attn_W_delta"], "W_B": i["L1_attn_W_B"], "W_C": i["L1_attn_W_C"],
        "W_ctx": i["L1_attn_W_ctx"], "A_log": i["L1_attn_A_log"],
        "gamma": i["L1_attn_ln_gamma"].reshape(D, 1), "beta": i["L1_attn_ln_beta"].reshape(D, 1),
        "ctx_scale": np.broadcast_to(i["L1_attn_context_scale"].reshape(1, 1), (P, 1)),
        "Wr": i["L1_ffn_Wr"], "W1": i["L1_ffn_W1"],
        "b1": i["L1_ffn_b1"].reshape(E1, NF, P).transpose(0, 2, 1),
        "W2": i["L1_ffn_W2"].reshape(E1, NF, P, D).transpose(0, 2, 1, 3).reshape(E1, P, NF * D),
        "b2": i["L1_ffn_b2"],
    }
    arrays = {f"{k}_dram": np.ascontiguousarray(v) for k, v in arrays.items()}
    nc = bacc.Bacc("TRN2", target_bir_lowering=False, num_devices=1)
    aps = {k[:-5]: nc.dram_tensor(k, v.shape, mybir.dt.from_np(v.dtype), kind="ExternalInput").ap()
           for k, v in arrays.items()}
    out = nc.dram_tensor("out_dram", (1, T, D), F32, kind="ExternalOutput").ap()
    sandwich(nc, aps, out)
    r = run(nc, [arrays], core_ids=[0])
    return r.results[0]["out_dram"]
```

```python
from contextlib import ExitStack

import concourse.bass as bass
from concourse import mybir

P = 128
D = 128
T = 2048
NT = T // P
GT = 4
G = GT * P
NG = NT // GT
H, DK = 16, 64
NP = H // 2
E0, NSH, HID = 8, 2, 256
NS = 16
LAG = 3
RS = 4
E1, FF = 8, 512
NF = FF // P
EPS = 1e-5
EULER = 2.718281828459045

ARENA = 20480

F32 = mybir.dt.float32
BF16 = mybir.dt.bfloat16
F32R = mybir.dt.float32r
U32 = mybir.dt.uint32
ALU = mybir.AluOpType
ACT = mybir.ActivationFunctionType
AX = mybir.AxisListType

STAGE1 = ("q0", "q1", "k0", "k1", "v0", "v1", "kt0", "kt1", "a0", "a1", "a2", "a3")
JOBS = ("w0", "w1", "q0", "q1", "b0", "b1", "b2", "b3", "k0", "k1", "wt0", "wt1",
        "v0", "v1", "kt0", "kt1", "o0", "o1", "a0", "a1", "a2", "a3", "y")
RING = 6


def bank_of(job):
    return JOBS.index(job) % RING


def use_of(slot, job, last=NT):
    b = bank_of(job)
    mine = [j for j in JOBS if bank_of(j) == b]
    first = [j for j in mine if j in STAGE1]
    if isinstance(slot, int) and slot == 0:
        return first.index(job) + 1
    if isinstance(slot, int) and slot == last:
        mine_last = [j for j in mine if j not in STAGE1]
        return len(first) + (last - 1) * len(mine) + mine_last.index(job) + 1
    return (slot - 1) * len(mine) + (len(first) + mine.index(job) + 1)


class Steps:

    def __init__(self, eng, sem, base=0):
        self.eng, self.sem, self.base, self.n = eng, sem, base, 0

    def mark(self, ins):
        ins.then_inc(self.sem, 1)
        self.n += 1

    def wait(self):
        self.eng.wait_ge(self.sem, self.base + self.n)


def sandwich(nc, a, out):
    with ExitStack() as ctx:
        def sb(name, shape, dt=F32):
            return ctx.enter_context(nc.sbuf_tensor(name, shape, dt))

        def sem(name):
            return ctx.enter_context(nc.semaphore(name))

        bank = [ctx.enter_context(nc.psum_tensor(f"bank{i}", [P, G], F32)) for i in range(8)]

        ident = sb("ident", [P, P])
        mask = sb("mask", [P, G])
        rank = sb("rank", [P, NT, E0])
        select = sb("select", [96, 2 * NS, P], BF16)
        neg_half = sb("neg_half", [P, NT])
        euler = sb("euler", [P, NT])
        ones = sb("ones", [P, P])

        x = sb("x", [P, NT, D])
        xn = sb("xn", [P, NT, D])
        xT = sb("xT", [P, T])
        n_stats = sb("n_stats", [P, NT, 6])
        n_mv = sb("n_mv", [P, NT, 2])
        n_var = sb("n_var", [P, NT])
        n_rstd = sb("n_rstd", [P, NT])
        r_stats = sb("r_stats", [P, GT, 6])
        r_mv = sb("r_mv", [P, GT, 2])
        r_var = sb("r_var", [P, GT])
        r_rstd = sb("r_rstd", [P, GT])
        r_val = sb("r_val", [P, GT, D])
        r_new = sb("r_new", [P, GT, D])
        m_stats = sb("m_stats", [P, GT, 6])
        m_mv = sb("m_mv", [P, GT, 2])
        m_var = sb("m_var", [P, GT])
        m_rstd = sb("m_rstd", [P, GT])

        Wq = sb("Wq", [P, H * DK])
        Wk = sb("Wk", [P, H * DK])
        Wv = sb("Wv", [P, H * DK])
        Wo = sb("Wo", [P, NP, D])
        Wk_hi, Wk_lo, Wv_hi, Wv_lo = [sb(n, [P, H * DK], F32R) for n in ("Wk_hi", "Wk_lo", "Wv_hi", "Wv_lo")]
        xt_hi, xt_lo = sb("xt_hi", [P, P], F32R), sb("xt_lo", [P, P], F32R)
        w1T = sb("w1T", [P, E0 + NSH, HID])
        w3T = sb("w3T", [P, E0 + NSH, HID])
        w2T = sb("w2T", [P, E0 + NSH, 2, D])
        routerT = sb("routerT", [P, E0])
        bias = sb("bias", [P, NT, E0])
        logit = sb("logit", [P, NT, E0])
        hit = sb("hit", [P, NT, E0])
        pick = sb("pick", [P, 2, NT, E0])
        top = sb("top", [P, 2, NT])
        place = sb("place", [P, 2, NT])
        gate = sb("gate", [P, 4, NT])
        combine = sb("combine", [P, NT, E0])
        W_delta = sb("W_delta", [P, D])
        W_BC3 = sb("W_BC3", [P, 96])
        W_ctx = sb("W_ctx", [P, D])
        negA = sb("negA", [P, NS])
        expA = sb("expA", [P, NS])
        gamma = sb("gamma", [P, 1])
        beta = sb("beta", [P, 1])
        ctx_scale = sb("ctx_scale", [P, 1])
        state = sb("state", [P, NS])
        y_stats = sb("y_stats", [P, GT, 6])
        y_mv = sb("y_mv", [P, GT, 2])
        y_var = sb("y_var", [P, GT])
        y_rstd, y_bias = sb("y_rstd", [P, NG, GT]), sb("y_bias", [P, NG, GT])
        t_rstd, t_bias = sb("t_rstd", [P, NG, GT]), sb("t_bias", [P, NG, GT])
        wait_slot = sb("wait_slot", [P, 1])
        bc = sb("bc", [96, T], BF16)
        bc_mid = sb("bc_mid", [96, G], BF16)
        bc_rest = r_val[0:96].rearrange("p k d -> p (k d)")
        z_all = sb("z_all", [P, (NG - 1) * G])
        wait_slot_v = sb("wait_slot_v", [P, 2])

        Wr = sb("Wr", [P, E1])
        b1s = sb("b1s", [P, 2, NF])
        b2s = sb("b2s", [1, 2 * D])
        pooled = sb("pooled", [P, 2])
        pool_part = sb("pool_part", [P, NG])
        lg = sb("lg", [1, 8])
        top8 = sb("top8", [1, 8])
        idx8 = sb("idx8", [1, 8], U32)
        dif = sb("dif", [1, 4])
        wrow = sb("wrow", [1, 2])
        wts = sb("wts", [P, 2])
        b2c = sb("b2c", [P, 1])

        attention_only = ExitStack()
        arena = attention_only.enter_context(nc.sbuf_tensor("arena", [P, ARENA], F32))
        at = [0]

        def part(n):
            at[0] += n
            assert at[0] <= ARENA
            return arena[:, at[0] - n:at[0]]

        xt = [part(P) for _ in range(2)]
        q_pad = [part(NP * 2 * P).rearrange("p (n r t) -> p n r t", n=NP, r=2) for _ in range(2)]
        v_tok = [part(H * DK) for _ in range(2)]
        k_T = part(NP * P)
        k_tok = part(H * DK)
        a_T = part(H * P)
        w_T = part(NP * P)
        w_tok = part(H * DK)
        b_T = part(H * P)
        o_T = part(NP * P)
        q_T = [part(NP * P) for _ in range(2)]
        S_sb, C_sb = [part(NP * P).rearrange("p (n c) -> p n c", n=NP) for _ in range(2)]

        attention_only.close()
        mixture_only = ExitStack()

        def mx(name, shape, dt=F32):
            return mixture_only.enter_context(nc.sbuf_tensor(name, shape, dt))

        w1_hi, w3_hi, w1_lo, w3_lo = [mx(n, [P, E0 + NSH, HID], F32R) for n in ("w1_hi", "w3_hi", "w1_lo", "w3_lo")]
        xT_hi, xT_lo = mx("xT_hi", [P, T], F32R), mx("xT_lo", [P, T], F32R)
        hid = mx("hid", [P, 2, 2, G])
        moe_out = mx("moe_out", [P, GT, D])
        mixture_only.close()

        def halves(t):
            flat = t[:].rearrange("p e h -> p (e h)")
            return [flat[:, n * 2 * FF:(n + 1) * 2 * FF].rearrange("p (k f) -> p k f", k=2) for n in range(2)]

        w1s_hi, w1s_lo = halves(w1_hi)
        w2w_hi, w2w_lo = halves(w3_hi)
        hg_hi, hg_lo = [[t[:].rearrange("p e h -> p (e h)")[:, n * G:(n + 1) * G] for n in range(RS)]
                        for t in (w1_lo, w3_lo)]
        sil = xn[:, GT:3 * GT, :].rearrange("p (m k) d -> p m (k d)", m=2)
        acc = xn[:, 3 * GT:, :]
        arena = sb("arena_late", [P, ARENA])

        at[0] = 0
        delta, dx, y_T = [part(T) for _ in range(3)]
        drive = part(RS * G).rearrange("p (b t) -> p b t", b=RS)
        c_sb = part(RS * G).rearrange("p (b t) -> p b t", b=RS)
        hs = part(RS * G).rearrange("p (b t) -> p b t", b=RS)
        hc = part(RS * G).rearrange("p (b t) -> p b t", b=RS)
        soft = [hc[:, g, :] for g in range(NG - 1)] + [z_all[:, 0:G]]
        y_n, z_T, ctx_v = [arena[:, i * 2 * G:(i + 1) * 2 * G].rearrange("p (b t) -> p b t", b=2)
                           for i in range(3)]
        B_bank = (0, 1, 6, 7)
        delta_g = part(G)
        at[0] = 4 * (E0 + NSH) * HID + 2 * T
        w1s = part(2 * FF).rearrange("p (k f) -> p k f", k=2)
        w2s = part(2 * FF).rearrange("p (k d) -> p k d", k=2)
        w2w = part(2 * FF).rearrange("p (k d) -> p k d", k=2)
        hg = [part(G) for _ in range(RS)]
        out_T = part(G)

        x_in = [sem(f"x_in{g}") for g in range(NG)]
        ident_in, mask_in = sem("ident_in"), sem("mask_in")
        wq_in, wk_in, wv_in = sem("wq_in"), sem("wk_in"), sem("wv_in")
        wo_in = sem("wo_in")
        moe_in = sem("moe_in")
        ssm_in = sem("ssm_in")
        wr_in = sem("wr_in")
        const_set = sem("const_set")
        n_step = sem("n_step")
        n_var_ready = sem("n_var_ready")
        n_rstd_ready = sem("n_rstd_ready")
        xn_ready = sem("xn_ready")
        xT_filled = sem("xT_filled")
        xT_ready = sem("xT_ready")
        filled = [sem(f"filled{b}") for b in range(RING)]
        drained = [sem(f"drained{b}") for b in range(RING)]
        xt_ready = sem("xt_ready")
        kv_step, Wk_split_ready, Wv_split_ready = sem("kv_step"), sem("Wk_split_ready"), sem("Wv_split_ready")
        xt_step, xt_split_ready = sem("xt_step"), sem("xt_split_ready")
        pad_zeroed = sem("pad_zeroed")
        S_updated, S_copied = sem("S_updated"), sem("S_copied")
        C_updated, C_copied = sem("C_updated"), sem("C_copied")
        y_step = sem("y_step")
        r_var_ready = sem("r_var_ready")
        r_rstd_ready = sem("r_rstd_ready")
        m_var_ready = sem("m_var_ready")
        m_rstd_ready = sem("m_rstd_ready")
        xn_row_ready = sem("xn_row_ready")
        logit_filled = sem("logit_filled")
        w_hi_ready, w_split_ready = sem("w_hi_ready"), sem("w_split_ready")
        x_split_step, x_split_ready = sem("x_split_step"), sem("x_split_ready")
        route_step = sem("route_step")
        gate_dif = sem("gate_dif")
        gate_exp = sem("gate_exp")
        ab_filled = sem("ab_filled")
        sil_ready = sem("sil_ready")
        hid_ready = sem("hid_ready")
        ye_filled = sem("ye_filled")
        acc_done = sem("acc_done")
        moe_step = sem("moe_step")
        expA_ready = sem("expA_ready")
        negA_ready = sem("negA_ready")
        z_filled, bc_filled = sem("z_filled"), sem("bc_filled")
        z_copied = sem("z_copied")
        z_step = sem("z_step")
        zlog_ready = sem("zlog_ready")
        delta_ready = sem("delta_ready")
        dx_ready = sem("dx_ready")
        delta_copied = sem("delta_copied")
        head_step = sem("head_step")
        bc_ready = sem("bc_ready")
        B_filled, C_filled = sem("B_filled"), sem("C_filled")
        C_copied_out = sem("C_copied_out")
        decay_ready = sem("decay_ready")
        drive_done = sem("drive_done")
        scan_done = sem("scan_done")
        hc_done = sem("hc_done")
        state_zeroed = sem("state_zeroed")
        state_saved = sem("state_saved")
        yacc_done = sem("yacc_done")
        yT_ready = sem("yT_ready")
        ytok_filled = sem("ytok_filled")
        yn_ready = sem("yn_ready")
        zT_filled = sem("zT_filled")
        zT_ready = sem("zT_ready")
        ctx_filled = sem("ctx_filled")
        ctx_drained = sem("ctx_drained")
        tail_step = sem("tail_step")
        y_var_ready, y_rstd_ready = sem("y_var_ready"), sem("y_rstd_ready")
        y_bias_ready, t_bias_ready = sem("y_bias_ready"), sem("t_bias_ready")
        r_scaled = sem("r_scaled")
        pooled_ready = sem("pooled_ready")
        lg_filled = sem("lg_filled")
        pick_step = sem("pick_step")
        idx_ready = sem("idx_ready")
        dif_ready = sem("dif_ready")
        dexp_ready = sem("dexp_ready")
        wrow_ready = sem("wrow_ready")
        w1_in = [sem(f"w1_in{k}") for k in range(2)]
        w2_in = [sem(f"w2_in{k}") for k in range(2)]
        b1_in, b2_in, b2_filled = sem("b1_in"), sem("b2_in"), sem("b2_filled")
        xf_step, xf_split_ready = sem("xf_step"), sem("xf_split_ready")
        w1s_step, w1s_split_ready = sem("w1s_step"), sem("w1s_split_ready")
        w2w_step, w2w_split_ready = sem("w2w_step"), sem("w2w_split_ready")
        wb_filled = sem("wb_filled")
        wb_ready = sem("wb_ready")
        hf_filled = sem("hf_filled")
        gelu_done = sem("gelu_done")
        yv_done = sem("yv_done")
        hg_hi_ready = sem("hg_hi_ready")
        hg_lo_pool, hg_lo_dve = sem("hg_lo_pool"), sem("hg_lo_dve")
        out_T_ready, out_filled, out_drained = sem("out_T_ready"), sem("out_filled"), sem("out_drained")
        ff_step = sem("ff_step")
        x_final = sem("x_final")
        out_done = sem("out_done")

        NV = 2 * NF

        def wait_hidden_split(eng, g, v):
            if v < 0:
                g, v = g - 1, v + NV
            if v % RS == RS - 1:
                eng.wait_ge(hg_lo_dve, g * (NV // RS) + (v // RS + 1))
            else:
                eng.wait_ge(hg_lo_pool, g * (NV - NV // RS) + (v - v // RS + 1))

        block = ctx.enter_context(nc.Block())
        x_dram = a["x"].rearrange("(t p) d -> p t d", p=P)
        out_dram = out.rearrange("a (t p) d -> p (a t) d", p=P)

        @block.sync
        def _(sp):
            def load_x(g):
                sp.dma_start(x[:, GT * g:GT * g + GT, :], x_dram[:, GT * g:GT * g + GT, :]).then_inc(x_in[g], 16)

            load_x(0)
            sp.dma_start(ident[:], a["ident"]).then_inc(ident_in, 16)
            sp.dma_start(Wq[:], a["W_q"]).then_inc(wq_in, 16)
            sp.dma_start(Wk[:], a["W_k"]).then_inc(wk_in, 16)
            sp.dma_start(Wv[:], a["W_v"]).then_inc(wv_in, 16)
            sp.dma_start(mask[:], a["mask"]).then_inc(mask_in, 16)
            for g in range(1, NG):
                load_x(g)
            sp.dma_start(Wo[:], a["W_o"].rearrange("(n p) d -> p n d", p=P)).then_inc(wo_in, 16)
            sp.dma_start(routerT[:], a["routerT"]).then_inc(moe_in, 16)
            sp.dma_start(bias[:], a["bias"]).then_inc(moe_in, 16)
            sp.dma_start(rank[:], a["rank"]).then_inc(moe_in, 16)
            sp.dma_start(w1T[:, 0:E0], a["w1T"]).then_inc(moe_in, 16)
            sp.dma_start(w1T[:, E0:], a["sw1T"]).then_inc(moe_in, 16)
            sp.dma_start(w3T[:, 0:E0], a["w3T"]).then_inc(moe_in, 16)
            sp.dma_start(w3T[:, E0:], a["sw3T"]).then_inc(moe_in, 16)
            sp.dma_start(w2T[:, 0:E0], a["w2T"]).then_inc(moe_in, 16)
            sp.dma_start(w2T[:, E0:], a["sw2T"]).then_inc(moe_in, 16)
            sp.dma_start(select[:], a["select"]).then_inc(ssm_in, 16)
            sp.dma_start(W_delta[:], a["W_delta"]).then_inc(ssm_in, 16)
            for c in range(3):
                sp.dma_start(W_BC3[:, 32 * c:32 * c + NS], a["W_B"]).then_inc(ssm_in, 16)
                sp.dma_start(W_BC3[:, 32 * c + NS:32 * c + 32], a["W_C"]).then_inc(ssm_in, 16)
            sp.dma_start(W_ctx[:], a["W_ctx"]).then_inc(ssm_in, 16)
            sp.dma_start(expA[:], a["A_log"]).then_inc(ssm_in, 16)
            sp.dma_start(gamma[:], a["gamma"]).then_inc(ssm_in, 16)
            sp.dma_start(beta[:], a["beta"]).then_inc(ssm_in, 16)
            sp.dma_start(ctx_scale[:], a["ctx_scale"]).then_inc(ssm_in, 16)
            sp.dma_start(Wr[:], a["Wr"]).then_inc(wr_in, 16)
            sp.wait_ge(idx_ready, 1)
            e = [sp.value_load(idx8[0:1, k:k + 1], min_val=0, max_val=E1 - 1) for k in range(2)]
            for k in range(2):
                sp.dma_start(w1s[:, k, :], a["W1"][bass.ds(e[k], 1)].rearrange("a p f -> p (a f)")).then_inc(w1_in[k], 16)
            for k in range(2):
                sp.dma_start(b1s[:, k, :], a["b1"][bass.ds(e[k], 1)].rearrange("a p f -> p (a f)")).then_inc(b1_in, 16)
                sp.dma_start(b2s[0:1, k * D:(k + 1) * D], a["b2"][bass.ds(e[k], 1), :]).then_inc(b2_in, 16)
            for k in range(2):
                sp.dma_start(w2s[:, k, :], a["W2"][bass.ds(e[k], 1)].rearrange("a p f -> p (a f)")).then_inc(w2_in[k], 16)
            for g in range(NG):
                sp.wait_ge(x_final, g + 1)
                sp.dma_start(out_dram[:, GT * g:GT * g + GT, :], x[:, GT * g:GT * g + GT, :]).then_inc(out_done, 16)
            sp.wait_ge(out_done, 16 * NG)

        @block.gpsimd
        def _(pool):
            pool.memset(neg_half[:], -0.5).then_inc(const_set, 1)
            pool.memset(q_pad[0][:], 0.0).then_inc(pad_zeroed, 1)

            def input_rstd(g):
                t = slice(GT * g, GT * g + GT)
                pool.wait_ge(n_var_ready, g + 1)
                pool.tensor_tensor(n_rstd[:, t], n_var[:, t], neg_half[:, 0:GT], ALU.pow).then_inc(n_rstd_ready, 1)

            pool.wait_ge(const_set, 1)
            input_rstd(0)
            pool.memset(q_pad[1][:], 0.0).then_inc(pad_zeroed, 1)
            pool.memset(S_sb[:], 0.0).then_inc(pad_zeroed, 1)
            pool.memset(C_sb[:], 0.0).then_inc(pad_zeroed, 1)
            pool.memset(euler[:], EULER).then_inc(const_set, 1)
            pool.memset(ones[:], 1.0).then_inc(const_set, 1)
            pool.memset(state[:], 0.0).then_inc(state_zeroed, 1)
            pool.wait_ge(const_set, 3)
            for g in range(1, NG):
                input_rstd(g)

            def result_rstd(n, cols):
                pool.wait_ge(r_var_ready, n + 1)
                pool.tensor_tensor(r_rstd[:, 0:cols], r_var[:, 0:cols], neg_half[:, 0:cols],
                                   ALU.pow).then_inc(r_rstd_ready, 1)

            def next_rstd(n, cols):
                pool.wait_ge(m_var_ready, n + 1)
                pool.tensor_tensor(m_rstd[:, 0:cols], m_var[:, 0:cols], neg_half[:, 0:cols],
                                   ALU.pow).then_inc(m_rstd_ready, 1)

            with pool.Fori(0, NT - 1) as t:
                result_rstd(t, 1)
                next_rstd(t, 1)
            result_rstd(NT - 1, 1)

            def lower_part(e):
                pool.wait_ge(w_hi_ready, e + 1)
                for full, hi, lo in ((w1T, w1_hi, w1_lo), (w3T, w3_hi, w3_lo)):
                    ins = pool.tensor_tensor(lo[:, e, :], full[:, e, :], hi[:, e, :].bitcast(F32), ALU.subtract)
                ins.then_inc(w_split_ready, 1)

            for e in range(E0 + NSH):
                lower_part(e)
                if e == 0:
                    next_rstd(NT - 1, 1)
                if e == 2:
                    pool.wait_ge(gate_dif, 1)
                    pool.tensor_tensor(gate[:, 1, :], euler[:], gate[:, 0, :], ALU.pow).then_inc(gate_exp, 1)
            with pool.Fori(0, NG) as g:
                result_rstd(g + NT, GT)
                next_rstd(g + NT, GT)
            def delta_x(g):
                pool.wait_ge(delta_ready, g + 1)
                pool.tensor_tensor(dx[:, g * G:(g + 1) * G], delta[:, g * G:(g + 1) * G], xT[:, g * G:(g + 1) * G],
                                   ALU.mult).then_inc(dx_ready, 1)

            for g in range(NG - 1):
                delta_x(g)

            def state_group(g):
                for n in range(NS):
                    step = g * NS + n
                    pool.wait_ge(scan_done, step + 1)
                    pool.wait_ge(C_copied_out, step + 1)
                    if not (isinstance(step, int) and step < RS):
                        pool.wait_ge(yacc_done, step - (RS - 1))
                    pool.tensor_tensor(hc[:, n % RS, :], hs[:, n % RS, :], c_sb[:, n % RS, :],
                                       ALU.mult).then_inc(hc_done, 1)
                    if isinstance(g, int) and n == 2 * RS:
                        delta_x(NG - 1)

            state_group(0)
            with pool.Fori(1, NG) as g:
                state_group(g)
            for i in range(NG + 2):
                if i < NG:
                    pool.wait_ge(y_var_ready, i + 1)
                    pool.tensor_tensor(y_rstd[:, i, :], y_var[:], neg_half[:, 0:GT], ALU.pow).then_inc(y_rstd_ready, 1)
                if i >= 2:
                    pool.wait_ge(m_var_ready, NT + NG + i - 1)
                    pool.tensor_tensor(t_rstd[:, i - 2, :], m_var[:], neg_half[:, 0:GT], ALU.pow).then_inc(m_rstd_ready, 1)
                if 1 <= i <= NG:
                    result_rstd(NT + NG + i - 1, GT)
            pool.wait_ge(dif_ready, 1)
            pool.tensor_tensor(dif[:, 1:2], euler[0:1, 0:1], dif[:, 0:1], ALU.pow).then_inc(dexp_ready, 1)

            def hidden_group(g):
                for v in range(NV):
                    if v == 5 and not isinstance(g, int):
                        result_rstd(g + (NT + 2 * NG - 1), GT)
                    if v % RS != RS - 1:
                        pool.wait_ge(hg_hi_ready, g * NV + (v + 1))
                        pool.tensor_tensor(hg_lo[v % RS], hg[v % RS], hg_hi[v % RS].bitcast(F32),
                                           ALU.subtract).then_inc(hg_lo_pool, 1)

            hidden_group(0)
            with pool.Fori(1, NG) as g:
                hidden_group(g)
            result_rstd(NT + 3 * NG - 1, GT)

        @block.tensor
        def _(pe):
            def input_transposes(layer, groups, after=None):
                for g in groups:
                    n = NG * layer + g
                    if layer == 0:
                        pe.wait_ge(xn_ready, g + 1)
                    else:
                        pe.wait_ge(xn_row_ready, GT * (g + 1))
                    if n >= 2:
                        pe.wait_ge(xT_ready, n - 1)
                    for k in range(GT):
                        last = pe.transpose(bank[6 + g % 2][:, k * P:(k + 1) * P], xn[:, GT * g + k, :], ident[:])
                    last.then_inc(xT_filled, 1)
                    if after and g > groups[0]:
                        after(g - 1)
                if after:
                    after(groups[-1])

            pe.wait_ge(ident_in, 16)
            input_transposes(0, [0])

            def attention_slot(s, odd, first=False, last=False, inter=True):
                now, old = odd, 1 - odd

                def bank_free(job):
                    n = use_of(s, job)
                    if not (isinstance(n, int) and n == 1):
                        pe.wait_ge(drained[bank_of(job)], n - 1)

                def copied(slot, job):
                    pe.wait_ge(drained[bank_of(job)], use_of(slot, job))

                def done(job, ins):
                    ins.then_inc(filled[bank_of(job)], 1)

                def w_job(w):
                    job = f"w{w}"
                    bank_free(job)
                    if w == 0:
                        copied(s - 1, "a1")
                        copied(s - 1, "k0")
                        copied(s - 1, "k1")
                    else:
                        copied(s - 1, "a2")
                        copied(s - 1, "a3")
                    if inter:
                        pe.wait_ge(S_copied, s - 1)
                    b = bank[bank_of(job)]
                    for i in range(4):
                        p = 4 * w + i
                        for r in range(2):
                            h = 2 * p + r
                            ins = pe.matmul(b[DK * r:DK * r + DK, i * P:(i + 1) * P], k_tok[:, h * DK:(h + 1) * DK],
                                            a_T[:, h * P:(h + 1) * P], start=(i == 0), stop=not inter,
                                            skip_group_check=True)
                    if inter:
                        for i in range(4):
                            p = 4 * w + i
                            ins = pe.matmul(b[:, i * P:(i + 1) * P], S_sb[:, p, :], q_T[old][:, p * P:(p + 1) * P],
                                            start=False, stop=True, skip_group_check=True)
                    done(job, ins)

                def state_update(target, keys, values, sem_done):
                    for p in range(NP):
                        for r in range(2):
                            h = 2 * p + r
                            ins = pe.matmul(target[DK * r:DK * r + DK, p * DK:(p + 1) * DK],
                                            keys[:, h * DK:(h + 1) * DK], values[:, h * DK:(h + 1) * DK],
                                            start=(not inter and p == 0), stop=True, skip_group_check=True)
                    ins.then_inc(sem_done, 1)

                def projection(job, w_sb):
                    bank_free(job)
                    for i in range(4):
                        p = 4 * int(job[-1]) + i
                        ins = pe.matmul(bank[bank_of(job)][:, i * P:(i + 1) * P], w_sb[:, p * P:(p + 1) * P],
                                        xt[now], start=True, stop=True)
                    done(job, ins)

                def wide_projection(job, w_hi, w_lo):
                    bank_free(job)
                    b = bank[bank_of(job)]
                    cols = slice(G * int(job[-1]), G * int(job[-1]) + G)
                    pe.matmul(b[:], xt_hi[:], w_hi[:, cols], start=True, stop=False)
                    pe.matmul(b[:], xt_hi[:], w_lo[:, cols], start=False, stop=False)
                    done(job, pe.matmul(b[:], xt_lo[:], w_hi[:, cols], start=False, stop=True))

                def scores(job, keys, queries):
                    for i in range(2):
                        p = 2 * int(job[-1]) + i
                        ins = pe.matmul(bank[bank_of(job)][:, i * 2 * P:(i + 1) * 2 * P], keys[:, p * P:(p + 1) * P],
                                        queries[:, p, :, :].rearrange("p r t -> p (r t)"), start=True, stop=True)
                    done(job, ins)

                def turn(job, src):
                    for i in range(4):
                        p = 4 * int(job[-1]) + i
                        ins = pe.transpose(bank[bank_of(job)][:, i * P:(i + 1) * P], src[:, p * P:(p + 1) * P], ident[:])
                    done(job, ins)

                if not first:
                    w_job(0)
                    w_job(1)
                    if not last:
                        if not inter:
                            pe.wait_ge(xT_ready, NG)
                        state_update(bank[6], k_tok, k_tok, S_updated)
                if not last:
                    pe.wait_ge(xt_ready, s + 1)
                    if first:
                        pe.wait_ge(wq_in, 16)
                    projection("q0", Wq)
                    projection("q1", Wq)
                if not first:
                    for n in range(4):
                        bank_free(f"b{n}")
                        if n < 3:
                            copied(s, f"w{n // 2}")
                        scores(f"b{n}", w_T, q_pad[old])
                if not last:
                    pe.wait_ge(xt_split_ready, s + 1)
                    if first:
                        pe.wait_ge(Wk_split_ready, 1)
                    wide_projection("k0", Wk_hi, Wk_lo)
                    wide_projection("k1", Wk_hi, Wk_lo)
                if not first:
                    bank_free("wt0")
                    turn("wt0", w_T)
                    bank_free("wt1")
                    turn("wt1", w_T)
                if not last:
                    if first:
                        pe.wait_ge(Wv_split_ready, 1)
                    wide_projection("v0", Wv_hi, Wv_lo)
                    wide_projection("v1", Wv_hi, Wv_lo)
                    bank_free("kt0")
                    turn("kt0", k_tok)
                    bank_free("kt1")
                    turn("kt1", k_tok)
                if not first:
                    for n in range(2):
                        job = f"o{n}"
                        bank_free(job)
                        copied(s, f"b{2 * n}")
                        copied(s, f"b{2 * n + 1}")
                        if n == 0:
                            copied(s - 1, "v0")
                            copied(s - 1, "v1")
                        if inter:
                            pe.wait_ge(C_copied, s - 1)
                        b = bank[bank_of(job)]
                        for i in range(4):
                            p = 4 * n + i
                            for r in range(2):
                                h = 2 * p + r
                                ins = pe.matmul(b[DK * r:DK * r + DK, i * P:(i + 1) * P],
                                                v_tok[old][:, h * DK:(h + 1) * DK], b_T[:, h * P:(h + 1) * P],
                                                start=(i == 0), stop=not inter, skip_group_check=True)
                        if inter:
                            for i in range(4):
                                p = 4 * n + i
                                ins = pe.matmul(b[:, i * P:(i + 1) * P], C_sb[:, p, :],
                                                q_T[old][:, p * P:(p + 1) * P], start=False, stop=True,
                                                skip_group_check=True)
                        done(job, ins)
                    if not last:
                        copied(s, "wt0")
                        copied(s, "wt1")
                        state_update(bank[7], w_tok, v_tok[old], C_updated)
                if not last:
                    for n in range(4):
                        bank_free(f"a{n}")
                        if n % 2 == 0:
                            copied(s, f"kt{n // 2}")
                        scores(f"a{n}", k_T, q_pad[now])
                if not first:
                    bank_free("y")
                    copied(s, "o0")
                    copied(s, "o1")
                    if not inter:
                        pe.wait_ge(wo_in, 16)
                    for p in range(NP):
                        ins = pe.matmul(bank[bank_of("y")][:, 0:D], o_T[:, p * P:(p + 1) * P], Wo[:, p, :],
                                        start=(p == 0), stop=(p == NP - 1))
                    done("y", ins)

            attention_slot(0, 0, first=True)
            input_transposes(0, range(1, NG))
            attention_slot(1, 1, inter=False)
            with pe.Fori(0, (NT - 2) // 2) as i:
                for u in range(2):
                    attention_slot(i * 2 + (2 + u), u)
            attention_slot(NT, 0, last=True)

            def logits(g):
                pe.wait_ge(xT_ready, NG + g + 1)
                for t in range(GT * g, GT * g + GT):
                    ins = pe.matmul(bank[5][:, t * E0:(t + 1) * E0], xT[:, t * P:(t + 1) * P], routerT[:],
                                    start=True, stop=True)
                ins.then_inc(logit_filled, 1)

            pe.wait_ge(moe_in, 16 * 9)
            pe.wait_ge(ssm_in, 16 * 13)
            input_transposes(1, range(NG - 1), logits)

            def expert_out(g, e):
                j = min(e, E0)
                b = bank[4 + j % 2]
                pe.wait_ge(hid_ready, g * 20 + (2 * e + 2))
                if isinstance(g, int) and g == 0 and e == 1:
                    pe.wait_ge(route_step, 1)
                if e <= E0 and not (isinstance(g, int) and g == 0 and j < 2):
                    pe.wait_ge(acc_done, g * (E0 + 1) + (j if j == 0 else j - 1))
                for k in range(GT):
                    for m in range(2):
                        ins = pe.matmul(b[:, k * P:(k + 1) * P], hid[:, e % 2, m, k * P:(k + 1) * P],
                                        w2T[:, e, m, :], start=(k == 0 and m == 0 and e <= E0), stop=(m == 1),
                                        skip_group_check=True)
                ins.then_inc(ye_filled, 1)

            def next_transposes(n):
                pe.wait_ge(xn_ready, n + (1 - NG))
                for k in range(GT):
                    ins = pe.transpose(bank[6][:, k * P:(k + 1) * P], xn[:, k, :], ident[:])
                ins.then_inc(xT_filled, 1)

            def state_projections(g):
                pe.wait_ge(xT_ready, g + (2 * NG + 1))
                cols = xT[:, g * G:(g + 1) * G] if isinstance(g, int) else xT[:, bass.ds(g * G, G)]
                pe.matmul(bank[6][:], W_delta[:], cols, start=True, stop=True).then_inc(z_filled, 1)
                pe.matmul(bank[7][0:96, :], W_BC3[:], cols, start=True, stop=True).then_inc(bc_filled, 1)

            def expert_group(g):
                first = isinstance(g, int)
                for e in range(E0 + NSH):
                    for m in range(2):
                        if not (first and e == 0):
                            pe.wait_ge(hid_ready, g * 20 + (2 * e + m - 1))
                        elif m == 0:
                            pe.wait_ge(x_split_ready, 1)
                        if first and m == 0:
                            pe.wait_ge(w_split_ready, e + 1)
                        if m == 0 and not first:
                            pe.wait_ge(x_split_ready, NG)
                        part_m = slice(m * P, (m + 1) * P)
                        x_hi, x_lo = xT_hi[:, bass.ds(g * G, G)], xT_lo[:, bass.ds(g * G, G)]
                        for b, w_hi, w_lo in ((2 * m, w1_hi, w1_lo), (2 * m + 1, w3_hi, w3_lo)):
                            pe.matmul(bank[b][:], w_hi[:, e, part_m], x_hi, start=True, stop=False)
                            pe.matmul(bank[b][:], w_hi[:, e, part_m], x_lo, start=False, stop=False)
                            ins = pe.matmul(bank[b][:], w_lo[:, e, part_m], x_hi, start=False, stop=True)
                        ins.then_inc(ab_filled, 1)
                    if first and e == 0:
                        input_transposes(1, [NG - 1], logits)
                    if e:
                        expert_out(g, e - 1)
                    elif not first:
                        expert_out(g - 1, E0 + NSH - 1)
                    if e == 6 and not first:
                        next_transposes(g + (2 * NG - 1))
                    if e == 8 and not first:
                        state_projections(g - 1)

            expert_group(0)
            with pe.Fori(1, NG) as g:
                expert_group(g)
            expert_out(NG - 1, E0 + NSH - 1)
            pe.wait_ge(z_copied, NG - 1)
            next_transposes(3 * NG - 1)

            def y_sum(g, n):
                pe.wait_ge(hc_done, g * NS + (n + 1))
                if n == 0 and not isinstance(g, int):
                    pe.wait_ge(yT_ready, g)
                pe.matmul(bank[5][:], ident[:], hc[:, n % RS, :], start=(n == 0), stop=(n == NS - 1),
                          skip_group_check=True).then_inc(yacc_done, 1)

            def state_group(g):
                first = isinstance(g, int)
                for n in range(NS):
                    step = g * NS + n
                    two = first and n < 2 * RS
                    if first and n == 0:
                        pe.wait_ge(bc_ready, NG - 1)
                        pe.wait_ge(acc_done, NG * (E0 + 1))
                    elif first and 2 <= n < 2 * RS + 2:
                        pe.wait_ge(drive_done, n - 1)
                    elif first and n == 2 * RS + 2:
                        pe.wait_ge(delta_ready, NG)
                        pe.wait_ge(bc_ready, NG)
                    elif not (first and n < 3 * RS):
                        pe.wait_ge(drive_done, step - (RS - 1))
                    pe.matmul(bank[B_bank[n % 2 if two else n % RS]][:], select[:, n, :], bc[:, bass.ds(g * G, G)], start=True,
                              stop=True).then_inc(B_filled, 1)
                    if not (first and n == 0):
                        pe.wait_ge(C_copied_out, step)
                    pe.matmul(bank[2][:], select[:, NS + n, :], bc[:, bass.ds(g * G, G)], start=True,
                              stop=True).then_inc(C_filled, 1)
                    if n >= LAG:
                        y_sum(g, n - LAG)
                    elif not first:
                        y_sum(g - 1, NS - LAG + n)
                    if first and n == 1:
                        state_projections(NG - 1)

            state_group(0)
            with pe.Fori(1, NG) as g:
                state_group(g)
            for n in range(NS - LAG, NS):
                y_sum(NG - 1, n)

            def tail_in(g):
                pe.wait_ge(yT_ready, g + 1)
                if g >= 2:
                    pe.wait_ge(yn_ready, g - 1)
                for k in range(GT):
                    ins = pe.transpose(bank[g % 2][:, k * P:(k + 1) * P], y_T[:, g * G + k * P:g * G + (k + 1) * P],
                                       ident[:])
                ins.then_inc(ytok_filled, 1)

            tail_in(0)
            tail_in(1)
            for i in range(NG + 2):
                if i < NG:
                    pe.wait_ge(yn_ready, i + 1)
                    if i >= 2:
                        pe.wait_ge(zT_ready, i - 1)
                    for k in range(GT):
                        ins = pe.transpose(bank[2 + i % 2][:, k * P:(k + 1) * P], y_n[:, i % 2, k * P:(k + 1) * P],
                                           ident[:])
                    ins.then_inc(zT_filled, 1)
                if i + 2 < NG:
                    tail_in(i + 2)
                if i >= 2:
                    o = i - 2
                    pe.wait_ge(xn_ready, 2 * NG + o + 1)
                    if o >= 2:
                        pe.wait_ge(xT_ready, 3 * NG + o - 1)
                    for k in range(GT):
                        ins = pe.transpose(bank[4 + o % 2][:, k * P:(k + 1) * P], xn[:, GT * o + k, :], ident[:])
                    ins.then_inc(xT_filled, 1)
                if i < NG:
                    pe.wait_ge(zT_ready, i + 1)
                    if i >= 2:
                        pe.wait_ge(ctx_drained, i - 1)
                    for k in range(GT):
                        ins = pe.matmul(bank[6 + i % 2][:, k * P:(k + 1) * P], z_T[:, i % 2, k * P:(k + 1) * P],
                                        W_ctx[:], start=True, stop=True)
                    ins.then_inc(ctx_filled, 1)

            pe.wait_ge(wr_in, 16)
            pe.wait_ge(pooled_ready, 1)
            pe.matmul(bank[0][0:1, 0:E1], pooled[:, 1:2], Wr[:], start=True, stop=True).then_inc(lg_filled, 1)
            pe.wait_ge(wrow_ready, 1)
            pe.matmul(bank[5][:, 0:2], ones[0:1, :], wrow[:], start=True, stop=True).then_inc(wb_filled, 1)
            pe.wait_ge(xf_split_ready, NG)

            def weighted_bias():
                pe.wait_ge(b2_in, 32)
                for k in range(2):
                    ins = pe.matmul(bank[7][:, 0:1], b2s[:, k * D:(k + 1) * D], wrow[:, k:k + 1], start=(k == 0),
                                    stop=(k == 1))
                ins.then_inc(b2_filled, 1)

            def out_part(g, v):
                pe.wait_ge(w2w_split_ready, v // NF + 1)
                wait_hidden_split(pe, g, v)
                if v == 0 and not (isinstance(g, int) and g == 0):
                    pe.wait_ge(out_T_ready, g)
                w = v // NF, slice((v % NF) * D, (v % NF + 1) * D)
                pe.matmul(bank[4][:], w2w_hi[:, w[0], w[1]], hg_hi[v % RS], start=(v == 0), stop=False,
                          skip_group_check=True)
                pe.matmul(bank[4][:], w2w_hi[:, w[0], w[1]], hg_lo[v % RS], start=False, stop=False,
                          skip_group_check=True)
                pe.matmul(bank[4][:], w2w_lo[:, w[0], w[1]], hg_hi[v % RS], start=False, stop=(v == NV - 1),
                          skip_group_check=True).then_inc(yv_done, 1)

            def out_turn(g):
                pe.wait_ge(out_T_ready, g + 1)
                if not (isinstance(g, int) and g == 0):
                    pe.wait_ge(out_drained, g)
                for k in range(GT):
                    ins = pe.transpose(bank[6][:, k * P:(k + 1) * P], out_T[:, k * P:(k + 1) * P], ident[:])
                ins.then_inc(out_filled, 1)

            def hidden_group(g, before):
                first = before is None
                for v in range(NV):
                    if not (first and v < RS):
                        pe.wait_ge(gelu_done, g * NV + (v - RS + 1))
                    pe.wait_ge(w1s_split_ready, v // NF + 1)
                    w = v // NF, slice((v % NF) * P, (v % NF + 1) * P)
                    x_hi, x_lo = xT_hi[:, bass.ds(g * G, G)], xT_lo[:, bass.ds(g * G, G)]
                    pe.matmul(bank[v % RS][:], w1s_hi[:, w[0], w[1]], x_hi, start=True, stop=False)
                    pe.matmul(bank[v % RS][:], w1s_hi[:, w[0], w[1]], x_lo, start=False, stop=False)
                    pe.matmul(bank[v % RS][:], w1s_lo[:, w[0], w[1]], x_hi, start=False,
                              stop=True).then_inc(hf_filled, 1)
                    if first and v == 0:
                        weighted_bias()
                    if v >= LAG:
                        out_part(g, v - LAG)
                    elif not first:
                        out_part(before, v - LAG + NV)
                    if v == LAG and not first:
                        out_turn(before)

            hidden_group(0, None)
            hidden_group(1, 0)
            with pe.Fori(2, NG) as g:
                hidden_group(g, g - 1)
            for v in range(NV - LAG, NV):
                out_part(NG - 1, v)
            out_turn(NG - 1)

        @block.scalar
        def _(act):
            def input_copies(layer, groups):
                for g in groups:
                    act.wait_ge(xT_filled, NG * layer + g + 1)
                    act.activation(xT[:, g * G:(g + 1) * G], bank[6 + g % 2][:], ACT.Copy).then_inc(xT_ready, 1)

            input_copies(0, [0])

            def tile_input(s, odd):
                act.wait_ge(xT_ready, 1 if isinstance(s, int) and s < GT else NG)
                act.activation(xt[odd], xT[:, s * P:(s + 1) * P] if isinstance(s, int) else xT[:, bass.ds(s * P, P)],
                               ACT.Copy).then_inc(xt_ready, 1)

            def attention_slot(s, odd, first=False, last=False):
                now = odd

                def copy(job, dst):
                    act.wait_ge(filled[bank_of(job)], use_of(s, job))
                    act.activation(dst, bank[bank_of(job)][:], ACT.Copy).then_inc(drained[bank_of(job)], 1)

                def copy_padded(job):
                    act.wait_ge(filled[bank_of(job)], use_of(s, job))
                    p = slice(4 * int(job[-1]), 4 * int(job[-1]) + 4)
                    act.activation(q_T[now][:, p.start * P:p.stop * P], bank[bank_of(job)][:], ACT.Copy)
                    for r in range(2):
                        half = slice(DK * r, DK * r + DK)
                        ins = act.activation(q_pad[now][half, p, r, :],
                                             bank[bank_of(job)][half, :].rearrange("p (n t) -> p n t", n=4), ACT.Copy)
                    ins.then_inc(drained[bank_of(job)], 1)

                if not first:
                    copy("w0", w_T[:, 0:G])
                    copy("w1", w_T[:, G:2 * G])
                if not last:
                    copy_padded("q0")
                    copy_padded("q1")
                    copy("k0", k_tok[:, 0:G])
                    copy("k1", k_tok[:, G:2 * G])
                if not first:
                    copy("wt0", w_tok[:, 0:G])
                    copy("wt1", w_tok[:, G:2 * G])
                if not last:
                    copy("v0", v_tok[now][:, 0:G])
                    copy("v1", v_tok[now][:, G:2 * G])
                    if not (isinstance(s, int) and s == NT - 1):
                        tile_input(s + 1, 1 - odd)
                    copy("kt0", k_T[:, 0:G])
                    copy("kt1", k_T[:, G:2 * G])
                if not first:
                    copy("o0", o_T[:, 0:G])
                    copy("o1", o_T[:, G:2 * G])

            act.wait_ge(pad_zeroed, 1)
            tile_input(0, 0)
            attention_slot(0, 0, first=True)
            input_copies(0, range(1, NG))
            act.wait_ge(pad_zeroed, 2)
            attention_slot(1, 1)
            with act.Fori(0, (NT - 2) // 2 - 1) as i:
                for u in range(2):
                    attention_slot(i * 2 + (2 + u), u)
            attention_slot(NT - 2, 0)
            attention_slot(NT - 1, 1)
            attention_slot(NT, 0, last=True)

            act.preload_act_table(ACT.Silu)
            input_copies(1, range(NG - 1))

            def next_copy(g):
                act.wait_ge(xT_filled, g + (2 * NG + 1))
                act.activation(wait_slot[:], neg_half[:, 0:1], ACT.Copy)
                dst = xT[:, g * G:(g + 1) * G] if isinstance(g, int) else xT[:, bass.ds(g * G, G)]
                act.activation(dst, bank[6][:], ACT.Copy).then_inc(xT_ready, 1)

            def expert_group(g):
                for e in range(E0 + NSH):
                    for m in range(2):
                        act.wait_ge(ab_filled, g * 20 + (2 * e + m + 1))
                        if not (isinstance(g, int) and e == 0):
                            act.wait_ge(hid_ready, g * 20 + (2 * e + m - 1))
                        act.activation(sil[:, m, :], bank[2 * m][:], ACT.Silu).then_inc(sil_ready, 1)
                    if e == 0 and isinstance(g, int):
                        input_copies(1, [NG - 1])
                    if e == 7 and not isinstance(g, int):
                        next_copy(g - 1)
                    if e == 9 and not isinstance(g, int):
                        act.wait_ge(z_filled, g)
                        act.activation(wait_slot[:], neg_half[:, 0:1], ACT.Copy)
                        act.activation(z_all[:, bass.ds((g - 1) * G, G)], bank[6][:], ACT.Copy).then_inc(z_copied, 1)

            expert_group(0)
            with act.Fori(1, NG) as g:
                expert_group(g)
            def softplus_terms(groups, source):
                for g in groups:
                    act.activation(soft[g], source(g), ACT.Abs).then_inc(z_step, 1)
                base = 2 * groups[0]
                for n, g in enumerate(groups):
                    act.wait_ge(z_step, base + n + 1)
                    act.activation(soft[g], soft[g], ACT.Exp, scale=-1.0).then_inc(z_step, 1)
                for n, g in enumerate(groups):
                    act.wait_ge(z_step, base + len(groups) + n + 1)
                    act.activation(soft[g], soft[g], ACT.Ln, bias=1.0).then_inc(zlog_ready, 1)

            act.wait_ge(ssm_in, 16 * 13)
            act.preload_act_table_set("natural_log_exp_and_others")
            act.activation(expA[:], expA[:], ACT.Exp).then_inc(expA_ready, 1)
            act.wait_ge(z_copied, NG - 1)
            softplus_terms(range(NG - 1), lambda g: z_all[:, g * G:(g + 1) * G])
            next_copy(NG - 1)
            act.wait_ge(negA_ready, 1)

            def y_copy(g):
                act.wait_ge(yacc_done, g * NS + NS)
                act.activation(wait_slot[:], neg_half[:, 0:1], ACT.Copy)
                dst = y_T[:, g * G:(g + 1) * G] if isinstance(g, int) else y_T[:, bass.ds(g * G, G)]
                act.activation(dst, bank[5][:], ACT.Copy).then_inc(yT_ready, 1)

            act.wait_ge(delta_ready, NG - 1)
            act.wait_ge(state_zeroed, 1)

            def state_group(g):
                first = isinstance(g, int)
                for n in range(NS):
                    step = g * NS + n
                    if n == 0:
                        if not first:
                            act.wait_ge(decay_ready, g * NS)
                            act.activation(wait_slot[:], neg_half[:, 0:1], ACT.Copy)
                        act.activation(delta_g, delta[:, bass.ds(g * G, G)], ACT.Copy).then_inc(delta_copied, 1)
                        act.wait_ge(delta_copied, g + 1)
                    act.wait_ge(C_filled, step + 1)
                    if not (first and n < RS):
                        act.wait_ge(hc_done, step - (RS - 1))
                    act.activation(c_sb[:, n % RS, :], bank[2][:], ACT.Copy).then_inc(C_copied_out, 1)
                    if not (first and n < 2):
                        act.wait_ge(scan_done, step - 1)
                    act.activation(bank[3 + n % 2][:], delta_g, ACT.Exp,
                                   scale=negA[:, n:n + 1]).then_inc(decay_ready, 1)
                    if not (first and n < 2):
                        o = (n - 2) % NS
                        act.activation(state[:, o:o + 1], hs[:, o % RS, G - 1:G], ACT.Copy).then_inc(state_saved, 1)
                    if n == LAG and not first:
                        y_copy(g - 1)
                    if n == LAG and first:
                        act.wait_ge(z_filled, NG)
                        softplus_terms([NG - 1], lambda g: bank[6][:])

            state_group(0)
            act.wait_ge(delta_ready, NG)
            with act.Fori(1, NG) as g:
                state_group(g)
            y_copy(NG - 1)

            def normed(dst, src, scale, bias):
                for k in range(GT):
                    ins = act.activation(dst(k), src(k), ACT.Identity, scale=scale[:, k:k + 1], bias=bias[:, k:k + 1])
                return ins

            for i in range(NG + 3):
                if 1 <= i <= NG:
                    o = i - 1
                    act.wait_ge(ctx_filled, i)
                    if i >= 3:
                        act.wait_ge(r_scaled, i - 2)
                    act.activation(ctx_v[:, o % 2, :], bank[6 + o % 2][:], ACT.Copy,
                                   scale=ctx_scale[:, 0:1]).then_inc(ctx_drained, 1)
                if i < NG:
                    act.wait_ge(y_bias_ready, i + 1)
                    if i >= 2:
                        act.wait_ge(zT_filled, i - 1)
                    normed(lambda k: y_n[:, i % 2, k * P:(k + 1) * P], lambda k: bank[i % 2][:, k * P:(k + 1) * P],
                           y_rstd[:, i], y_bias[:, i]).then_inc(yn_ready, 1)
                if 2 <= i < NG + 2:
                    act.wait_ge(t_bias_ready, i - 1)
                    normed(lambda k: xn[:, GT * (i - 2) + k, :], lambda k: x[:, GT * (i - 2) + k, :],
                           t_rstd[:, i - 2], t_bias[:, i - 2]).then_inc(xn_ready, 1)
                if i < NG:
                    act.wait_ge(zT_filled, i + 1)
                    if i >= 2:
                        act.wait_ge(ctx_filled, i - 1)
                    act.activation(z_T[:, i % 2, :], bank[2 + i % 2][:], ACT.Identity, scale=gamma[:, 0:1],
                                   bias=beta[:, 0:1]).then_inc(zT_ready, 1)
                if i >= 3:
                    o = i - 3
                    if i == NG + 2:
                        act.preload_act_table(ACT.Gelu)
                    act.wait_ge(xT_filled, 3 * NG + o + 1)
                    act.activation(xT[:, o * G:(o + 1) * G], bank[4 + o % 2][:], ACT.Copy,
                                   accum_out=pool_part[:, o:o + 1]).then_inc(xT_ready, 1)

            act.wait_ge(b1_in, 32)

            def result_copy(g):
                act.wait_ge(yv_done, g * NV + NV)
                if not (isinstance(g, int) and g == 0):
                    act.wait_ge(out_filled, g)
                act.activation(out_T, bank[4][:], ACT.Identity, bias=b2c[:, 0:1]).then_inc(out_T_ready, 1)

            def hidden_group(g, before):
                for v in range(NV):
                    if v == LAG and before is not None:
                        result_copy(before)
                    act.wait_ge(hf_filled, g * NV + (v + 1))
                    if not (before is None and v < RS):
                        wait_hidden_split(act, g, v - RS)
                    act.activation(hg[v % RS], bank[v % RS][:], ACT.Gelu,
                                   bias=b1s[:, v // NF, v % NF:v % NF + 1]).then_inc(gelu_done, 1)

            hidden_group(0, None)
            act.wait_ge(wb_ready, 1)
            hidden_group(1, 0)
            with act.Fori(2, NG) as g:
                hidden_group(g, g - 1)
            result_copy(NG - 1)

        @block.vector
        def _(dve):
            n_steps = Steps(dve, n_step)

            def normalise(g):
                dve.wait_ge(n_rstd_ready, g + 1)
                for k in range(GT):
                    t = GT * g + k
                    ins = dve.tensor_scalar(xn[:, t, :], x[:, t, :], n_mv[:, t, 0:1], n_rstd[:, t:t + 1],
                                            ALU.subtract, ALU.mult)
                ins.then_inc(xn_ready, 1)

            def weight_split(w, hi, lo, done):
                kv_steps.mark(dve.tensor_copy(hi[:], w[:]))
                kv_steps.wait()
                dve.tensor_tensor(lo[:], w[:], hi[:].bitcast(F32), ALU.subtract).then_inc(done, 1)

            def tile_split(t):
                cols = xT[:, t * P:(t + 1) * P] if isinstance(t, int) else xT[:, bass.ds(t * P, P)]
                dve.tensor_copy(xt_hi[:], cols).then_inc(xt_step, 1)
                dve.wait_ge(xt_step, t + 1)
                dve.tensor_tensor(xt_lo[:], cols, xt_hi[:].bitcast(F32), ALU.subtract).then_inc(xt_split_ready, 1)

            kv_steps = Steps(dve, kv_step)
            for g in range(NG):
                dve.wait_ge(x_in[g], 16)
                for k in range(GT):
                    ins = dve.bn_stats(n_stats[:, GT * g + k, :], x[:, GT * g + k, :])
                n_steps.mark(ins)
                n_steps.wait()
                for k in range(GT):
                    ins = dve.bn_aggr(n_mv[:, GT * g + k, :], n_stats[:, GT * g + k, :])
                n_steps.mark(ins)
                n_steps.wait()
                dve.tensor_scalar(n_var[:, GT * g:GT * g + GT], n_mv[:, GT * g:GT * g + GT, 1],
                                  EPS, None, ALU.add).then_inc(n_var_ready, 1)
                if g != 1:
                    normalise(max(g - 1, 0))
                if g == 0:
                    dve.wait_ge(wk_in, 16)
                    weight_split(Wk, Wk_hi, Wk_lo, Wk_split_ready)
                    dve.wait_ge(xT_ready, 1)
                    tile_split(0)
                    dve.wait_ge(wv_in, 16)
                    weight_split(Wv, Wv_hi, Wv_lo, Wv_split_ready)
            normalise(NG - 1)

            def row_stats(steps, srcs, stats, mv, var, var_ready):
                k_all = len(srcs)
                for k, src in enumerate(srcs):
                    ins = dve.bn_stats(stats[:, k, :], src)
                steps.mark(ins)
                steps.wait()
                dve.memset(var[:, 0:k_all], 0.0)
                for k in range(k_all):
                    ins = dve.bn_aggr(mv[:, k, :], stats[:, k, :])
                steps.mark(ins)
                steps.wait()
                dve.tensor_scalar(var[:, 0:k_all], mv[:, 0:k_all, 1], EPS, None, ALU.add).then_inc(var_ready, 1)

            def scaled(dsts, srcs, mv, rstd):
                for k, (dst, src) in enumerate(zip(dsts, srcs)):
                    ins = dve.tensor_scalar(dst, src, mv[:, k, 0:1], rstd[:, k:k + 1], ALU.subtract, ALU.mult)
                return ins

            def result_stats(steps, srcs):
                row_stats(steps, srcs, r_stats, r_mv, r_var, r_var_ready)

            def next_stats(steps, cols):
                row_stats(steps, [r_new[:, k, :] for k in range(cols)], m_stats, m_mv, m_var, m_var_ready)

            dve.wait_ge(mask_in, 16)
            dve.wait_ge(pad_zeroed, 4)

            def attention_slot(s, first=False, last=False):
                def masked(job, dst):
                    dve.wait_ge(filled[bank_of(job)], use_of(s, job))
                    dve.tensor_tensor(dst, bank[bank_of(job)][:], mask[:], ALU.mult)\
                       .then_inc(drained[bank_of(job)], 1)

                def state_copy(dst, src):
                    for r in range(2):
                        half = slice(DK * r, DK * r + DK)
                        ins = dve.tensor_copy(dst[half, :, half], src[half, :].rearrange("p (n c) -> p n c", n=NP))
                    return ins

                if not first and not last:
                    dve.wait_ge(S_updated, s)
                    state_copy(S_sb, bank[6]).then_inc(S_copied, 1)
                if not first:
                    for n in range(4):
                        masked(f"b{n}", b_T[:, n * G:(n + 1) * G])
                    if not last:
                        dve.wait_ge(C_updated, s)
                        state_copy(C_sb, bank[7]).then_inc(C_copied, 1)
                if not last and not (isinstance(s, int) and s == NT - 1):
                    if first:
                        dve.wait_ge(filled[bank_of("v1")], use_of(0, "v1"))
                    tile_split(s + 1)
                if not last:
                    for n in range(4):
                        masked(f"a{n}", a_T[:, n * G:(n + 1) * G])
                if not first:
                    y = bank[bank_of("y")][:, 0:D]
                    dve.wait_ge(filled[bank_of("y")], use_of(s, "y"))
                    steps = Steps(dve, y_step, (s - 1) * 5)
                    result_stats(steps, [y])
                    if last:
                        dve.wait_ge(moe_in, 16 * 9)
                        upper_parts(0)
                        split_x(0)
                    dve.wait_ge(r_rstd_ready, s)
                    dve.tensor_scalar(r_val[:, 0, :], y, r_mv[:, 0, 0:1], r_rstd[:, 0:1], ALU.subtract, ALU.mult)\
                       .then_inc(drained[bank_of("y")], 1)
                    dve.wait_ge(drained[bank_of("y")], use_of(s, "y"))
                    row = x[:, s - 1, :] if isinstance(s, int) else x[:, bass.ds(s - 1, 1), :].rearrange("p a d -> p (a d)")
                    steps.mark(dve.tensor_tensor(r_new[:, 0, :], row, r_val[:, 0, :], ALU.add))
                    steps.wait()
                    dve.tensor_scalar(row, r_new[:, 0, :], 1.0, None, ALU.mult)
                    next_stats(steps, 1)
                    dve.wait_ge(m_rstd_ready, s)
                    row_n = xn[:, s - 1, :] if isinstance(s, int) else xn[:, bass.ds(s - 1, 1), :].rearrange("p a d -> p (a d)")
                    scaled([row_n], [r_new[:, 0, :]], m_mv, m_rstd).then_inc(xn_row_ready, 1)
                    assert steps.n == 5, steps.n

            x_steps = Steps(dve, x_split_step)

            def upper_parts(e):
                for hi, full in ((w1_hi, w1T), (w3_hi, w3T)):
                    ins = dve.tensor_copy(hi[:, e, :], full[:, e, :])
                ins.then_inc(w_hi_ready, 1)

            def split_x(g):
                cols = slice(g * G, (g + 1) * G)
                dve.wait_ge(xT_ready, NG + g + 1)
                x_steps.mark(dve.tensor_copy(xT_hi[:, cols], xT[:, cols]))
                x_steps.wait()
                dve.tensor_tensor(xT_lo[:, cols], xT[:, cols], xT_hi[:, cols].bitcast(F32), ALU.subtract)\
                   .then_inc(x_split_ready, 1)

            attention_slot(0, first=True)
            attention_slot(1)
            with dve.Fori(2, NT - 1) as s:
                attention_slot(s)
            attention_slot(NT - 1)
            attention_slot(NT, last=True)
            dve.wait_ge(xn_row_ready, NT)

            route = Steps(dve, route_step)

            def step(ins):
                route.mark(ins)
                route.wait()

            def wide(v):
                return v.unsqueeze(2).to_broadcast([P, NT, E0])

            def route_choice(c):
                if c == 0:
                    dve.wait_ge(logit_filled, NG)
                    step(dve.tensor_tensor(logit[:], bank[5][:, 0:NT * E0].rearrange("p (t e) -> p t e", t=NT),
                                           bias[:], ALU.add))
                step(dve.tensor_reduce(top[:, c, :], logit[:], AX.X, ALU.max))
                step(dve.tensor_tensor(hit[:], logit[:], wide(top[:, c, :]), ALU.is_equal))
                step(dve.tensor_tensor(hit[:], hit[:], rank[:], ALU.mult))
                step(dve.tensor_reduce(place[:, c, :], hit[:], AX.X, ALU.min))
                step(dve.tensor_tensor(pick[:, c], rank[:], wide(place[:, c, :]), ALU.is_equal))
                if c == 0:
                    step(dve.scalar_tensor_tensor(out=logit[:], in0=pick[:, 0], scalar=-3e38, in1=logit[:],
                                                  op0=ALU.mult, op1=ALU.add))
                else:
                    dve.tensor_tensor(gate[:, 0, :], top[:, 1, :], top[:, 0, :], ALU.subtract).then_inc(gate_dif, 1)

            def route_weights():
                dve.wait_ge(gate_exp, 1)
                step(dve.tensor_scalar(gate[:, 2, :], gate[:, 1, :], 1.0, None, ALU.add))
                step(dve.reciprocal(gate[:, 2, :], gate[:, 2, :]))
                step(dve.tensor_tensor(gate[:, 3, :], gate[:, 1, :], gate[:, 2, :], ALU.mult))
                step(dve.tensor_tensor(pick[:, 0], pick[:, 0], wide(gate[:, 2, :]), ALU.mult))
                step(dve.tensor_tensor(pick[:, 1], pick[:, 1], wide(gate[:, 3, :]), ALU.mult))
                step(dve.tensor_tensor(combine[:], pick[:, 0], pick[:, 1], ALU.add))

            def new_rows(steps, g, srcs, n_result):
                rows = x[:, g * GT:(g + 1) * GT, :] if isinstance(g, int) else x[:, bass.ds(g * GT, GT), :]
                dve.wait_ge(r_rstd_ready, n_result)
                steps.mark(scaled([r_val[:, k, :] for k in range(GT)], srcs, r_mv, r_rstd))
                steps.wait()
                steps.mark(dve.tensor_tensor(r_new[:], rows, r_val[:], ALU.add))
                steps.wait()
                return dve.tensor_scalar(rows, r_new[:], 1.0, None, ALU.mult)

            moe_rows = [moe_out[:, k, :] for k in range(GT)]

            def add_expert(g, e):
                j = min(e, E0)
                b = bank[4 + j % 2]
                dve.wait_ge(ye_filled, g * 10 + (e + 1))
                if not (isinstance(g, int) and g == 0 and e == 0):
                    dve.wait_ge(acc_done, g * (E0 + 1) + j)
                if e < E0:
                    for k in range(GT):
                        w = combine[:, bass.ds(g * GT + k, 1), e:e + 1].rearrange("p a b -> p (a b)")
                        if e == 0:
                            ins = dve.tensor_scalar(acc[:, k, :], b[:, k * P:(k + 1) * P], w, None, ALU.mult)
                        else:
                            ins = dve.scalar_tensor_tensor(out=acc[:, k, :], in0=b[:, k * P:(k + 1) * P], scalar=w,
                                                           in1=acc[:, k, :], op0=ALU.mult, op1=ALU.add)
                else:
                    ins = dve.tensor_tensor(moe_out[:], b[:].rearrange("p (k d) -> p k d", k=GT), acc[:], ALU.add)
                ins.then_inc(acc_done, 1)

            def next_xn(g):
                dve.wait_ge(m_rstd_ready, g + (NT + 1))
                if not isinstance(g, int):
                    dve.wait_ge(xT_filled, g + 2 * NG)
                scaled([xn[:, k, :] for k in range(GT)], [r_new[:, k, :] for k in range(GT)], m_mv, m_rstd)\
                    .then_inc(xn_ready, 1)

            def split_bc(g):
                cols = slice(g * G, (g + 1) * G) if isinstance(g, int) else bass.ds(g * G, G)
                head = Steps(dve, head_step, g * 3)
                dve.wait_ge(bc_filled, g + 1)
                dve.memset(wait_slot_v[:, 0:1], 0.0)
                head.mark(dve.tensor_copy(bc[:, cols], bank[7][0:96, :]))
                head.wait()
                head.mark(dve.tensor_tensor(bc_rest, bank[7][0:96, :], bc[:, cols], ALU.subtract))
                head.wait()
                head.mark(dve.tensor_copy(bc_mid[:], bc_rest))
                head.wait()
                dve.memset(wait_slot_v[:, 1:2], 0.0)
                dve.tensor_copy(bc[32:64, cols], bc_mid[32:64, :])
                dve.tensor_tensor(bc[64:96, cols], bc_rest[64:96, :], bc_mid[64:96, :],
                                  ALU.subtract).then_inc(bc_ready, 1)

            def delta_of(g, z):
                cols = slice(g * G, (g + 1) * G)
                dve.wait_ge(zlog_ready, g + 1)
                dve.scalar_tensor_tensor(out=delta[:, cols], in0=z, scalar=0.0, in1=soft[g],
                                         op0=ALU.max, op1=ALU.add).then_inc(delta_ready, 1)

            def expert_group(g):
                first = isinstance(g, int)
                steps = None if first else Steps(dve, moe_step, (g - 1) * 6)
                for e in range(E0 + NSH):
                    for m in range(2):
                        dve.wait_ge(sil_ready, g * 20 + (2 * e + m + 1))
                        if not (first and e < 2):
                            dve.wait_ge(ye_filled, g * 10 + e - 1)
                        dve.tensor_tensor(hid[:, e % 2, m, :], bank[2 * m + 1][:], sil[:, m, :], ALU.mult)\
                           .then_inc(hid_ready, 1)
                    if first:
                        if e + 2 < E0 + NSH:
                            upper_parts(e + 2)
                        if e < 2:
                            route_choice(e)
                        elif e == 2:
                            route_weights()
                            add_expert(g, 0)
                        if 4 <= e < 4 + NG - 1:
                            split_x(e - 3)
                    if 1 <= e <= E0 and not (first and e == 1):
                        add_expert(g, e - 1)
                    if not first:
                        if e == 0:
                            add_expert(g - 1, E0 + NSH - 1)
                        elif e == 1:
                            dve.wait_ge(acc_done, g * (E0 + 1))
                            result_stats(steps, moe_rows)
                        elif e == 2:
                            new_rows(steps, g - 1, moe_rows, g + NT)
                        elif e == 4:
                            next_stats(steps, GT)
                        elif e == 5:
                            next_xn(g - 1)
                        elif e == 9:
                            split_bc(g - 1)

            upper_parts(1)
            expert_group(0)
            with dve.Fori(1, NG) as g:
                expert_group(g)
            last_steps = Steps(dve, moe_step, (NG - 1) * 6)
            add_expert(NG - 1, E0 + NSH - 1)
            dve.wait_ge(acc_done, NG * (E0 + 1))
            result_stats(last_steps, moe_rows)
            new_rows(last_steps, NG - 1, moe_rows, NT + NG)
            next_stats(last_steps, GT)
            dve.wait_ge(xT_filled, 3 * NG - 1)
            next_xn(NG - 1)

            dve.wait_ge(expA_ready, 1)
            dve.tensor_scalar(negA[:], expA[:], -1.0, None, ALU.mult).then_inc(negA_ready, 1)
            for g in range(NG - 1):
                delta_of(g, z_all[:, g * G:(g + 1) * G])
            dve.wait_ge(state_zeroed, 1)

            def state_group(g):
                first = isinstance(g, int)

                def drive_n(n):
                    if n == 0:
                        dve.wait_ge(dx_ready, g + 1)
                    dve.wait_ge(B_filled, g * NS + (n + 1))
                    two = first and n < 2 * RS
                    if not (first and n < RS):
                        dve.wait_ge(scan_done, g * NS + n - (RS - 1))
                    dve.tensor_tensor(drive[:, n % RS, :], dx[:, bass.ds(g * G, G)],
                                      bank[B_bank[n % 2 if two else n % RS]][:], ALU.mult).then_inc(drive_done, 1)

                drive_n(0)
                for n in range(NS):
                    step = g * NS + n
                    if n + 1 < NS:
                        drive_n(n + 1)
                    dve.wait_ge(decay_ready, step + 1)
                    dve.wait_ge(drive_done, step + 1)
                    if not (first and n < RS):
                        dve.wait_ge(state_saved, step - (RS - 1))
                        dve.wait_ge(hc_done, step - (RS - 1))
                    dve.tensor_tensor_scan(hs[:, n % RS, :], bank[3 + n % 2][:], drive[:, n % RS, :],
                                           state[:, n:n + 1], ALU.mult, ALU.add).then_inc(scan_done, 1)
                    if first and n == RS:
                        split_bc(NG - 1)
                    if first and n == RS + 1:
                        delta_of(NG - 1, bank[6][:])

            state_group(0)
            with dve.Fori(1, NG) as g:
                state_group(g)

            tail = Steps(dve, tail_step)

            def ctx_rows(g):
                return [ctx_v[:, g % 2, k * P:(k + 1) * P] for k in range(GT)]

            def y_rows(g):
                return [bank[g % 2][:, k * P:(k + 1) * P] for k in range(GT)]

            xf_steps = Steps(dve, xf_step)

            def split_tokens(g):
                cols = slice(g * G, (g + 1) * G)
                dve.wait_ge(xT_ready, 3 * NG + g + 1)
                xf_steps.mark(dve.tensor_copy(xT_hi[:, cols], xT[:, cols]))
                xf_steps.wait()
                dve.tensor_tensor(xT_lo[:, cols], xT[:, cols], xT_hi[:, cols].bitcast(F32), ALU.subtract)\
                   .then_inc(xf_split_ready, 1)

            def bias_of(out, mv, rstd):
                return dve.scalar_tensor_tensor(out=out, in0=mv[:, :, 0], scalar=-1.0, in1=rstd,
                                                op0=ALU.mult, op1=ALU.mult)

            for i in range(NG + 2):
                if i < NG:
                    dve.wait_ge(ytok_filled, i + 1)
                    row_stats(tail, y_rows(i), y_stats, y_mv, y_var, y_var_ready)
                if i >= 2:
                    o = i - 2
                    rows = x[:, o * GT:(o + 1) * GT, :]
                    dve.wait_ge(r_rstd_ready, NT + NG + o + 1)
                    ins = scaled([r_val[:, k, :] for k in range(GT)], ctx_rows(o), r_mv, r_rstd)
                    ins.then_inc(r_scaled, 1)
                    dve.wait_ge(r_scaled, o + 1)
                    tail.mark(dve.tensor_tensor(rows, rows, r_val[:], ALU.add))
                    tail.wait()
                    row_stats(tail, [rows[:, k, :] for k in range(GT)], m_stats, m_mv, m_var, m_var_ready)
                if i < NG:
                    dve.wait_ge(y_rstd_ready, i + 1)
                    bias_of(y_bias[:, i, :], y_mv, y_rstd[:, i, :]).then_inc(y_bias_ready, 1)
                if i >= 2:
                    dve.wait_ge(m_rstd_ready, NT + NG + o + 1)
                    bias_of(t_bias[:, o, :], m_mv, t_rstd[:, o, :]).then_inc(t_bias_ready, 1)
                if i == NG + 1:
                    for g in range(NG - 1):
                        split_tokens(g)
                if 1 <= i <= NG:
                    dve.wait_ge(ctx_drained, i)
                    result_stats(tail, ctx_rows(i - 1))

            dve.wait_ge(xT_ready, 4 * NG)
            pick_steps = Steps(dve, pick_step)

            def pick_do(ins):
                pick_steps.mark(ins)
                pick_steps.wait()

            pick_do(dve.tensor_reduce(pooled[:, 0:1], pool_part[:], AX.X, ALU.add))
            dve.tensor_scalar(pooled[:, 1:2], pooled[:, 0:1], 1.0 / T, None, ALU.mult).then_inc(pooled_ready, 1)
            dve.wait_ge(lg_filled, 1)
            pick_do(dve.tensor_copy(lg[:], bank[0][0:1, 0:E1]))
            pick_do(dve.max(top8[:], lg[:]))
            dve.max_index(idx8[:], top8[:], lg[:]).then_inc(idx_ready, 1)
            dve.tensor_tensor(dif[:, 0:1], top8[:, 1:2], top8[:, 0:1], ALU.subtract).then_inc(dif_ready, 1)
            dve.wait_ge(dexp_ready, 1)
            pick_do(dve.tensor_scalar(dif[:, 2:3], dif[:, 1:2], 1.0, None, ALU.add))
            pick_do(dve.reciprocal(wrow[:, 0:1], dif[:, 2:3]))
            dve.tensor_tensor(wrow[:, 1:2], dif[:, 1:2], wrow[:, 0:1], ALU.mult).then_inc(wrow_ready, 1)
            split_tokens(NG - 1)
            dve.wait_ge(wb_filled, 1)
            pick_do(dve.tensor_copy(wts[:], bank[5][:, 0:2]))
            w1s_steps = Steps(dve, w1s_step)
            for k in range(2):
                dve.wait_ge(w1_in[k], 16)
                w1s_steps.mark(dve.tensor_copy(w1s_hi[:, k, :], w1s[:, k, :]))
                w1s_steps.wait()
                dve.tensor_tensor(w1s_lo[:, k, :], w1s[:, k, :], w1s_hi[:, k, :].bitcast(F32), ALU.subtract)\
                   .then_inc(w1s_split_ready, 1)
            w2w_steps = Steps(dve, w2w_step)

            def weighted_w2(k):
                dve.wait_ge(w2_in[k], 16)
                w2w_steps.mark(dve.tensor_scalar(w2w[:, k, :], w2s[:, k, :], wts[:, k:k + 1], None, ALU.mult))
                w2w_steps.wait()
                w2w_steps.mark(dve.tensor_copy(w2w_hi[:, k, :], w2w[:, k, :]))
                w2w_steps.wait()
                dve.tensor_tensor(w2w_lo[:, k, :], w2w[:, k, :], w2w_hi[:, k, :].bitcast(F32), ALU.subtract)\
                   .then_inc(w2w_split_ready, 1)

            out_rows = [bank[6][:, k * P:(k + 1) * P] for k in range(GT)]

            def final_stats(g, steps):
                dve.wait_ge(out_filled, g + 1)
                result_stats(steps, out_rows)

            def final_scaled(g, tiles):
                for k in tiles:
                    ins = dve.tensor_scalar(r_val[:, k, :], out_rows[k], r_mv[:, k, 0:1], r_rstd[:, k:k + 1],
                                            ALU.subtract, ALU.mult)
                if k == GT - 1:
                    ins.then_inc(out_drained, 1)

            def final_sum(g):
                dve.wait_ge(out_drained, g + 1)
                rows = x[:, bass.ds(g * GT, GT), :]
                dve.tensor_tensor(rows, rows, r_val[:], ALU.add).then_inc(x_final, 1)

            def hidden_group(g, before):
                for v in range(NV):
                    dve.wait_ge(gelu_done, g * NV + (v + 1))
                    if not (before is None and v < RS):
                        dve.wait_ge(yv_done, g * NV + (v - RS + 1))
                    dve.tensor_copy(hg_hi[v % RS], hg[v % RS]).then_inc(hg_hi_ready, 1)
                    if v % RS == RS - 1:
                        dve.wait_ge(hg_hi_ready, g * NV + (v + 1))
                        dve.tensor_tensor(hg_lo[v % RS], hg[v % RS], hg_hi[v % RS].bitcast(F32),
                                          ALU.subtract).then_inc(hg_lo_dve, 1)
                    if before is None:
                        if v < 2:
                            weighted_w2(v)
                        elif v == 2:
                            dve.wait_ge(b2_filled, 1)
                            dve.tensor_copy(b2c[:], bank[7][:, 0:1]).then_inc(wb_ready, 1)
                    if before is not None:
                        if v == 4:
                            final_stats(before, Steps(dve, ff_step, before * 2))
                        elif v == 5:
                            dve.wait_ge(r_rstd_ready, before + (NT + 2 * NG + 1))
                            final_scaled(before, (0, 1))
                        elif v == 6:
                            final_scaled(before, (2, 3))
                        elif v == 7:
                            final_sum(before)

            hidden_group(0, None)
            hidden_group(1, 0)
            with dve.Fori(2, NG) as g:
                hidden_group(g, g - 1)
            final_stats(NG - 1, Steps(dve, ff_step, (NG - 1) * 2))
            dve.wait_ge(r_rstd_ready, NT + 3 * NG)
            final_scaled(NG - 1, range(GT))
            final_sum(NG - 1)

def kernel(**inputs):
    import ml_dtypes
    import numpy as np

    import concourse.bacc as bacc
    from concourse.bass_utils import run_bass_kernel_spmd as run

    i = {k: np.asarray(v) for k, v in inputs.items()}
    later = np.triu(np.ones((P, P), np.float32))
    select = np.zeros((96, 2 * NS, P), ml_dtypes.bfloat16)
    for c in range(3):
        for n in range(2 * NS):
            select[32 * c + n, n, :] = 1
    arrays = {
        "x": i["L0_attn_x"].reshape(T, D),
        "ident": np.eye(P, dtype=np.float32),
        "mask": np.tile(later, (1, GT)),
        "W_q": i["L0_attn_W_q"], "W_k": i["L0_attn_W_k"], "W_v": i["L0_attn_W_v"], "W_o": i["L0_attn_W_o"],
        "routerT": i["L0_ffn_router_w"].T,
        "bias": np.broadcast_to(i["L0_ffn_expert_bias"], (P, NT, E0)),
        "rank": np.broadcast_to(np.arange(E0, dtype=np.float32) - E0, (P, NT, E0)),
        "w1T": i["L0_ffn_w1"].transpose(2, 0, 1), "sw1T": i["L0_ffn_sw1"].transpose(2, 0, 1),
        "w3T": i["L0_ffn_w3"].transpose(2, 0, 1), "sw3T": i["L0_ffn_sw3"].transpose(2, 0, 1),
        "w2T": i["L0_ffn_w2"].reshape(E0, D, 2, P).transpose(3, 0, 2, 1),
        "sw2T": i["L0_ffn_sw2"].reshape(NSH, D, 2, P).transpose(3, 0, 2, 1),
        "select": select,
        "W_delta": i["L1_attn_W_delta"], "W_B": i["L1_attn_W_B"], "W_C": i["L1_attn_W_C"],
        "W_ctx": i["L1_attn_W_ctx"], "A_log": i["L1_attn_A_log"],
        "gamma": i["L1_attn_ln_gamma"].reshape(D, 1), "beta": i["L1_attn_ln_beta"].reshape(D, 1),
        "ctx_scale": np.broadcast_to(i["L1_attn_context_scale"].reshape(1, 1), (P, 1)),
        "Wr": i["L1_ffn_Wr"], "W1": i["L1_ffn_W1"],
        "b1": i["L1_ffn_b1"].reshape(E1, NF, P).transpose(0, 2, 1),
        "W2": i["L1_ffn_W2"].reshape(E1, NF, P, D).transpose(0, 2, 1, 3).reshape(E1, P, NF * D),
        "b2": i["L1_ffn_b2"],
    }
    arrays = {f"{k}_dram": np.ascontiguousarray(v) for k, v in arrays.items()}
    nc = bacc.Bacc("TRN2", target_bir_lowering=False, num_devices=1)
    aps = {k[:-5]: nc.dram_tensor(k, v.shape, mybir.dt.from_np(v.dtype), kind="ExternalInput").ap()
           for k, v in arrays.items()}
    out = nc.dram_tensor("out_dram", (1, T, D), F32, kind="ExternalOutput").ap()
    sandwich(nc, aps, out)
    r = run(nc, [arrays], core_ids=[0])
    return r.results[0]["out_dram"]
```
